# Optimizing a Trainium2 kernel written in Bass

```python
import numpy as np
import jax
import jax.numpy as jnp

def _softmax(x, axis=-1):
    return jax.nn.softmax(x, axis=axis)

def _gelu(x):
    return jax.nn.gelu(x, approximate=True)

def _silu(x):
    return jax.nn.silu(x)

def _sigmoid(x):
    return jax.nn.sigmoid(x)

def _layernorm(x, axis=-1, eps=1e-05):
    m = jnp.mean(x, axis=axis, keepdims=True)
    v = jnp.var(x, axis=axis, keepdims=True)
    return (x - m) / jnp.sqrt(v + eps)

def _scatter_add(tgt, idx, src, axis=0):
    return tgt.at[idx].add(src)

def _segment_sum(src, seg, n):
    return jax.ops.segment_sum(src, seg, n)
kernel_name = 'mk_sandwich_d2_jaxref_r8_8373c8'

def setup_inputs(seed: int=0):
    np.random.seed(seed)
    _w = jnp.asarray

    def _L0_attn_setup():
        import jax, jax.numpy as jnp
        import numpy as np
        HID = 256
        NH = 32
        NKV = 8
        HD = 64
        LR = 32
        TOPK = 16
        THETA = 10000.0
        B, S = (1, 256)
        _half = np.ones(HD // 2, dtype=bool)
        _half[:TOPK] = False
        _per_head = np.concatenate([_half, _half])
        NOPE_MASK = np.tile(_per_head, NKV)
        ROPE_IDX = jnp.asarray(np.where(~NOPE_MASK)[0])
        NOPE_IDX = jnp.asarray(np.where(NOPE_MASK)[0])
        N_ROPE = int((~NOPE_MASK).sum())
        N_NOPE = int(NOPE_MASK.sum())

        def _rotate_half(x):
            return jnp.concatenate([-x[..., HD // 2:], x[..., :HD // 2]], axis=-1)
        key = jax.random.key(seed)
        ks = jax.random.split(key, 8)
        sc = 0.02
        return {'hidden_states': jax.random.normal(ks[0], (B, S, HID), dtype=jnp.float32), 'q_w': jax.random.normal(ks[1], (NH * HD, HID), dtype=jnp.float32) * sc, 'kr_w': jax.random.normal(ks[2], (N_ROPE, HID), dtype=jnp.float32) * sc, 'down_w': jax.random.normal(ks[3], (LR * NKV, HID), dtype=jnp.float32) * sc, 'upk_w': jax.random.normal(ks[4], (N_NOPE, LR * NKV), dtype=jnp.float32) * sc, 'upv_w': jax.random.normal(ks[5], (NKV * HD, LR * NKV), dtype=jnp.float32) * sc, 'o_w': jax.random.normal(ks[6], (HID, NH * HD), dtype=jnp.float32) * sc}
    _L0_attn_in = _L0_attn_setup()

    def _L0_ffn_setup():
        import jax, jax.numpy as jnp
        import numpy as np
        E = 8
        TOP_K = 2
        D = 256
        DE = 176
        DS = 352
        B, S = (2, 256)
        key = jax.random.key(seed)
        ks = jax.random.split(key, 8)
        std = 0.02
        return {'x': jax.random.normal(ks[0], (B, S, D), jnp.float32), 'W_router': jax.random.normal(ks[1], (D, E), jnp.float32) * std, 'We_gate': jax.random.normal(ks[2], (E, D, DE), jnp.float32) * std, 'We_up': jax.random.normal(ks[3], (E, D, DE), jnp.float32) * std, 'We_down': jax.random.normal(ks[4], (E, DE, D), jnp.float32) * std, 'Ws_gate': jax.random.normal(ks[5], (D, DS), jnp.float32) * std, 'Ws_up': jax.random.normal(ks[6], (D, DS), jnp.float32) * std, 'Ws_down': jax.random.normal(ks[7], (DS, D), jnp.float32) * std}
    _L0_ffn_in = _L0_ffn_setup()

    def _L1_attn_setup():
        import jax, jax.numpy as jnp
        import numpy as np
        D_MODEL = 256
        N_HEADS = 16
        QK_ROPE = 64
        QK_NOPE = 128
        KV_LORA = 64
        V_DIM = 128
        QK_DIM = QK_ROPE + QK_NOPE
        RMS_EPS = 1.1920928955078125e-07

        def apply_rope(x, base=10000.0):
            B, S, H, D = x.shape
            freqs = 1.0 / base ** (jnp.arange(0, D, 2, dtype=jnp.float32) / D)
            t = jnp.arange(S, dtype=jnp.float32)[:, None] * freqs[None, :]
            cos = jnp.cos(t)[None, :, None, :]
            sin = jnp.sin(t)[None, :, None, :]
            x1 = x[..., 0::2]
            x2 = x[..., 1::2]
            out = jnp.stack([x1 * cos - x2 * sin, x2 * cos + x1 * sin], axis=-1)
            return out.reshape(B, S, H, D).astype(x.dtype)
        key = jax.random.key(seed)
        ks = jax.random.split(key, 6)
        s = lambda fan_in: 1.0 / np.sqrt(fan_in)
        x = jax.random.normal(ks[0], (2, 256, D_MODEL), dtype=jnp.float32)
        Wq = jax.random.normal(ks[1], (D_MODEL, N_HEADS * QK_DIM), dtype=jnp.float32) * s(D_MODEL)
        Wkv_a = jax.random.normal(ks[2], (D_MODEL, KV_LORA + QK_ROPE), dtype=jnp.float32) * s(D_MODEL)
        kv_norm_w = jnp.ones((KV_LORA,), dtype=jnp.float32)
        Wkv_b = jax.random.normal(ks[3], (KV_LORA, N_HEADS * (QK_NOPE + V_DIM)), dtype=jnp.float32) * s(KV_LORA)
        Wo = jax.random.normal(ks[4], (N_HEADS * V_DIM, D_MODEL), dtype=jnp.float32) * s(N_HEADS * V_DIM)
        return {'x': x, 'Wq': Wq, 'Wkv_a': Wkv_a, 'kv_norm_w': kv_norm_w, 'Wkv_b': Wkv_b, 'Wo': Wo}
    _L1_attn_in = _L1_attn_setup()

    def _L1_ffn_setup():
        import jax, jax.numpy as jnp
        import numpy as np
        HIDDEN = 256
        INTER = 1024
        BATCH, LOCAL_SEQ = (2, 512)
        key = jax.random.key(seed)
        k1, k2, k3 = jax.random.split(key, 3)
        h_shard = jax.random.normal(k1, (BATCH, LOCAL_SEQ, HIDDEN), dtype=jnp.float32)
        w_gate_up = jax.random.normal(k2, (2 * INTER, HIDDEN), dtype=jnp.float32) * 0.02
        w_down = jax.random.normal(k3, (HIDDEN, INTER), dtype=jnp.float32) * 0.02
        return {'h_shard': h_shard, 'w_gate_up': w_gate_up, 'w_down': w_down}
    _L1_ffn_in = _L1_ffn_setup()
    _d = {'L0_attn_hidden_states': _L0_attn_in['hidden_states'], 'L0_attn_q_w': _L0_attn_in['q_w'], 'L0_attn_kr_w': _L0_attn_in['kr_w'], 'L0_attn_down_w': _L0_attn_in['down_w'], 'L0_attn_upk_w': _L0_attn_in['upk_w'], 'L0_attn_upv_w': _L0_attn_in['upv_w'], 'L0_attn_o_w': _L0_attn_in['o_w'], 'L0_ffn_W_router': _L0_ffn_in['W_router'], 'L0_ffn_We_gate': _L0_ffn_in['We_gate'], 'L0_ffn_We_up': _L0_ffn_in['We_up'], 'L0_ffn_We_down': _L0_ffn_in['We_down'], 'L0_ffn_Ws_gate': _L0_ffn_in['Ws_gate'], 'L0_ffn_Ws_up': _L0_ffn_in['Ws_up'], 'L0_ffn_Ws_down': _L0_ffn_in['Ws_down'], 'L1_attn_Wq': _L1_attn_in['Wq'], 'L1_attn_Wkv_a': _L1_attn_in['Wkv_a'], 'L1_attn_kv_norm_w': _L1_attn_in['kv_norm_w'], 'L1_attn_Wkv_b': _L1_attn_in['Wkv_b'], 'L1_attn_Wo': _L1_attn_in['Wo'], 'L1_ffn_w_gate_up': _L1_ffn_in['w_gate_up'], 'L1_ffn_w_down': _L1_ffn_in['w_down']}
    _x0 = _d['L0_attn_hidden_states']
    _d['L0_attn_hidden_states'] = jax.random.normal(jax.random.fold_in(jax.random.key(seed), 1), (4, 512, 256), dtype=_x0.dtype)
    del _x0
    return _d

def reference(L0_attn_hidden_states, L0_attn_q_w, L0_attn_kr_w, L0_attn_down_w, L0_attn_upk_w, L0_attn_upv_w, L0_attn_o_w, L0_ffn_W_router, L0_ffn_We_gate, L0_ffn_We_up, L0_ffn_We_down, L0_ffn_Ws_gate, L0_ffn_Ws_up, L0_ffn_Ws_down, L1_attn_Wq, L1_attn_Wkv_a, L1_attn_kv_norm_w, L1_attn_Wkv_b, L1_attn_Wo, L1_ffn_w_gate_up, L1_ffn_w_down):

    def _L0_attn_ref(hidden_states, q_w, kr_w, down_w, upk_w, upv_w, o_w):
        import jax, jax.numpy as jnp
        import numpy as np
        HID = 256
        NH = 32
        NKV = 8
        HD = 64
        LR = 32
        TOPK = 16
        THETA = 10000.0
        B, S = (1, 256)
        _half = np.ones(HD // 2, dtype=bool)
        _half[:TOPK] = False
        _per_head = np.concatenate([_half, _half])
        NOPE_MASK = np.tile(_per_head, NKV)
        ROPE_IDX = jnp.asarray(np.where(~NOPE_MASK)[0])
        NOPE_IDX = jnp.asarray(np.where(NOPE_MASK)[0])
        N_ROPE = int((~NOPE_MASK).sum())
        N_NOPE = int(NOPE_MASK.sum())

        def _rotate_half(x):
            return jnp.concatenate([-x[..., HD // 2:], x[..., :HD // 2]], axis=-1)
        b, s, _ = hidden_states.shape
        dt = hidden_states.dtype
        q = (hidden_states @ q_w.T).reshape(b, s, NH, HD).transpose(0, 2, 1, 3)
        k_r = hidden_states @ kr_w.T
        k0 = jnp.zeros((b, s, NKV * HD), dtype=dt).at[..., ROPE_IDX].set(k_r)
        k = k0.reshape(b, s, NKV, HD).transpose(0, 2, 1, 3)
        pos = jnp.arange(s, dtype=jnp.float32)
        inv_freq = 1.0 / THETA ** (jnp.arange(0, HD, 2, dtype=jnp.float32) / HD)
        freqs = pos[:, None] * inv_freq[None, :]
        emb = jnp.concatenate([freqs, freqs], axis=-1)
        cos = jnp.cos(emb).astype(dt)
        sin = jnp.sin(emb).astype(dt)
        q = q * cos + _rotate_half(q) * sin
        k = k * cos + _rotate_half(k) * sin
        k_r2 = k.transpose(0, 2, 1, 3).reshape(b, s, NKV * HD)[..., ROPE_IDX]
        c_kv = hidden_states @ down_w.T
        k_c = c_kv @ upk_w.T
        v = (c_kv @ upv_w.T).reshape(b, s, NKV, HD).transpose(0, 2, 1, 3)
        kf = jnp.zeros((b, s, NKV * HD), dtype=dt).at[..., NOPE_IDX].set(k_c).at[..., ROPE_IDX].set(k_r2).reshape(b, s, NKV, HD).transpose(0, 2, 1, 3)
        g = NH // NKV
        kf = jnp.repeat(kf, g, axis=1)
        v = jnp.repeat(v, g, axis=1)
        scores = jnp.einsum('bhqd,bhkd->bhqk', q, kf) / jnp.sqrt(jnp.asarray(HD, dt))
        causal = jnp.tril(jnp.ones((s, s), dtype=bool))
        scores = jnp.where(causal, scores, jnp.finfo(dt).min)
        attn = jax.nn.softmax(scores, axis=-1)
        out = jnp.einsum('bhqk,bhkd->bhqd', attn, v)
        out = out.transpose(0, 2, 1, 3).reshape(b, s, NH * HD)
        return out @ o_w.T

    def _L0_ffn_ref(x, W_router, We_gate, We_up, We_down, Ws_gate, Ws_up, Ws_down):
        import jax, jax.numpy as jnp
        import numpy as np
        E = 8
        TOP_K = 2
        D = 256
        DE = 176
        DS = 352
        B, S = (2, 256)
        b, s, d = x.shape
        shared = jax.nn.silu(x @ Ws_gate) * (x @ Ws_up) @ Ws_down
        scores = jax.nn.softmax(x @ W_router, axis=-1)
        topk_vals, topk_idx = jax.lax.top_k(scores, TOP_K)
        onehot = jax.nn.one_hot(topk_idx, E, dtype=x.dtype)
        combine = jnp.einsum('bsk,bske->bse', topk_vals, onehot)
        combine = combine.reshape(b * s, E)
        xf = x.reshape(b * s, d)
        h = jax.nn.silu(jnp.einsum('td,edh->eth', xf, We_gate)) * jnp.einsum('td,edh->eth', xf, We_up)
        y_all = jnp.einsum('eth,ehd->etd', h, We_down)
        routed = jnp.einsum('etd,te->td', y_all, combine)
        return routed.reshape(b, s, d) + shared

    def _L1_attn_ref(x, Wq, Wkv_a, kv_norm_w, Wkv_b, Wo):
        import jax, jax.numpy as jnp
        import numpy as np
        D_MODEL = 256
        N_HEADS = 16
        QK_ROPE = 64
        QK_NOPE = 128
        KV_LORA = 64
        V_DIM = 128
        QK_DIM = QK_ROPE + QK_NOPE
        RMS_EPS = 1.1920928955078125e-07

        def apply_rope(x, base=10000.0):
            B, S, H, D = x.shape
            freqs = 1.0 / base ** (jnp.arange(0, D, 2, dtype=jnp.float32) / D)
            t = jnp.arange(S, dtype=jnp.float32)[:, None] * freqs[None, :]
            cos = jnp.cos(t)[None, :, None, :]
            sin = jnp.sin(t)[None, :, None, :]
            x1 = x[..., 0::2]
            x2 = x[..., 1::2]
            out = jnp.stack([x1 * cos - x2 * sin, x2 * cos + x1 * sin], axis=-1)
            return out.reshape(B, S, H, D).astype(x.dtype)
        B, S, _ = x.shape
        q = (x @ Wq).reshape(B, S, N_HEADS, QK_DIM)
        q_nope, q_rope = (q[..., :QK_NOPE], q[..., QK_NOPE:])
        q = jnp.concatenate([q_nope, apply_rope(q_rope)], axis=-1)
        kv = x @ Wkv_a
        c_kv, k_rope = (kv[..., :KV_LORA], kv[..., KV_LORA:])
        k_rope = apply_rope(k_rope.reshape(B, S, 1, QK_ROPE))
        c_kv = c_kv * jax.lax.rsqrt(jnp.mean(c_kv * c_kv, axis=-1, keepdims=True) + RMS_EPS) * kv_norm_w
        kv = (c_kv @ Wkv_b).reshape(B, S, N_HEADS, QK_NOPE + V_DIM)
        k_nope, v = (kv[..., :QK_NOPE], kv[..., QK_NOPE:])
        k = jnp.concatenate([k_nope, jnp.broadcast_to(k_rope, (B, S, N_HEADS, QK_ROPE))], axis=-1)
        scale = 1.0 / np.sqrt(QK_DIM)
        scores = jnp.einsum('bqhd,bkhd->bhqk', q, k) * scale
        mask = jnp.tril(jnp.ones((S, S), dtype=bool))
        scores = jnp.where(mask, scores, jnp.finfo(scores.dtype).min)
        attn = jax.nn.softmax(scores, axis=-1)
        out = jnp.einsum('bhqk,bkhd->bqhd', attn, v).reshape(B, S, N_HEADS * V_DIM)
        return out @ Wo

    def _L1_ffn_ref(h_shard, w_gate_up, w_down):
        import jax, jax.numpy as jnp
        import numpy as np
        HIDDEN = 256
        INTER = 1024
        BATCH, LOCAL_SEQ = (2, 512)
        batch, local_seq, hidden = h_shard.shape
        gate_up = jnp.einsum('bsh,oh->bso', h_shard, w_gate_up)
        gate, up = jnp.split(gate_up, 2, axis=-1)
        h = jax.nn.silu(gate) * up
        out = jnp.einsum('bsi,hi->bsh', h, w_down)
        return out
    x = L0_attn_hidden_states
    x = x + _layernorm(_L0_attn_ref(_layernorm(x, axis=-1), L0_attn_q_w, L0_attn_kr_w, L0_attn_down_w, L0_attn_upk_w, L0_attn_upv_w, L0_attn_o_w), axis=-1)
    x = x + _layernorm(_L0_ffn_ref(_layernorm(x, axis=-1), L0_ffn_W_router, L0_ffn_We_gate, L0_ffn_We_up, L0_ffn_We_down, L0_ffn_Ws_gate, L0_ffn_Ws_up, L0_ffn_Ws_down), axis=-1)
    x = x + _layernorm(_L1_attn_ref(_layernorm(x, axis=-1), L1_attn_Wq, L1_attn_Wkv_a, L1_attn_kv_norm_w, L1_attn_Wkv_b, L1_attn_Wo), axis=-1)
    x = x + _layernorm(_L1_ffn_ref(_layernorm(x, axis=-1), L1_ffn_w_gate_up, L1_ffn_w_down), axis=-1)
    return x

_drawn_inputs = setup_inputs


def setup_inputs(seed=0):
    import zlib

    import numpy as np

    out = dict(_drawn_inputs(seed))
    spreads = {'L1_attn_kv_norm_w': (1.0, 0.2)}
    factors = {}
    for name, (base, spread) in spreads.items():
        noise = np.random.default_rng([zlib.crc32(name.encode()), seed]).standard_normal(out[name].shape)
        drawn = base * np.exp(spread * noise) if base else spread * noise
        out[name] = jnp.asarray(drawn.astype(out[name].dtype))
    for name, factor in factors.items():
        out[name] = (out[name] * factor).astype(out[name].dtype)
    return out
```

```python
from contextlib import ExitStack

import numpy as np

import concourse.bass as bass
from concourse import mybir

F32 = mybir.dt.float32
F32R = mybir.dt.float32r
BF16 = mybir.dt.bfloat16
ALU = mybir.AluOpType
ACT = mybir.ActivationFunctionType
AX = mybir.AxisListType

P = 128
D = 256
KD = D // P
NSEQ, SEQ = 4, 512
TT = SEQ // P
LN_EPS = 1e-5
RMS_EPS = 1.1920928955078125e-07
MASKED = -1e30

NH0, NKV0, HD0 = 32, 8, 64
ROPE0 = 16
NE, DE, DS = 8, 176, 352
MOE_H = NE * DE + DS
NH1, NOPE1, ROT1, LAT1, VD1 = 16, 128, 64, 64, 128
INTER = 1024

HG = 4
HPAIR = 2 * HG


def at(t, offset, *dims):
    base = t[:] if not isinstance(t, bass.AP) else t
    return bass.AP(tensor=base.tensor, offset=base.offset + offset,
                   ap=[list(base.ap[0])] + [list(d) for d in dims])


class Names:

    def __init__(self, nc, ctx, tag):
        self.nc, self.ctx, self.tag = nc, ctx, tag

    def sb(self, name, shape, dt=F32):
        return self.ctx.enter_context(self.nc.sbuf_tensor(f"{self.tag}_{name}", shape, dt))

    def ps(self, name, shape, dt=F32):
        return self.ctx.enter_context(self.nc.psum_tensor(f"{self.tag}_{name}", shape, dt))

    def sem(self, name):
        return self.ctx.enter_context(self.nc.semaphore(f"{self.tag}_{name}"))



LN_LINKS = 3


class Norm:

    def __init__(self, m, const, which):
        self.stats = m.sb(f"{which}_stats", [P, TT, 6])
        self.mv = m.sb(f"{which}_mv", [P, TT, 2])
        self.var = m.sb(f"{which}_var", [P, TT])
        self.rstd = m.sb(f"{which}_rstd", [P, TT])
        self.pause = m.sb(f"{which}_pause", [P, 1])
        self.minus_half = const["minus_half"]
        self.linked = m.sem(f"{which}_ln_linked")
        self.var_ready = m.sem(f"{which}_ln_var_ready")
        self.rstd_ready = m.sem(f"{which}_ln_rstd_ready")

    def statistics(self, nc, dve, tiles, count):
        for j, tile in enumerate(tiles):
            ins = nc.vector.bn_stats(self.stats[:, j, :], tile)
        ins.then_inc(self.linked, 1)
        dve.wait_ge(self.linked, count * 2 + 1)
        nc.vector.memset(self.pause[:], 0.0)
        for j in range(len(tiles)):
            ins = nc.vector.bn_aggr(self.mv[:, j, :], self.stats[:, j, :])
        ins.then_inc(self.linked, 1)
        dve.wait_ge(self.linked, count * 2 + 2)
        nc.vector.tensor_scalar(self.var[:], self.mv[:, :, 1], LN_EPS, None, ALU.add).then_inc(self.var_ready, 1)
        dve.wait_ge(self.rstd_ready, count + 1)

    def power(self, nc, pool, count):
        pool.wait_ge(self.var_ready, count + 1)
        nc.gpsimd.tensor_tensor(self.rstd[:], self.var[:], self.minus_half[:, 0:TT],
                                ALU.pow).then_inc(self.rstd_ready, 1)

    def apply(self, nc, out, tile, j):
        return nc.vector.tensor_scalar(out, tile, self.mv[:, j, 0:1], self.rstd[:, j:j + 1],
                                       ALU.subtract, ALU.mult)



def split_weights(nc, tag, jobs, sources=(), products=None):
    CHUNK = 2048
    pieces = []
    for src, hi, lo in jobs:
        if hi.ndim == 3:
            pieces.append((src, hi, lo))
            continue
        for c in range(0, src.shape[1], CHUNK):
            e = min(c + CHUNK, src.shape[1])
            pieces.append((src[:, c:e], hi[:, c:e], lo[:, c:e] if lo is not None else None))
    with ExitStack() as ctx:
        w = Names(nc, ctx, f"{tag}_w")
        NB = 3
        stage = w.sb("stage", [P, NB, CHUNK])
        junk = w.sb("junk", [P, 32])
        loaded = [w.sem(f"piece_loaded{i}") for i in range(NB)]
        hi_done = w.sem("hi_done")
        lo_done = w.sem("lo_done")
        src_loaded = w.sem("src_loaded")
        fold_ready = w.sem("fold_ready")
        fold_hi = w.sem("fold_hi")
        fold_free = w.sem("fold_free")
        bank = [w.ps(f"fold{i}", [P, 512]) for i in range(2)]
        factors = [w.sb(f"factor{k}", shape) for k, (_, shape) in enumerate(sources)]
        folds = products(factors, bank) if products else []
        block = ctx.enter_context(nc.Block())

        def slot(i):
            src, hi, _ = pieces[i]
            v = stage[:, i % NB, 0:src.shape[1]]
            return v.rearrange("p (a b) -> p a b", a=hi.shape[1]) if hi.ndim == 3 else v

        @block.sync
        def _(sp):
            for t, (src, _) in zip(factors, sources):
                sp.dma_start(flat(t), src).then_inc(src_loaded, 16)
            for i, (src, _, _) in enumerate(pieces):
                if i >= NB:
                    sp.wait_ge(lo_done, i - NB + 1)
                sp.dma_start(stage[:, i % NB, 0:src.shape[1]], src).then_inc(loaded[i % NB], 16)

        @block.scalar
        def _(act):
            for i, (_, hi, _) in enumerate(pieces):
                act.wait_ge(loaded[i % NB], 16 * (i // NB + 1))
                nc.scalar.activation(hi, slot(i), ACT.Copy).then_inc(hi_done, 1)
            for i, (_, view, hi, _) in enumerate(folds):
                act.wait_ge(fold_ready, i + 1)
                nc.scalar.activation(hi, view, ACT.Copy).then_inc(fold_hi, 1)

        @block.vector
        def _(dve):
            for i, (_, hi, lo) in enumerate(pieces):
                dve.wait_ge(hi_done, i + 1)
                ins = (nc.vector.memset(junk[:, i:i + 1], 0.0) if lo is None else
                       nc.vector.tensor_tensor(lo, slot(i), hi.bitcast(F32), ALU.subtract))
                ins.then_inc(lo_done, 1)
            for i, (_, view, hi, lo) in enumerate(folds):
                dve.wait_ge(fold_hi, i + 1)
                ins = (nc.vector.memset(junk[:, i:i + 1], 0.0) if lo is None else
                       nc.vector.tensor_tensor(lo, view, hi.bitcast(F32), ALU.subtract))
                ins.then_inc(fold_free, 1)

        @block.tensor
        def _(pe):
            if folds:
                pe.wait_ge(src_loaded, 16 * len(factors))
            for i, (matmuls, _, _, _) in enumerate(folds):
                if i >= 2:
                    pe.wait_ge(fold_free, i - 1)
                for part, col, n, stat, mov, start, stop in matmuls:
                    ins = nc.tensor.matmul(bank[i % 2][part:part + stat.shape[1], col:col + n], stat, mov,
                                           start=start, stop=stop)
                ins.then_inc(fold_ready, 1)



def feed_forward(nc, tag, x, const, hidden, gate, up, down, moe=None, out=None):
    NT = -(-hidden // P)
    width = [min(P, hidden - t * P) for t in range(NT)]
    with ExitStack() as ctx:
        m = Names(nc, ctx, tag)
        norm = Norm(m, const, "in")
        ident = const["ident"]
        xn = m.sb("xn", [P, TT, D])
        xTh = m.sb("xTh", [P, KD, SEQ], F32R)
        xTl = m.sb("xTl", [P, KD, SEQ], F32R)
        sg = m.sb("sg", [P, 2, SEQ])
        hf = m.sb("hf", [P, 2, SEQ])
        hg = m.sb("hg", [P, 2, SEQ]) if moe else None
        hh = m.sb("hh", [P, 2, SEQ], F32R)
        hl = m.sb("hl", [P, 2, SEQ], F32R)
        yT = m.sb("yT", [P, KD, SEQ])
        misc = [m.ps(f"misc{i}", [P, 512]) for i in range(2)]
        gb = [m.ps(f"gate{i}", [P, 512]) for i in range(2)]
        ub = [m.ps(f"up{i}", [P, 512]) for i in range(2)]
        yb = [m.ps(f"y{i}", [P, 512]) for i in range(KD)]

        xn_ready = m.sem("xn_ready")
        misc_ready = m.sem("misc_ready")
        misc_free = m.sem("misc_free")
        xh_ready = m.sem("xh_ready")
        g_ready = m.sem("g_ready")
        u_ready = m.sem("u_ready")
        s_done = m.sem("s_done")
        hf_done = m.sem("hf_done")
        hh_done = m.sem("hh_done")
        hl_done = m.sem("hl_done")
        dn_done = m.sem("dn_done")
        y_evac = m.sem("y_evac")
        x_done = m.sem("x_done")
        tmp_done = m.sem("tmp_done")
        stored = m.sem("stored")
        if moe:
            router, spread = moe
            ce = m.sb("ce", [P, TT, NE])
            mx = m.sb("mx", [P, TT])
            su = m.sb("su", [P, TT])
            rs = m.sb("rs", [P, TT])
            gtm = m.sb("gtm", [P, TT, NE, NE])
            eqm = m.sb("eqm", [P, TT, NE, NE])
            cnt = m.sb("cnt", [P, TT, NE])
            cmb = m.sb("cmb", [P, TT, 16])
            cT = m.sb("cT", [P, SEQ], F32R)
            exp_done = m.sem("exp_done")
            rt_link = m.sem("rt_link")
            cmb_ready = m.sem("cmb_ready")
            cT_ready = m.sem("cT_ready")
            set_up = m.sem("set_up")
        RT_LINKS = 8
        NMISC = KD + 2 + (2 + NT if moe else 0)
        block = ctx.enter_context(nc.Block())

        @block.gpsimd
        def _(pool):
            with pool.Fori(0, NSEQ) as b:
                norm.power(nc, pool, b * 2)
                norm.power(nc, pool, b * 2 + 1)

        @block.scalar
        def _(act):
            act.sem_inc(s_done, 2)
            with act.Fori(0, NSEQ) as b:
                for k in range(KD):
                    act.wait_ge(misc_ready, b * NMISC + k + 1)
                    nc.scalar.activation(xTh[:, k, :], misc[k % 2][:], ACT.Copy).then_inc(xh_ready, 1)
                if moe:
                    act.wait_ge(misc_free, b * NMISC + KD + 3)
                    nc.scalar.activation(ce[:], ce[:], ACT.Exp).then_inc(exp_done, 1)

                def high(t):
                    if moe:
                        act.wait_ge(misc_free, b * NMISC + KD + 2 + t + 3)
                    else:
                        act.wait_ge(hf_done, b * NT + t + 3)
                    act.wait_ge(dn_done, b * NT + t + 1)
                    nc.scalar.activation(hh[0:width[t], t % 2, :], (hg if moe else hf)[0:width[t], t % 2, :],
                                         ACT.Copy).then_inc(hh_done, 1)

                for t in range(NT):
                    act.wait_ge(g_ready, b * NT + t + 1)
                    act.wait_ge(hf_done, b * NT + t + 1)
                    nc.scalar.activation(sg[0:width[t], t % 2, :], gb[t % 2][0:width[t], :],
                                         ACT.Silu).then_inc(s_done, 1)
                    if t >= 1:
                        high(t - 1)
                high(NT - 1)

        @block.vector
        def _(dve):
            dve.sem_inc(misc_free, 2)
            dve.sem_inc(hf_done, 2)
            dve.sem_inc(y_evac, 2)
            if moe:
                nc.vector.memset(cT[:].bitcast(F32), 0.0).then_inc(set_up, 1)
                nc.vector.memset(cmb[:], 0.0).then_inc(set_up, 1)
                dve.wait_ge(set_up, 2)
                nc.vector.memset(cmb[:, :, NE:NE + 1], 1.0).then_inc(set_up, 1)
                dve.wait_ge(set_up, 3)
            with dve.Fori(0, NSEQ) as b:
                xb = [x[:, bass.ds(b * TT + j, 1), :].rearrange("p a d -> p (a d)") for j in range(TT)]
                norm.statistics(nc, dve, xb, b * 2)
                for j in range(TT):
                    ins = norm.apply(nc, xn[:, j, :], xb[j], j)
                ins.then_inc(xn_ready, 1)
                for k in range(KD):
                    dve.wait_ge(xh_ready, b * KD + k + 1)
                    nc.vector.tensor_tensor(xTl[:, k, :], misc[k % 2][:], xTh[:, k, :].bitcast(F32),
                                            ALU.subtract).then_inc(misc_free, 1)
                i = KD
                if moe:
                    links = [0]

                    def link(ins):
                        links[0] += 1
                        ins.then_inc(rt_link, 1)
                        dve.wait_ge(rt_link, b * RT_LINKS + links[0])

                    dve.wait_ge(misc_ready, b * NMISC + i + 1)
                    logits = at(misc[i % 2], 0, (NE, TT), (1, NE))
                    link(nc.vector.tensor_reduce(mx[:], logits, AX.X, ALU.max))
                    nc.vector.tensor_tensor(ce[:], logits, at(mx, 0, (1, TT), (0, NE)),
                                            ALU.subtract).then_inc(misc_free, 1)
                    dve.wait_ge(exp_done, b + 1)
                    link(nc.vector.tensor_reduce(su[:], ce[:], AX.X, ALU.add))
                    link(nc.vector.reciprocal(rs[:], su[:]))
                    link(nc.vector.tensor_tensor(ce[:], ce[:], at(rs, 0, (1, TT), (0, NE)), ALU.mult))
                    mine = at(ce, 0, (NE, TT), (1, NE), (0, NE))
                    other = at(ce, 0, (NE, TT), (0, NE), (1, NE))
                    nc.vector.tensor_tensor(gtm[:], other, mine, ALU.is_gt)
                    link(nc.vector.tensor_tensor(eqm[:], other, mine, ALU.is_equal))
                    before = at(const["before"], 0, (0, TT), (NE, NE), (1, NE))
                    link(nc.vector.tensor_tensor(eqm[:], eqm[:], before, ALU.mult))
                    link(nc.vector.tensor_tensor(gtm[:], gtm[:], eqm[:], ALU.add))
                    link(nc.vector.tensor_reduce(cnt[:], gtm[:], AX.X, ALU.add))
                    nc.vector.scalar_tensor_tensor(out=cmb[:, :, 0:NE], in0=cnt[:], scalar=1.5, in1=ce[:],
                                                   op0=ALU.is_lt, op1=ALU.mult).then_inc(cmb_ready, 1)
                    assert links[0] == RT_LINKS
                    i += 1
                    dve.wait_ge(misc_ready, b * NMISC + i + 1)
                    bank = misc[i % 2]
                    nc.vector.tensor_copy(cT[0:16, :], bank[0:16, :]).then_inc(cT_ready, 1)
                    dve.wait_ge(cT_ready, b + 1)
                    nc.vector.tensor_tensor(cT[32:48, :], bank[0:16, :], cT[0:16, :].bitcast(F32),
                                            ALU.subtract).then_inc(misc_free, 1)
                    i += 1

                def low(t):
                    dve.wait_ge(hh_done, b * NT + t + 1)
                    nc.vector.tensor_tensor(hl[0:width[t], t % 2, :], (hg if moe else hf)[0:width[t], t % 2, :],
                                            hh[0:width[t], t % 2, :].bitcast(F32), ALU.subtract).then_inc(hl_done, 1)

                for t in range(NT):
                    w = width[t]
                    if t >= 2:
                        low(t - 2)
                    dve.wait_ge(s_done, b * NT + t + 3)
                    dve.wait_ge(u_ready, b * NT + t + 1)
                    if t >= 2:
                        dve.wait_ge(hl_done, b * NT + t - 1)
                    nc.vector.tensor_tensor(hf[0:w, t % 2, :], sg[0:w, t % 2, :], ub[t % 2][0:w, :],
                                            ALU.mult).then_inc(hf_done, 1)
                    if moe:
                        dve.wait_ge(misc_ready, b * NMISC + i + 1)
                        dve.wait_ge(hf_done, b * NT + t + 3)
                        nc.vector.tensor_tensor(hg[0:w, t % 2, :], hf[0:w, t % 2, :], misc[i % 2][0:w, :],
                                                ALU.mult).then_inc(misc_free, 1)
                        i += 1
                low(NT - 2)
                low(NT - 1)
                dve.wait_ge(dn_done, b * NT + NT + 2)
                for k in range(KD):
                    nc.vector.tensor_copy(yT[:, k, :], yb[k][:]).then_inc(y_evac, 1)
                for c in range(2):
                    dve.wait_ge(misc_ready, b * NMISC + i + 1 + c)
                yt = [misc[(i + j // 2) % 2][:, (j % 2) * D:(j % 2 + 1) * D] for j in range(TT)]
                norm.statistics(nc, dve, yt, b * 2 + 1)
                for j in range(TT):
                    ins = norm.apply(nc, xn[:, j, :], yt[j], j)
                    if j % 2:
                        ins.then_inc(misc_free, 1)
                dve.wait_ge(misc_free, b * NMISC + NMISC + 2)
                for j in range(TT):
                    ins = nc.vector.tensor_tensor(xb[j], xb[j], xn[:, j, :], ALU.add)
                ins.then_inc(x_done, 1)
                dve.wait_ge(x_done, b + 1)

        @block.tensor
        def _(pe):
            pe.sem_inc(dn_done, 2)
            with pe.Fori(0, NSEQ) as b:
                pe.wait_ge(xn_ready, b + 1)
                for k in range(KD):
                    pe.wait_ge(misc_free, b * NMISC + k + 1)
                    for j in range(TT):
                        ins = nc.tensor.transpose(misc[k % 2][:, j * P:(j + 1) * P], xn[:, j, k * P:(k + 1) * P],
                                                  ident[:])
                    ins.then_inc(misc_ready, 1)
                pe.wait_ge(misc_free, b * NMISC + KD + 2)
                i = KD
                if moe:
                    for j in range(TT):
                        tok = slice(j * P, (j + 1) * P)
                        terms = [(xs[:, k, tok], r[:, k, :]) for k in range(KD)
                                 for xs, r in ((xTh, router[0]), (xTh, router[1]), (xTl, router[0]))]
                        for n, (st, mv) in enumerate(terms):
                            ins = nc.tensor.matmul(misc[i % 2][:, j * NE:(j + 1) * NE], st, mv, start=(n == 0),
                                                   stop=(n == len(terms) - 1))
                    ins.then_inc(misc_ready, 1)
                    i += 1

                def project(bank, w, t):
                    wd = width[t]
                    hid = slice(t * P, t * P + wd)
                    terms = [(ws[:, k, hid], xs[:, k, :]) for k in range(KD)
                             for ws, xs in ((w[0], xTh), (w[0], xTl), (w[1], xTh))]
                    for n, (st, mv) in enumerate(terms):
                        ins = nc.tensor.matmul(bank[0:wd, :], st, mv, start=(n == 0), stop=(n == len(terms) - 1))
                    return ins

                def down_product(t):
                    wd = width[t]
                    pe.wait_ge(hl_done, b * NT + t + 1)
                    terms = ((down[0], hh), (down[0], hl), (down[1], hh))
                    if t == 0:
                        pe.wait_ge(y_evac, b * KD + 2)
                    for k in range(KD):
                        for n, (wt, hs) in enumerate(terms):
                            ins = nc.tensor.matmul(yb[k][:], wt[0:wd, t, k * P:(k + 1) * P], hs[0:wd, t % 2, :],
                                                   start=(t == 0 and n == 0), stop=(t == NT - 1 and n == 2))
                    ins.then_inc(dn_done, 1)

                for t in range(NT):
                    pe.wait_ge(s_done, b * NT + t + 1)
                    project(gb[t % 2], gate, t).then_inc(g_ready, 1)
                    pe.wait_ge(hf_done, b * NT + t + 1)
                    project(ub[t % 2], up, t).then_inc(u_ready, 1)
                    if moe:
                        if t == 0:
                            pe.wait_ge(cmb_ready, b + 1)
                            for j in range(TT):
                                ins = nc.tensor.transpose(misc[i % 2][0:16, j * P:(j + 1) * P], cmb[:, j, :], ident[:])
                            ins.then_inc(misc_ready, 1)
                            i += 1
                            pe.wait_ge(misc_free, b * NMISC + i + 2)
                        pe.wait_ge(misc_free, b * NMISC + i + 1)
                        nc.tensor.matmul(misc[i % 2][0:width[t], :], spread[:, t * P:t * P + width[t]], cT[:],
                                         start=True, stop=True).then_inc(misc_ready, 1)
                        i += 1
                    if t >= 2:
                        down_product(t - 2)
                down_product(NT - 2)
                down_product(NT - 1)
                pe.wait_ge(y_evac, b * KD + KD + 2)
                for c in range(2):
                    pe.wait_ge(misc_free, b * NMISC + i + 1)
                    for j in range(2):
                        tok = slice((2 * c + j) * P, (2 * c + j + 1) * P)
                        for k in range(KD):
                            ins = nc.tensor.transpose(misc[i % 2][:, j * D + k * P:j * D + (k + 1) * P],
                                                      yT[:, k, tok], ident[:])
                    ins.then_inc(misc_ready, 1)
                    i += 1
                assert i == NMISC

        @block.sync
        def _(sp):
            if out is not None:
                with sp.Fori(0, NSEQ) as b:
                    sp.wait_ge(x_done, b + 1)
                    sp.dma_start(out[:, bass.ds(b * TT, TT), :], x[:, bass.ds(b * TT, TT), :]).then_inc(stored, 16)
                sp.wait_ge(stored, 16 * NSEQ)



HIGH = ("xT", "keyT", "queryT")


def attention_steps(latent, rslots):
    npair = (NH1 if latent else NH0) // HPAIR
    steps = []
    count = {"m": 0, "top": 0, "unit": 0, "evac": 0, "rope": 0, "high": 0}

    def add(kind, *args, ring=None):
        n = None
        if ring:
            n = count[ring]
            count[ring] += 1
        steps.append((kind, args, n))
        count["high"] += kind in HIGH

    def rope(kind, *args):
        n = count["m"]
        count["m"] += 1
        steps.append((kind, (*args, count["rope"]), n))
        count["rope"] += 1

    def query(p):
        return [lambda c=c: rope("query", p, c) for c in range(TT * (2 if latent else 1))]

    def queryT(p):
        return [lambda i=i: add("queryT", p, i, ring="m") for i in range(HPAIR if latent else HPAIR // 2)]

    def tops(p, q):
        n = P * (q + 1)
        per = max(1, 512 // n)
        per = {1: 4, 2: 2, 3: 1, 4: 1}[q + 1]
        return [lambda h=h: add("top", p, q, tuple(range(h, h + per)), ring="top")
                for h in range(0, HPAIR, per)]

    def topT(p, q):
        return [lambda: add("topT", p, q, ring="m")]

    def output(p):
        chain = [lambda: add("dload", p), lambda: add("recip", p)]
        for hp in range(HG + rslots - 1):
            if hp < HG:
                chain.append(lambda hp=hp: add("rload", p, hp))
            if hp >= rslots - 1:
                chain.append(lambda hp=hp: add("scale", p, hp - rslots + 1))
        return chain, [lambda k=k: add("oproj", p, k, ring="m") for k in range(KD)]

    def run(fs):
        for f in fs:
            f()

    last_keyT = 0 if latent else NKV0 // 2 - 1

    def early(place=None):
        return ([lambda: add("norm")] + [lambda k=k: add("xT", k, ring="m") for k in range(KD)] +
                [lambda j=j: rope("key", j) for j in range(TT)] +
                [lambda h=h: add("keyT", h, ring="m") for h in range(last_keyT)])

    def late():
        fs = [lambda: add("cnorm")] if latent else [lambda j=j: add("value", j, ring="m") for j in range(TT)]
        return (fs + [lambda: add("keyT", last_keyT, ring="m")] + query(0) + queryT(0) + tops(0, 0) +
                topT(0, 0) + tops(0, 1))

    run(early() + late())
    if count["m"] % 2:
        add("even", ring="m")
    assert count["top"] % 2 == 0
    prologue, before = steps, dict(count)
    steps = []
    for k in count:
        count[k] = 0

    units = [(p, q, g, k) for p in range(npair) for q in range(TT) for g in range(2) for k in range(q + 1)]

    def finish(u):
        add("pv", *units[u], u)
        p, q, g, k = units[u]
        if k == q:
            add("evac", p, q, g, ring="evac")

    UNITS = TT * (TT + 1)

    def beside(p):
        after = [[] for _ in range(UNITS)]

        def place(items, places):
            for f, n in zip(items, places, strict=True):
                after[n].append(f)

        place(topT(p, 1), [0])
        place(tops(p, 2), [0, 1, 1, 2, 2, 3, 3, 3])
        place(topT(p, 2), [4])
        place(tops(p, 3), [5, 5, 6, 6, 7, 7, 8, 8])
        place(topT(p, 3), [9])
        if p:
            chain, proj = output(p - 1)
            place(chain, [3, 5, 6, 8, 8, 10, 10, 12, 12, 14] if rslots == 1 else [3, 5, 6, 6, 8, 8, 10, 10, 12, 14])
            place(proj, [15, 16])
        if p + 1 == npair:
            place(early(), [5, 6, 7, 9, 10, 11, 12, 13, 14, 15][:7 + last_keyT])
        if p + 1 < npair:
            place(query(p + 1), range(3, 11) if latent else [4, 6, 8, 10])
            place(queryT(p + 1), [11, 12, 12, 13, 13, 14, 14, 15] if latent else [11, 12, 13, 14])
            place(tops(p + 1, 0), [16, 16])
            place(tops(p + 1, 1), [16, 17, 17, 18])
            place(topT(p + 1, 0), [18])
        return after

    u = 0
    for p in range(npair):
        for share in beside(p):
            add("unit", *units[u], ring="unit")
            if u >= 2:
                finish(u - 2)
            run(share)
            u += 1
    finish(u - 2)
    finish(u - 1)
    chain, proj = output(npair - 1)
    end = chain + proj + [lambda c=c: add("yT", c, ring="m") for c in range(2)] + [lambda: add("residual")]
    start = late()
    ahead = 0
    for t, f in enumerate(end):
        f()
        upto = -(-(t + 1) * len(start) // (len(end) - 3))
        run(start[ahead:upto])
        ahead = max(ahead, upto)
    if count["m"] % 2:
        add("even", ring="m")
    assert ahead >= len(start) and count["top"] % 2 == 0
    before["norm"], count["norm"] = 1, 1
    return prologue, before, steps, count, npair


def last_item(steps, s, kind, *args):
    found = [i for k, a, i in steps[:s] if k == kind and a[:len(args)] == args]
    return found[-1] if found else -1


def attention(nc, tag, x, const, w, a):
    latent = w["latent"]
    prologue, before, body, count, NPAIR = attention_steps(latent, w["rslots"])
    NM, NTOP, NU, NG, NR, NHIGH = (count[k] for k in ("m", "top", "unit", "evac", "rope", "high"))
    none = dict.fromkeys(before, 0)

    def numbering(b, base):
        return lambda ring, i: base[ring] + b * count[ring] + i
    scale = w["scale"]
    KW = P if latent else NKV0 * HD0
    with ExitStack() as ctx:
        m = Names(nc, ctx, tag)
        norm = Norm(m, const, "in")
        norm_y = Norm(m, const, "out")
        ident = const["ident"]
        yT = m.sb("yT", [P, KD, SEQ])
        addend = at(yT, 0, (D, TT), (1, D))
        xTh = m.sb("xTh", [P, KD, SEQ], F32R)
        xTl = m.sb("xTl", [P, KD, SEQ], F32R)
        nkey = 1 if latent else NKV0
        keyh = m.sb("keyh", [P, nkey, SEQ], F32R)
        keyl = m.sb("keyl", [P, nkey, SEQ], F32R)
        VH = 1 if latent else NKV0 // 2
        VW = P if latent else 192
        V = m.sb("V", [P, TT, VH, VW])
        qa = m.sb("qa", [P, 2, HPAIR, SEQ], F32R)
        qb = m.sb("qb", [P, 2, HPAIR, SEQ], F32R) if latent else None
        QW = HPAIR * (P if latent else HD0)
        RW = max(QW, KW)
        rot = m.sb("rot", [P, TT, RW])
        xnt = at(rot, 0, (D, TT), (1, D))
        crossed = m.sb("crossed", [P, 2, 512])
        probs = m.sb("probs", [P, 3, 512])
        out = m.sb("out", [P, 2, HG, SEQ])
        mcol = m.sb("mcol", [P, TT, HPAIR])
        mrow = m.sb("mrow", [P, 2, HPAIR, P], F32R)
        drow = m.sb("drow", [P, 512])
        dcol = m.sb("dcol", [P, 32])
        rcol = dcol
        RSLOTS = w["rslots"]
        rtile = m.sb("rtile", [P, RSLOTS, SEQ])
        misc = [m.ps(f"misc{i}", [P, 512]) for i in range(2)]
        topb = [m.ps(f"top{i}", [P, 512]) for i in range(2)]
        score = [m.ps(f"score{i}", [P, 512]) for i in range(2)]
        pvb = [m.ps(f"pv{i}", [P, 512]) for i in range(2)]
        d_dram = nc.dram_tensor(f"{tag}_rowsums", [NPAIR, HPAIR, SEQ], F32, kind="Internal").ap()
        r_dram = nc.dram_tensor(f"{tag}_recips", [NPAIR, HPAIR, SEQ], F32, kind="Internal").ap()
        if not latent:
            wo = m.sb("wo", [P, HG, D])
        else:
            craw = m.sb("craw", [P, TT, 64])
            csq = m.sb("csq", [P, TT, 64])
            css = m.sb("css", [P, TT])
            crs = m.sb("crs", [P, TT])

        pause = m.sb("pause", [P, 3])
        set_up = m.sem("set_up")
        xn_ready = m.sem("xn_ready")
        misc_ready = m.sem("misc_ready")
        misc_free = m.sem("misc_free")
        high_done = m.sem("high_done")
        parts = m.sem("parts")
        rotated = m.sem("rotated")
        top_ready = m.sem("top_ready")
        top_free = m.sem("top_free")
        score_ready = m.sem("score_ready")
        probs_ready = m.sem("probs_ready")
        pv_ready = m.sem("pv_ready")
        pv_free = m.sem("pv_free")
        drow_done = m.sem("drow_done")
        d_stored = [m.sem(f"d_stored{i}") for i in range(4)]
        d_loaded = m.sem("d_loaded")
        recips = m.sem("recips")
        r_stored = m.sem("r_stored")
        passed = m.sem("passed")
        r_loaded = [m.sem(f"r_loaded{i}") for i in range(RSLOTS)]
        scaled = m.sem("scaled")
        wo_loaded = m.sem("wo_loaded")
        x_done = m.sem("x_done")
        c_link = m.sem("c_link")
        c_var = m.sem("c_var")
        c_rstd = m.sem("c_rstd")
        c_ready = m.sem("c_ready")
        block = ctx.enter_context(nc.Block())

        def vals(h, k):
            return V[:, k, h // 2, 64 * (h % 2):64 * (h % 2) + P]

        def rotated_at(kind, args, split=False):
            if kind == "key":
                off, step, heads = args[0] * RW, 64, 1 if latent else NKV0
            elif latent:
                off, step, heads = (args[1] // 2) * RW + (args[1] % 2) * 512, P, HG
            else:
                off, step, heads = args[1] * RW, 64, HPAIR
            return at(rot, off, (step, heads), (32, 2), (1, 32)) if split else at(rot, off, (step, heads), (1, 64))

        @block.gpsimd
        def _(pool):
            pool.sem_inc(rotated, 2)

            def section(steps, b, base):
                item = numbering(b, base)
                for kind, args, i in steps:
                    if kind == "norm":
                        norm.power(nc, pool, b + base["norm"])
                    if kind == "residual":
                        norm_y.power(nc, pool, b)
                    if kind in ("key", "query"):
                        r = args[-1]
                        pool.wait_ge(parts, item("rope", r) + 1)
                        heads = (1 if latent else NKV0) if kind == "key" else HG if latent else HPAIR
                        dst = rotated_at(kind, args)
                        nc.gpsimd.tensor_tensor(dst, dst, at(crossed, r % 2 * 512, (64, heads), (1, 64)),
                                                ALU.add).then_inc(rotated, 1)
                    if kind == "cnorm":
                        pool.wait_ge(c_var, b + base["norm"] + 1)
                        nc.gpsimd.tensor_tensor(crs[:], css[:], const["minus_half"][:, 0:TT],
                                                ALU.pow).then_inc(c_rstd, 1)

            section(prologue, 0, none)
            with pool.Fori(0, NSEQ) as b:
                section(body, b, before)

        @block.scalar
        def _(act):
            act.sem_inc(probs_ready, 2)
            act.sem_inc(pv_free, 2)

            def section(steps, b, base):
                item = numbering(b, base)
                for s, (kind, args, i) in enumerate(steps):
                    if kind in HIGH:
                        act.wait_ge(misc_ready, item("m", i) + 1)
                        bank = misc[i % 2]
                    if kind == "xT":
                        nc.scalar.activation(xTh[:, args[0], :], bank[:], ACT.Copy).then_inc(high_done, 1)
                    if kind == "keyT":
                        if latent:
                            nc.scalar.activation(keyh[:, 0, :], bank[:], ACT.Copy).then_inc(high_done, 1)
                        else:
                            for src in (0, 64):
                                for dst in (0, 64):
                                    ins = nc.scalar.activation(keyh[dst:dst + 64, 2 * args[0] + src // 64, :],
                                                               bank[src:src + 64, :], ACT.Copy)
                            ins.then_inc(high_done, 1)
                    if kind == "queryT":
                        p, n = args
                        if latent:
                            nc.scalar.activation(qa[:, p % 2, n, :], bank[:], ACT.Copy).then_inc(high_done, 1)
                        else:
                            nc.scalar.activation(qa[0:64, p % 2, 2 * n, :], bank[0:64, :], ACT.Copy)
                            nc.scalar.activation(qa[64:128, p % 2, 2 * n + 1, :], bank[64:128, :],
                                                 ACT.Copy).then_inc(high_done, 1)
                    if kind == "unit":
                        act.wait_ge(score_ready, b * NU + i + 1)
                        nc.scalar.activation(probs[:, i % 3, :], score[i % 2][:], ACT.Exp,
                                             scale=scale).then_inc(probs_ready, 1)
                    if kind == "evac":
                        p, q, g = args
                        act.wait_ge(pv_ready, b * NG + i + 1)
                        bank = pvb[i % 2]
                        slot = i % 4
                        act.wait_ge(d_stored[slot], (b * (NG // 4) + i // 4 + 1) * 16)
                        vals_at, sums_at = (0, 64) if latent or g == 0 else (64, 0)
                        nc.scalar.activation(drow[32 * slot:32 * slot + 1, :], bank[sums_at:sums_at + 1, :],
                                             ACT.Copy).then_inc(drow_done, 1)
                        for odd in range(2):
                            dst = bass.AP(tensor=out[:].tensor,
                                          offset=out[64 * odd:64 * odd + 64, p % 2, 2 * g, q * P:q * P + P].offset,
                                          ap=[[out[:].ap[0][0], 64], [SEQ, 2], [1, P]])
                            v = bank[vals_at:vals_at + 64, :].rearrange("p (h n) -> p h n", h=HG)
                            ins = nc.scalar.activation(dst, v[:, odd::2, :], ACT.Copy)
                        ins.then_inc(pv_free, 1)

            section(prologue, 0, none)
            with act.Fori(0, NSEQ) as b:
                section(body, b, before)

        @block.vector
        def _(dve):
            dve.sem_inc(misc_free, 2)
            dve.sem_inc(top_free, 2)
            dve.sem_inc(scaled, RSLOTS)
            nc.vector.memset(mrow[:].bitcast(F32), 0.0).then_inc(set_up, 1)
            nc.vector.memset(V[:, :, :, 64:128], 1.0).then_inc(set_up, 1)
            dve.wait_ge(set_up, 2)

            def tiles_of(n):
                return [x[:, bass.ds(n * TT + j, 1), :].rearrange("p a d -> p (a d)") for j in range(TT)]

            def section(steps, b, base):
                item = numbering(b, base)
                high = 0
                for s, (kind, args, i) in enumerate(steps):
                    if kind == "norm":
                        n = (b + base["norm"]) % NSEQ
                        xb = tiles_of(n) if base["norm"] else [x[:, j, :] for j in range(TT)]
                        norm.statistics(nc, dve, xb, b + base["norm"])
                        for j in range(TT):
                            ins = norm.apply(nc, xnt[:, j, :], xb[j], j)
                        ins.then_inc(xn_ready, 1)
                    if kind in HIGH:
                        high += 1
                        dve.wait_ge(high_done, item("high", high - 1) + 1)
                        bank = misc[i % 2]
                    if kind == "xT":
                        k, = args
                        nc.vector.tensor_tensor(xTl[:, k, :], bank[:], xTh[:, k, :].bitcast(F32),
                                                ALU.subtract).then_inc(misc_free, 1)
                    if kind == "keyT":
                        h, = args
                        if latent:
                            ins = nc.vector.tensor_tensor(keyl[:, 0, :], bank[:], keyh[:, 0, :].bitcast(F32),
                                                          ALU.subtract)
                        else:
                            for src in (0, 64):
                                for dst in (0, 64):
                                    k = 2 * h + src // 64
                                    ins = nc.vector.tensor_tensor(keyl[dst:dst + 64, k, :], bank[src:src + 64, :],
                                                                  keyh[dst:dst + 64, k, :].bitcast(F32), ALU.subtract)
                        ins.then_inc(misc_free, 1)
                    if kind == "queryT":
                        p, n = args
                        if latent:
                            nc.vector.tensor_tensor(qb[:, p % 2, n, :], bank[:], qa[:, p % 2, n, :].bitcast(F32),
                                                    ALU.subtract).then_inc(misc_free, 1)
                        else:
                            e, o = qa[:, p % 2, 2 * n, :], qa[:, p % 2, 2 * n + 1, :]
                            nc.vector.tensor_tensor(e[64:128], bank[0:64, :], e[0:64].bitcast(F32), ALU.subtract)
                            nc.vector.tensor_tensor(o[0:64], bank[64:128, :], o[64:128].bitcast(F32),
                                                    ALU.subtract).then_inc(misc_free, 1)
                    if kind in ("key", "query"):
                        r = args[-1]
                        dve.wait_ge(misc_ready, item("m", i) + 1)
                        dve.wait_ge(rotated, item("rope", r) + 1)
                        bank = misc[i % 2]
                        if kind == "key":
                            j, (cos, sin) = args[0], w["key_tables"]
                            heads, step = (1, 64) if latent else (NKV0, 64)
                        else:
                            j = args[1] // 2 if latent else args[1]
                            cos, sin = w["query_tables"]
                            heads, step = (HG, P) if latent else (HPAIR, 64)
                        nc.vector.tensor_tensor(rotated_at(kind, args, split=True),
                                                at(bank, 0, (step, heads), (32, 2), (1, 32)),
                                                at(cos, j * 32, (0, heads), (0, 2), (1, 32)), ALU.mult)
                        for lo, hi in ((0, 32), (32, 0)):
                            ins = nc.vector.tensor_tensor(at(crossed, r % 2 * 512 + lo, (64, heads), (1, 32)),
                                                          at(bank, hi, (step, heads), (1, 32)),
                                                          at(sin, j * 64 + lo, (0, heads), (1, 32)), ALU.mult)
                        ins.then_inc(parts, 1)
                        if latent and kind == "key":
                            nc.vector.tensor_copy(craw[:, j, :], bank[:, 64:128]).then_inc(misc_free, 1)
                        elif latent:
                            nc.vector.tensor_copy(at(rot, j * RW + (args[1] % 2) * 512 + 64, (P, HG), (1, 64)),
                                                  at(bank, 64, (P, HG), (1, 64))).then_inc(misc_free, 1)
                        else:
                            dve.wait_ge(parts, item("rope", r) + 1)
                            nc.vector.memset(pause[:, 0:1], 0.0).then_inc(misc_free, 1)
                    if kind == "value":
                        j, = args
                        dve.wait_ge(misc_ready, item("m", i) + 1)
                        nc.vector.tensor_copy(at(V, j * VH * VW, (VW, VH), (P, 2), (1, 64)),
                                              at(misc[i % 2], 0, (P, VH), (64, 2), (1, 64))).then_inc(misc_free, 1)
                    if kind == "cnorm":
                        dve.wait_ge(misc_free, item("m", last_item(steps, s, "key")) + 3)
                        nc.vector.tensor_tensor(csq[:], craw[:], craw[:], ALU.mult).then_inc(c_link, 1)
                        dve.wait_ge(c_link, (b + base["norm"]) * 3 + 1)
                        nc.vector.tensor_reduce(css[:], csq[:], AX.X, ALU.add).then_inc(c_link, 1)
                        dve.wait_ge(c_link, (b + base["norm"]) * 3 + 2)
                        nc.vector.tensor_scalar(css[:], css[:], 1.0 / LAT1, RMS_EPS, ALU.mult, ALU.add).then_inc(c_var, 1)
                        dve.wait_ge(c_rstd, b + base["norm"] + 1)
                        nc.vector.tensor_tensor(csq[:], craw[:], at(crs, 0, (1, TT), (0, 64)), ALU.mult).then_inc(c_link, 1)
                        dve.wait_ge(c_link, (b + base["norm"]) * 3 + 3)
                        if base["norm"]:
                            dve.wait_ge(pv_ready, b * NG + NG)
                        weight = at(w["norm_w"], 0, (0, TT), (1, 64))
                        nc.vector.tensor_tensor(V[:, :, 0, 0:64], csq[:], weight, ALU.mult)
                        nc.vector.tensor_tensor(at(rot, 64, (RW, TT), (1, 64)), csq[:], weight,
                                                ALU.mult).then_inc(c_ready, 1)
                    if kind == "top":
                        p, q, heads = args
                        dve.wait_ge(top_ready, item("top", i) + 1)
                        n = P * (q + 1)
                        v = topb[i % 2][:, 0:len(heads) * n].rearrange("p (h n) -> p h n", h=len(heads))
                        nc.vector.tensor_reduce(mcol[:, q, heads[0]:heads[-1] + 1], v, AX.X,
                                                ALU.max).then_inc(top_free, 1)
                    if kind == "topT":
                        p, q = args
                        dve.wait_ge(misc_ready, item("m", i) + 1)
                        nc.vector.tensor_tensor(mrow[0:HPAIR, q % 2, :, :],
                                                bass.AP(tensor=misc[i % 2][:].tensor, offset=misc[i % 2][:].offset,
                                                        ap=[[misc[i % 2][:].ap[0][0], HPAIR], [0, HPAIR], [1, P]]),
                                                bass.AP(tensor=ident[:].tensor, offset=ident[:].offset,
                                                        ap=[[ident[:].ap[0][0], HPAIR], [1, HPAIR], [0, P]]),
                                                ALU.mult).then_inc(misc_free, 1)
                    if kind == "even":
                        dve.wait_ge(misc_ready, item("m", i) + 1)
                        nc.vector.memset(pause[:, 1:2], 0.0).then_inc(misc_free, 1)
                    if kind == "recip":
                        p, = args
                        dve.wait_ge(d_loaded, (b * NPAIR + p + 1) * 16)
                        nc.vector.reciprocal(rcol[:], dcol[:]).then_inc(recips, 1)
                    if kind == "scale":
                        p, hp = args
                        n = (b * NPAIR + p) * (HG // RSLOTS) + hp // RSLOTS
                        dve.wait_ge(r_loaded[hp % RSLOTS], (n + 1) * 32)
                        dve.wait_ge(pv_free, b * NG + (p + 1) * 2 * TT + 2)
                        o = out[:, p % 2, hp, :]
                        nc.vector.tensor_tensor(o, o, rtile[:, hp % RSLOTS, :], ALU.mult).then_inc(scaled, 1)
                    if kind == "oproj":
                        p, k = args
                        dve.wait_ge(misc_ready, item("m", i) + 1)
                        if p == 0:
                            nc.vector.tensor_copy(yT[:, k, :], misc[i % 2][:]).then_inc(misc_free, 1)
                        else:
                            nc.vector.tensor_tensor(yT[:, k, :], yT[:, k, :], misc[i % 2][:],
                                                    ALU.add).then_inc(misc_free, 1)
                    if kind == "residual":
                        c = last_item(steps, s, "yT", 0)
                        dve.wait_ge(misc_ready, item("m", last_item(steps, s, "yT", 1)) + 1)
                        half = [misc[c % 2], misc[last_item(steps, s, "yT", 1) % 2]]
                        yt = [half[j // 2][:, (j % 2) * D:(j % 2 + 1) * D] for j in range(TT)]
                        norm_y.statistics(nc, dve, yt, b)
                        for j in range(TT):
                            ins = norm_y.apply(nc, addend[:, j, :], yt[j], j)
                            if j % 2:
                                ins.then_inc(misc_free, 1)
                        dve.wait_ge(misc_free, item("m", last_item(steps, s, "yT", 1)) + 3)
                        xb = tiles_of(b)
                        for j in range(TT):
                            ins = nc.vector.tensor_tensor(xb[j], xb[j], addend[:, j, :], ALU.add)
                        ins.then_inc(x_done, 1)
                        dve.wait_ge(x_done, b + 1)
                        nc.vector.memset(pause[:, 2:3], 0.0)

            section(prologue, 0, none)
            with dve.Fori(0, NSEQ) as b:
                section(body, b, before)

        @block.tensor
        def _(pe):
            pe.wait_ge(set_up, 2)

            def section(steps, b, base):
                item = numbering(b, base)
                for s, (kind, args, i) in enumerate(steps):
                    if kind in ("xT", "key", "value", "keyT", "query", "queryT", "topT", "oproj", "yT", "even"):
                        pe.wait_ge(misc_free, item("m", i) + 1)
                        bank = misc[i % 2]
                    if kind == "xT":
                        k, = args
                        pe.wait_ge(xn_ready, b + base["norm"] + 1)
                        for j in range(TT):
                            ins = nc.tensor.transpose(bank[:, j * P:(j + 1) * P], xnt[:, j, k * P:(k + 1) * P],
                                                      ident[:])
                        ins.then_inc(misc_ready, 1)
                    if kind in ("key", "value", "query"):
                        if kind == "key":
                            j, n = args[0], (P if latent else 512)
                            wh, wl = (t[:, :, 0:n] for t in w["key"])
                            if j == 0:
                                pe.wait_ge(misc_free, item("m", last_item(steps, s, "xT")) + 3)
                        elif kind == "value":
                            j, n = args[0], 512
                            wh, wl = (t[:, :, 512:1024] for t in w["key"])
                        else:
                            p, c, _ = args
                            j, half = divmod(c, 2) if latent else (c, 0)
                            n = 512
                            off = p * QW + half * 512
                            wh, wl = (t[:, :, off:off + 512] for t in w["query"])
                        tok = slice(j * P, (j + 1) * P)
                        terms = [(xs[:, k, tok], ws[:, k, :]) for k in range(KD)
                                 for xs, ws in ((xTh, wh), (xTh, wl), (xTl, wh))]
                        for t, (st, mv) in enumerate(terms):
                            ins = nc.tensor.matmul(bank[:, 0:n], st, mv, start=(t == 0), stop=(t == len(terms) - 1))
                        ins.then_inc(misc_ready, 1)
                        if kind != "value":
                            last_rope = item("rope", args[-1])
                    if kind == "keyT":
                        pe.wait_ge(rotated, last_rope + 3)
                        if latent:
                            pe.wait_ge(c_ready, b + base["norm"] + 1)
                        for j in range(TT):
                            ins = nc.tensor.transpose(bank[:, j * P:(j + 1) * P],
                                                      rot[:, j, args[0] * P:(args[0] + 1) * P], ident[:])
                        ins.then_inc(misc_ready, 1)
                    if kind == "queryT":
                        pe.wait_ge(rotated, last_rope + 3)
                        if latent:
                            pe.wait_ge(misc_free, item("m", last_item(steps, s, "query", args[0])) + 3)
                        for j in range(TT):
                            ins = nc.tensor.transpose(bank[:, j * P:(j + 1) * P],
                                                      rot[:, j, args[1] * P:(args[1] + 1) * P], ident[:])
                        ins.then_inc(misc_ready, 1)
                    if kind == "top":
                        p, q, heads = args
                        pe.wait_ge(top_free, item("top", i) + 1)
                        if q == 0:
                            pe.wait_ge(misc_free, item("m", last_item(steps, s, "queryT", p)) + 3)
                        n = P * (q + 1)
                        for c, h in enumerate(heads):
                            kh = keyh[:, 0 if latent else 2 * p + h // HG, 0:n]
                            nc.tensor.matmul(topb[i % 2][:, c * n:(c + 1) * n], qa[:, p % 2, h, q * P:(q + 1) * P], kh,
                                             start=True, stop=False)
                            ins = nc.tensor.matmul(topb[i % 2][:, (c + 1) * n - P:(c + 1) * n], w["identb"][:],
                                                   w["mask_q"][:], start=False, stop=True)
                        ins.then_inc(top_ready, 1)
                    if kind == "topT":
                        p, q = args
                        pe.wait_ge(top_free, item("top", last_item(steps, s, "top", p, q)) + 3)
                        nc.tensor.transpose(bank[0:HPAIR, 0:P], mcol[:, q, :], ident[:]).then_inc(misc_ready, 1)
                    if kind == "even":
                        nc.tensor.transpose(bank[0:HPAIR, 0:P], mcol[:, 0, :], ident[:]).then_inc(misc_ready, 1)
                    if kind == "unit":
                        p, q, g, k = args
                        pe.wait_ge(probs_ready, b * NU + i + 1)
                        if g == 0 and k == 0:
                            pe.wait_ge(misc_free, item("m", last_item(steps, s, "topT", p, q)) + 3)
                        bank = score[i % 2]
                        kt = slice(k * P, (k + 1) * P)
                        kv = 0 if latent else 2 * p + g
                        qs = [t[:, p % 2, g * HG:(g + 1) * HG, q * P:(q + 1) * P] for t in (qa, qb) if t is not None]
                        terms = [(keyh[:, kv, kt], qs[0]), (keyl[:, kv, kt], qs[0])]
                        if latent:
                            terms.append((keyh[:, kv, kt], qs[1]))
                        terms.append((w["minus_one"][:], mrow[:, q % 2, g * HG:(g + 1) * HG, :]))
                        if k == q:
                            terms.append((w["identb"][:], at(w["mask_k"], 0, (0, HG), (1, P))))
                        for t, (st, mv) in enumerate(terms):
                            ins = nc.tensor.matmul(bank[:], st, mv, start=(t == 0), stop=(t == len(terms) - 1))
                        ins.then_inc(score_ready, 1)
                    if kind == "pv":
                        p, q, g, k, u = args
                        group = (p * TT + q) * 2 + g
                        pe.wait_ge(probs_ready, b * NU + u + 3)
                        if k == 0:
                            pe.wait_ge(pv_free, b * NG + group + 1)
                        ins = nc.tensor.matmul(pvb[group % 2][:], vals(0 if latent else 2 * p + g, k),
                                               probs[:, u % 3, :], start=(k == 0), stop=(k == q))
                        if k == q:
                            ins.then_inc(pv_ready, 1)
                    if kind == "oproj":
                        p, k = args
                        pe.wait_ge(scaled, (b * NPAIR + p + 1) * HG + RSLOTS)
                        if not latent:
                            pe.wait_ge(wo_loaded, (b * NPAIR + p + 1) * 16)
                        for hp in range(HG):
                            st = (w["out"][:, p * HG + hp, k * P:(k + 1) * P] if latent else
                                  wo[:, hp, k * P:(k + 1) * P])
                            ins = nc.tensor.matmul(bank[:], st, out[:, p % 2, hp, :], start=(hp == 0), stop=(hp == HG - 1))
                        ins.then_inc(misc_ready, 1)
                    if kind == "yT":
                        c, = args
                        if c == 0:
                            pe.wait_ge(misc_free, item("m", last_item(steps, s, "oproj")) + 3)
                        for j in range(2):
                            tok = slice((2 * c + j) * P, (2 * c + j + 1) * P)
                            for k in range(KD):
                                ins = nc.tensor.transpose(bank[:, j * D + k * P:j * D + (k + 1) * P],
                                                          yT[:, k, tok], ident[:])
                        ins.then_inc(misc_ready, 1)

            section(prologue, 0, none)
            with pe.Fori(0, NSEQ) as b:
                section(body, b, before)

        @block.sync
        def _(sp):
            for s in d_stored:
                sp.sem_inc(s, 16)
            if not latent:
                sp.dma_start(flat(wo), w["out"][0]).then_inc(wo_loaded, 16)
            with sp.Fori(0, NSEQ) as b:
                for s, (kind, args, i) in enumerate(body):
                    if kind == "evac":
                        p, q, g = args
                        slot = i % 4
                        sp.wait_ge(drow_done, b * NG + i + 1)
                        sp.dma_start(d_dram[p:p + 1, g * HG:(g + 1) * HG, q * P:(q + 1) * P],
                                     drow[32 * slot:32 * slot + 1, :].rearrange("p (h n) -> p h n", h=HG)
                                     ).then_inc(d_stored[slot], 16)
                    if kind == "dload":
                        p, = args
                        last = (p + 1) * 2 * TT - 1
                        for g in range(last - 3, last + 1):
                            sp.wait_ge(d_stored[g % 4], (b * (NG // 4) + g // 4 + 2) * 16)
                        sp.dma_start(dcol[:], d_dram[p].rearrange("h n -> (h n)").rearrange("(a c) -> a c", c=32)
                                     ).then_inc(d_loaded, 16)
                    if kind == "recip":
                        p, = args
                        sp.wait_ge(recips, b * NPAIR + p + 1)
                        sp.dma_start(r_dram[p].rearrange("h n -> (h n)").rearrange("(a c) -> a c", c=32),
                                     rcol[:]).then_inc(r_stored, 16)
                        sp.wait_ge(r_stored, (b * NPAIR + p + 1) * 16)
                        sp.sem_inc(passed, 1)
                    if kind == "rload":
                        p, hp = args
                        sp.wait_ge(scaled, (b * NPAIR + p) * HG + hp + 1)
                        for odd in range(2):
                            row = r_dram[p, 2 * hp + odd, :]
                            sp.dma_start(rtile[64 * odd:64 * odd + 64, hp % RSLOTS, :],
                                         bass.AP(tensor=row.tensor, offset=row.offset, ap=[[0, 64], [1, SEQ]])
                                         ).then_inc(r_loaded[hp % RSLOTS], 16)
                    if kind == "oproj" and args[1] == KD - 1 and not latent:
                        p, _ = args
                        sp.wait_ge(misc_ready, before["m"] + b * NM + i + 1)
                        sp.dma_start(flat(wo), w["out"][(p + 1) % NPAIR]).then_inc(wo_loaded, 16)
            if not latent:
                sp.wait_ge(wo_loaded, (NSEQ * NPAIR + 1) * 16)


def attention_constants(nc, m, a, tag, rows):
    c = {"identb": m.sb("identb", [P, P], BF16), "mask_q": m.sb("mask_q", [P, P], BF16),
         "mask_k": m.sb("mask_k", [P, P], BF16), "minus_one": m.sb("minus_one", [P, P], F32R)}
    raw = [("ident", c["identb"]), ("mask_q", c["mask_q"]), ("mask_k", c["mask_k"])]
    tables = {n: m.sb(n, shape) for n, shape in rows.items()}
    with ExitStack() as c0:
        s = c0.enter_context(nc.semaphore(f"{tag}_table_loaded"))
        made = c0.enter_context(nc.semaphore(f"{tag}_masks_made"))
        stage = c0.enter_context(nc.sbuf_tensor(f"{tag}_mask_stage", [P, 4, P], F32))
        block = c0.enter_context(nc.Block())

        @block.sync
        def _(sp):
            for n, (src, _) in enumerate(raw):
                sp.dma_start(stage[:, n, :], a[src]).then_inc(s, 16)
            for n in tables:
                sp.dma_start(flat(tables[n]), a[f"{tag}_{n}"]).then_inc(s, 16)
            sp.wait_ge(s, 16 * (len(raw) + len(tables)))

        @block.vector
        def _(dve):
            nc.vector.memset(stage[:, 3, :], -1.0).then_inc(made, 1)
            dve.wait_ge(s, 16 * (len(raw) + len(tables)))
            dve.wait_ge(made, 1)
            for n, (_, dst) in enumerate(raw):
                nc.vector.tensor_copy(dst[:], stage[:, n, :])
            nc.vector.tensor_copy(c["minus_one"][:], stage[:, 3, :]).then_inc(made, 1)
            dve.wait_ge(made, 2)
    return c | tables


def attention0(nc, a, x, const):
    with ExitStack() as ctx:
        m = Names(nc, ctx, "a0")
        query = [m.sb(f"wquery{s}", [P, KD, NH0 * HD0], F32R) for s in "hl"]
        key = [m.sb(f"wkey{s}", [P, KD, 2 * NKV0 * HD0], F32R) for s in "hl"]
        G, HALF = 2 * NKV0, HD0 // 2

        def products(f, bank):
            down, upk, upv = f
            for k in range(KD):
                hid = slice(k * P, (k + 1) * P)
                stat = [down[:, r, hid] for r in range(KD)]
                yield ([(0, 0, D, stat[r], upk[:, r, :], r == 0, r == KD - 1) for r in range(KD)],
                       None, [at(t, k * 1024 + ROPE0, (HALF, G), (1, HALF - ROPE0)) for t in key])
                yield ([(0, 0, 512, stat[r], upv[:, r, :], r == 0, r == KD - 1) for r in range(KD)],
                       None, [t[:, k, 512:1024] for t in key])

        def listed(f, bank):
            got = []
            for i, (mm, _, (hi, lo)) in enumerate(products(f, bank)):
                view = at(bank[i % 2], 0, (16, G), (1, 16)) if i % 2 == 0 else bank[i % 2][:]
                got.append((mm, view, hi, lo))
            return got

        jobs = [(a["a0_query"], flat(query[0]), flat(query[1]))]
        for k in range(KD):
            hi, lo = (at(t, k * 1024, (HALF, G), (1, ROPE0)) for t in key)
            jobs.append((a["a0_rope"][:, k * 256:(k + 1) * 256], hi, lo))
        split_weights(nc, "a0", jobs, [(a["a0_down"], [P, KD, D]), (a["a0_upk"], [P, KD, 256]),
                                       (a["a0_upv"], [P, KD, 512])], listed)
        t = attention_constants(nc, m, a, "a0", {"qcos": [P, TT, 32], "qsin": [P, TT, 64],
                                                 "kcos": [P, TT, 32], "ksin": [P, TT, 64]})
        w = dict(t, latent=False, rslots=1, scale=1.0 / 8.0, query=query, key=key, out=a["a0_out"],
                 query_tables=(t["qcos"], t["qsin"]), key_tables=(t["kcos"], t["ksin"]))
        attention(nc, "a0", x, const, w, a)


def attention1(nc, a, x, const):
    with ExitStack() as ctx:
        m = Names(nc, ctx, "a1")
        query = [m.sb(f"wquery{s}", [P, KD, NH1 * P], F32R) for s in "hl"]
        key = [m.sb(f"wkey{s}", [P, KD, P], F32R) for s in "hl"]
        outw = m.sb("outw", [P, NH1 // 2, D])

        def folds(f, bank):
            qn, bk, bv, wo = f
            got = []
            for k in range(KD):
                for half in range(2):
                    mm = [(0, h * 64, 64, qn[:, half * 8 + h, k * P:(k + 1) * P], bk[:, half * 8 + h, :], True, True)
                          for h in range(8)]
                    hi, lo = (at(t, k * NH1 * P + half * 8 * P + 64, (P, 8), (1, 64)) for t in query)
                    got.append((mm, at(bank[len(got) % 2], 0, (64, 8), (1, 64)), hi, lo))
            for hp in range(NH1 // 2):
                mm = [(64 * o, 0, D, bv[:, 2 * hp + o, :], wo[:, 2 * hp + o, :], True, True) for o in range(2)]
                got.append((mm, bank[len(got) % 2][:, 0:D], outw[:, hp, :], None))
            return got

        jobs = [(a["a1_key"], flat(key[0]), flat(key[1]))]
        for k in range(KD):
            hi, lo = (at(t, k * NH1 * P, (P, NH1), (1, 64)) for t in query)
            jobs.append((a["a1_rope"][:, k * 1024:(k + 1) * 1024], hi, lo))
        split_weights(nc, "a1", jobs, [(a["a1_nope"], [P, NH1, D]), (a["a1_bk"], [P, NH1, 64]),
                                       (a["a1_bv"], [P, NH1, 64]), (a["a1_wo"], [P, NH1, D])], folds)
        t = attention_constants(nc, m, a, "a1", {"qcos": [P, TT, 32], "qsin": [P, TT, 64], "norm_w": [P, 64]})
        w = dict(t, latent=True, rslots=2, scale=float(1.0 / np.sqrt(ROT1 + NOPE1)), query=query, key=key, out=outw,
                 query_tables=(t["qcos"], t["qsin"]), key_tables=(t["qcos"], t["qsin"]))
        attention(nc, "a1", x, const, w, a)



def build_program(nc, a, out, stages=("a0", "f0", "a1", "f1")):
    with ExitStack() as ctx:
        m = Names(nc, ctx, "all")
        x = m.sb("x", [P, NSEQ * TT, D])
        const = {
            "ident": m.sb("ident", [P, P]),
            "minus_half": m.sb("minus_half", [P, 8]),
        }
        with ExitStack() as c0:
            loaded, made = c0.enter_context(nc.semaphore("const_loaded")), c0.enter_context(nc.semaphore("const_made"))
            block = c0.enter_context(nc.Block())

            @block.sync
            def _(sp):
                sp.dma_start(x[:], a["x"]).then_inc(loaded, 16)
                sp.dma_start(const["ident"][:], a["ident"]).then_inc(loaded, 16)
                sp.wait_ge(loaded, 32)

            @block.vector
            def _(dve):
                nc.vector.memset(const["minus_half"][:], -0.5).then_inc(made, 1)
                dve.wait_ge(made, 1)

        if "a0" in stages:
            attention0(nc, a, x, const)
        if "f0" in stages:
            experts(nc, a, x, const, out if stages[-1] == "f0" else None)
        if "a1" in stages:
            attention1(nc, a, x, const)
        if "f1" in stages:
            swiglu(nc, a, x, const, out)
        if stages[-1] not in ("f0", "f1"):
            with ExitStack() as c0:
                s = c0.enter_context(nc.semaphore("dbg"))
                block = c0.enter_context(nc.Block())

                @block.sync
                def _(sp):
                    sp.dma_start(out, x[:]).then_inc(s, 16)
                    sp.wait_ge(s, 16)


def flat(t, p=P):
    v = t[:] if not isinstance(t, bass.AP) else t
    names = " ".join(f"d{i}" for i in range(v.ndim - 1))
    return v.rearrange(f"p {names} -> p ({names})")[0:p, :] if v.ndim > 2 else v[0:p, :]


def swiglu(nc, a, x, const, out):
    with ExitStack() as ctx:
        m = Names(nc, ctx, "f1")
        two = {n: [m.sb(f"{n}{s}", shape, F32R) for s in ("h", "l")]
               for n, shape in (("gate", [P, KD, INTER]), ("up", [P, KD, INTER]), ("down", [P, INTER // P, D]))}
        split_weights(nc, "f1", [(a[f"f1_{n}"], flat(two[n][0]), flat(two[n][1])) for n in two])
        feed_forward(nc, "f1", x, const, INTER, two["gate"], two["up"], two["down"], out=out)


def experts(nc, a, x, const, out=None):
    NT = -(-MOE_H // P)
    with ExitStack() as ctx:
        m = Names(nc, ctx, "f0")
        two = {n: [m.sb(f"{n}{s}", shape, F32R) for s in ("h", "l")]
               for n, shape in (("gate", [P, KD, MOE_H]), ("up", [P, KD, MOE_H]), ("down", [P, NT, D]),
                                ("router", [P, KD, NE]))}
        spread = m.sb("spread", [P, MOE_H], F32R)
        const = dict(const, before=m.sb("before", [P, NE, NE]))
        split_weights(nc, "f0", [(a[f"f0_{n}"], flat(two[n][0]), flat(two[n][1])) for n in two]
                      + [(a["f0_spread"], spread[:], None)])
        with ExitStack() as c0:
            s = c0.enter_context(nc.semaphore("f0_before"))
            block = c0.enter_context(nc.Block())

            @block.sync
            def _(sp):
                sp.dma_start(flat(const["before"]), a["f0_before"]).then_inc(s, 16)
                sp.wait_ge(s, 16)
        feed_forward(nc, "f0", x, const, MOE_H, two["gate"], two["up"], two["down"],
                     moe=(two["router"], spread), out=out)



def _layouts(inputs):
    f = {k: np.asarray(v) for k, v in inputs.items()}
    tiles = lambda w: np.ascontiguousarray(w.reshape(-1, P, w.shape[-1]).transpose(1, 0, 2).reshape(P, -1))

    def padded(w):
        rows = -(-w.shape[0] // P) * P
        out = np.zeros((rows, w.shape[1]), w.dtype)
        out[:w.shape[0]] = w
        return out

    g = {}
    g["x"] = np.ascontiguousarray(f["L0_attn_hidden_states"].reshape(NSEQ * TT, P, D).transpose(1, 0, 2))
    g["ident"] = np.eye(P, dtype=np.float32)
    w = f["L1_ffn_w_gate_up"].T
    g["f1_gate"], g["f1_up"] = tiles(w[:, :INTER]), tiles(w[:, INTER:])
    g["f1_down"] = tiles(f["L1_ffn_w_down"].T)
    beside = lambda e: e.transpose(1, 0, 2).reshape(D, NE * DE)
    g["f0_gate"] = tiles(np.concatenate([beside(f["L0_ffn_We_gate"]), f["L0_ffn_Ws_gate"]], 1))
    g["f0_up"] = tiles(np.concatenate([beside(f["L0_ffn_We_up"]), f["L0_ffn_Ws_up"]], 1))
    g["f0_down"] = tiles(padded(np.concatenate([f["L0_ffn_We_down"].reshape(NE * DE, D), f["L0_ffn_Ws_down"]], 0)))
    g["f0_router"] = tiles(f["L0_ffn_W_router"])
    owner = np.minimum(np.arange(MOE_H) // DE, NE)
    spread = np.zeros((P, MOE_H), np.float32)
    for base in (0, 32):
        spread[base + owner, np.arange(MOE_H)] = 1.0
    g["f0_spread"] = spread
    g["f0_before"] = np.tile((np.arange(NE)[None, :] < np.arange(NE)[:, None]).astype(np.float32).reshape(1, -1), (P, 1))
    i = np.arange(P)
    g["mask_q"] = np.where(i[None, :] > i[:, None], MASKED, 0.0).astype(np.float32)
    g["mask_k"] = np.ascontiguousarray(g["mask_q"].T)
    g["a0_query"] = tiles(f["L0_attn_q_w"].T)
    g["a0_rope"] = tiles(f["L0_attn_kr_w"].T)
    g["a0_down"] = tiles(f["L0_attn_down_w"])
    g["a0_upk"] = tiles(f["L0_attn_upk_w"].T)
    g["a0_upv"] = tiles(f["L0_attn_upv_w"].T)
    g["a0_out"] = np.ascontiguousarray(
        f["L0_attn_o_w"].T.reshape(NH0 // HPAIR, HG, P, D).transpose(0, 2, 1, 3).reshape(NH0 // HPAIR, P, HG * D))
    pos = np.arange(SEQ, dtype=np.float32)

    def table(freq):
        angle = (pos[:, None] * freq[None, :]).astype(np.float32).astype(np.float64)
        c = np.cos(angle)
        s = np.concatenate([-np.sin(angle), np.sin(angle)], 1)
        return c.astype(np.float32), s.astype(np.float32)

    inv = (np.float32(1.0) / np.float32(10000.0) ** (np.arange(0, 64, 2, dtype=np.float32) / np.float32(64))).astype(np.float32)
    cos, sin = table(inv)
    for tag in ("a0", "a1"):
        g[f"{tag}_qcos"], g[f"{tag}_qsin"] = tiles(cos), tiles(sin)
    rotated = np.tile(np.arange(HD0 // 2) < ROPE0, 2)
    g["a0_kcos"] = tiles(np.where(rotated[:32], cos, np.float32(1.0)))
    g["a0_ksin"] = tiles(np.where(rotated, sin, np.float32(0.0)))
    apart = np.concatenate([np.arange(0, ROT1, 2), np.arange(1, ROT1, 2)])
    wq = f["L1_attn_Wq"].reshape(D, NH1, NOPE1 + ROT1)
    g["a1_rope"] = tiles(np.ascontiguousarray(wq[:, :, NOPE1 + apart]).reshape(D, NH1 * ROT1))
    g["a1_nope"] = np.ascontiguousarray(wq[:, :, :NOPE1].transpose(2, 1, 0)).reshape(NOPE1, NH1 * D)
    wb = f["L1_attn_Wkv_b"].reshape(LAT1, NH1, NOPE1 + VD1)
    g["a1_bk"] = np.ascontiguousarray(wb[:, :, :NOPE1].transpose(2, 1, 0)).reshape(NOPE1, NH1 * LAT1)
    g["a1_bv"] = np.ascontiguousarray(wb[:, :, NOPE1:].transpose(2, 1, 0)).reshape(VD1, NH1 * LAT1)
    g["a1_wo"] = np.ascontiguousarray(f["L1_attn_Wo"].reshape(NH1, VD1, D).transpose(1, 0, 2)).reshape(VD1, NH1 * D)
    wa = f["L1_attn_Wkv_a"]
    g["a1_key"] = tiles(np.concatenate([wa[:, LAT1 + apart], wa[:, :LAT1]], 1))
    g["a1_norm_w"] = np.tile(f["L1_attn_kv_norm_w"][None, :], (P, 1))
    return g


def kernel(**inputs):
    import numpy as _np
    import concourse.bacc as _bacc
    from concourse import mybir as _mybir
    from concourse.bass_utils import run_bass_kernel_spmd as _run

    g = _layouts(inputs)
    nc = _bacc.Bacc("TRN2", target_bir_lowering=False, num_devices=1)
    a = {k: nc.dram_tensor(f"in_{k}", v.shape, _mybir.dt.from_np(v.dtype), kind="ExternalInput").ap()
         for k, v in g.items()}
    out = nc.dram_tensor("out_x", [P, NSEQ * TT, D], _mybir.dt.float32, kind="ExternalOutput").ap()
    build_program(nc, a, out)
    r = _run(nc, [{f"in_{k}": v for k, v in g.items()}], core_ids=[0])
    y = r.results[0]["out_x"]
    return _np.ascontiguousarray(y.reshape(P, NSEQ * TT, D).transpose(1, 0, 2)).reshape(NSEQ, SEQ, D)
```

```python
from contextlib import ExitStack

import numpy as np

import concourse.bass as bass
from concourse import mybir

F32 = mybir.dt.float32
F32R = mybir.dt.float32r
BF16 = mybir.dt.bfloat16
ALU = mybir.AluOpType
ACT = mybir.ActivationFunctionType
AX = mybir.AxisListType

P = 128
D = 256
KD = D // P
NSEQ, SEQ = 4, 512
TT = SEQ // P
LN_EPS = 1e-5
RMS_EPS = 1.1920928955078125e-07
MASKED = -1e30

NH0, NKV0, HD0 = 32, 8, 64
ROPE0 = 16
NE, DE, DS = 8, 176, 352
MOE_H = NE * DE + DS
NH1, NOPE1, ROT1, LAT1, VD1 = 16, 128, 64, 64, 128
INTER = 1024

HG = 4
HPAIR = 2 * HG


def at(t, offset, *dims):
    base = t[:] if not isinstance(t, bass.AP) else t
    return bass.AP(tensor=base.tensor, offset=base.offset + offset,
                   ap=[list(base.ap[0])] + [list(d) for d in dims])


class Names:

    def __init__(self, nc, ctx, tag):
        self.nc, self.ctx, self.tag = nc, ctx, tag

    def sb(self, name, shape, dt=F32):
        return self.ctx.enter_context(self.nc.sbuf_tensor(f"{self.tag}_{name}", shape, dt))

    def ps(self, name, shape, dt=F32):
        return self.ctx.enter_context(self.nc.psum_tensor(f"{self.tag}_{name}", shape, dt))

    def sem(self, name):
        return self.ctx.enter_context(self.nc.semaphore(f"{self.tag}_{name}"))





class Norm:

    def __init__(self, m, const, which):
        self.stats = m.sb(f"{which}_stats", [P, TT, 6])
        self.mv = m.sb(f"{which}_mv", [P, TT, 2])
        self.var = m.sb(f"{which}_var", [P, TT])
        self.rstd = m.sb(f"{which}_rstd", [P, TT])
        self.pause = m.sb(f"{which}_pause", [P, 1])
        self.minus_half = const["minus_half"]
        self.linked = m.sem(f"{which}_ln_linked")
        self.var_ready = m.sem(f"{which}_ln_var_ready")
        self.rstd_ready = m.sem(f"{which}_ln_rstd_ready")

    def statistics(self, nc, dve, tiles, count):
        for j, tile in enumerate(tiles):
            ins = nc.vector.bn_stats(self.stats[:, j, :], tile)
        ins.then_inc(self.linked, 1)
        dve.wait_ge(self.linked, count * 2 + 1)
        nc.vector.memset(self.pause[:], 0.0)
        for j in range(len(tiles)):
            ins = nc.vector.bn_aggr(self.mv[:, j, :], self.stats[:, j, :])
        ins.then_inc(self.linked, 1)
        dve.wait_ge(self.linked, count * 2 + 2)
        nc.vector.tensor_scalar(self.var[:], self.mv[:, :, 1], LN_EPS, None, ALU.add).then_inc(self.var_ready, 1)

    def power(self, nc, pool, count):
        pool.wait_ge(self.var_ready, count + 1)
        nc.gpsimd.tensor_tensor(self.rstd[:], self.var[:], self.minus_half[:, 0:TT],
                                ALU.pow).then_inc(self.rstd_ready, 1)

    def apply(self, nc, out, tile, j):
        return nc.vector.tensor_scalar(out, tile, self.mv[:, j, 0:1], self.rstd[:, j:j + 1],
                                       ALU.subtract, ALU.mult)



def split_weights(nc, tag, jobs, sources=(), products=None):
    CHUNK = 2048
    pieces = []
    for src, hi, lo in jobs:
        if hi.ndim == 3:
            pieces.append((src, hi, lo))
            continue
        for c in range(0, src.shape[1], CHUNK):
            e = min(c + CHUNK, src.shape[1])
            pieces.append((src[:, c:e], hi[:, c:e], lo[:, c:e] if lo is not None else None))
    with ExitStack() as ctx:
        w = Names(nc, ctx, f"{tag}_w")
        NB = 3
        stage = w.sb("stage", [P, NB, CHUNK])
        junk = w.sb("junk", [P, 32])
        loaded = [w.sem(f"piece_loaded{i}") for i in range(NB)]
        hi_done = w.sem("hi_done")
        lo_done = w.sem("lo_done")
        if sources:
            src_loaded = w.sem("src_loaded")
            fold_ready = w.sem("fold_ready")
            fold_hi = w.sem("fold_hi")
            fold_free = w.sem("fold_free")
        bank = [w.ps(f"fold{i}", [P, 512]) for i in range(2)]
        factors = [w.sb(f"factor{k}", shape) for k, (_, shape) in enumerate(sources)]
        folds = products(factors, bank) if products else []
        block = ctx.enter_context(nc.Block())

        def slot(i):
            src, hi, _ = pieces[i]
            v = stage[:, i % NB, 0:src.shape[1]]
            return v.rearrange("p (a b) -> p a b", a=hi.shape[1]) if hi.ndim == 3 else v

        @block.sync
        def _(sp):
            for t, (src, _) in zip(factors, sources):
                sp.dma_start(flat(t), src).then_inc(src_loaded, 16)
            for i, (src, _, _) in enumerate(pieces):
                if i >= NB:
                    sp.wait_ge(lo_done, i - NB + 1)
                sp.dma_start(stage[:, i % NB, 0:src.shape[1]], src).then_inc(loaded[i % NB], 16)

        @block.scalar
        def _(act):
            for i, (_, hi, _) in enumerate(pieces):
                act.wait_ge(loaded[i % NB], 16 * (i // NB + 1))
                nc.scalar.activation(hi, slot(i), ACT.Copy).then_inc(hi_done, 1)
            for i, (_, view, hi, _) in enumerate(folds):
                act.wait_ge(fold_ready, i + 1)
                nc.scalar.activation(hi, view, ACT.Copy).then_inc(fold_hi, 1)

        @block.vector
        def _(dve):
            for i, (_, hi, lo) in enumerate(pieces):
                dve.wait_ge(hi_done, i + 1)
                ins = (nc.vector.memset(junk[:, i:i + 1], 0.0) if lo is None else
                       nc.vector.tensor_tensor(lo, slot(i), hi.bitcast(F32), ALU.subtract))
                ins.then_inc(lo_done, 1)
            for i, (_, view, hi, lo) in enumerate(folds):
                dve.wait_ge(fold_hi, i + 1)
                ins = (nc.vector.memset(junk[:, i:i + 1], 0.0) if lo is None else
                       nc.vector.tensor_tensor(lo, view, hi.bitcast(F32), ALU.subtract))
                ins.then_inc(fold_free, 1)

        @block.tensor
        def _(pe):
            if folds:
                pe.wait_ge(src_loaded, 16 * len(factors))
            for i, (matmuls, _, _, _) in enumerate(folds):
                if i >= 2:
                    pe.wait_ge(fold_free, i - 1)
                for part, col, n, stat, mov, start, stop in matmuls:
                    ins = nc.tensor.matmul(bank[i % 2][part:part + stat.shape[1], col:col + n], stat, mov,
                                           start=start, stop=stop)
                ins.then_inc(fold_ready, 1)


def last_item(steps, s, kind, *args):
    found = [i for k, a, i in steps[:s] if k == kind and a[:len(args)] == args]
    return found[-1] if found else -1



AHEAD = 5


def feed_forward_steps(nt, moe):
    counts = {}

    def build(tiles, begin_at, end_at, first=False):
        steps, items = [], 0

        def add(kind, *args, ring=False):
            nonlocal items
            steps.append((kind, args, items if ring else None))
            items += ring

        def begin(stage):
            if stage == 0:
                add("center")
            if stage == 1:
                add("norm")
                for k in range(KD):
                    add("xT", k, ring=True)
            if stage == 2 and moe:
                add("routerT", ring=True)
                add("logits", ring=True)
            if stage == 3 and moe:
                add("share")
            if stage == 4 and moe:
                add("rank")
                add("combine", ring=True)

        def down(t):
            add("down", t)
            if t == nt - 1:
                add("leave")

        if tiles[0] == 0:
            begin(0)
            add("weights", 0)
            begin(1)
            add("weights", 1)
            if moe:
                add("router")
            for stage in (2, 3, 4):
                begin(stage)
        for t in tiles:
            if begin_at is not None:
                begin(t - begin_at)
                if moe and t == begin_at + 6:
                    add("even", ring=True)
            if t >= 2:
                add("low", t - 2)
            add("project", t)
            if first and t + 2 < nt:
                add("weights", t + 2)
            if t == end_at:
                for c in range(2):
                    add("yT", c, ring=True)
            if moe:
                add("spread", t, ring=True)
            add("product", t)
            if t >= 1:
                add("high", t - 1)
            if t >= 2:
                down(t - 2)
            if t == end_at + 1:
                add("y_center")
            if t == end_at + 2:
                add("residual")
        if tiles[-1] == nt - 1:
            add("low", nt - 2)
            add("high", nt - 1)
            down(nt - 2)
            add("low", nt - 1)
            down(nt - 1)
            for c in range(2):
                add("yT", c, ring=True)
            add("y_center")
            add("residual")
        counts[len(counts)] = items
        return steps

    prologue = build(range(AHEAD), None, nt + 2, first=True)
    opening = build(range(AHEAD, nt + AHEAD), AHEAD, nt + 2, first=True)
    body = build(range(AHEAD, nt + AHEAD), AHEAD, nt + 2)
    final = build(range(AHEAD, nt), None, nt + 2)
    if counts[0] % 2:
        raise ValueError("the prologue needs an even number of items")
    assert counts[1] == counts[2] and counts[1] % 2 == 0
    return prologue, opening, body, final, counts[0], counts[1]


def feed_forward(nc, tag, x, const, weights, hidden, moe=None, out=None):
    NT = -(-hidden // P)
    TW = 2 * D + D
    NSTAGE = 3
    prologue, opening, body, final, BEFORE, NMISC = feed_forward_steps(NT, moe is not None)
    with ExitStack() as ctx:
        m = Names(nc, ctx, tag)
        norm = Norm(m, const, "in")
        norm_y = Norm(m, const, "out")
        ident = const["ident"]
        xn = m.sb("xn", [P, TT, D])
        y = m.sb("y", [P, TT, D])
        xTh = m.sb("xTh", [P, 2, KD, SEQ], F32R)
        xTl = m.sb("xTl", [P, 2, KD, SEQ], F32R)
        sg = m.sb("sg", [P, 2, SEQ])
        hf = m.sb("hf", [P, 2, SEQ])
        hg = m.sb("hg", [P, 2, SEQ]) if moe else hf
        hh = m.sb("hh", [P, 2, SEQ], F32R)
        hl = m.sb("hl", [P, 2, SEQ], F32R)
        yT = m.sb("yT", [P, KD, SEQ])
        wh = m.sb("wh", [P, NT, TW], F32R)
        wl = m.sb("wl", [P, NT, TW], F32R)
        stage = m.sb("stage", [P, NSTAGE, TW])
        pause = m.sb("pause", [P, 1])
        misc = [m.ps(f"misc{i}", [P, 512]) for i in range(2)]
        gb = [m.ps(f"gate{i}", [P, 512]) for i in range(2)]
        ub = [m.ps(f"up{i}", [P, 512]) for i in range(2)]
        yb = [m.ps(f"y{i}", [P, 512]) for i in range(KD)]

        xn_ready = m.sem("xn_ready")
        misc_ready = m.sem("misc_ready")
        misc_free = m.sem("misc_free")
        xh_ready = m.sem("xh_ready")
        g_ready = m.sem("g_ready")
        u_ready = m.sem("u_ready")
        s_done = m.sem("s_done")
        hf_done = m.sem("hf_done")
        hh_done = m.sem("hh_done")
        hl_done = m.sem("hl_done")
        dn_done = m.sem("dn_done")
        y_left = m.sem("y_left")
        y_normed = m.sem("y_normed")
        x_done = m.sem("x_done")
        if out is not None:
            stored = m.sem("stored")
        w_loaded = [m.sem(f"w_loaded{i}") for i in range(NSTAGE)]
        wh_done = m.sem("wh_done")
        wl_done = m.sem("wl_done")
        if moe:
            router_raw = m.sb("router_raw", [P, KD, NE])
            spread_raw = m.sb("spread_raw", [P, NT * P])
            before = m.sb("before", [P, NE, NE])
            router = [m.sb(f"router{s}", [P, KD, NE], F32R) for s in "hl"]
            spread = m.sb("spread", [P, NT * P], F32R)
            lt = m.sb("lt", [P, SEQ])
            ce = m.sb("ce", [P, TT, NE])
            mx = m.sb("mx", [P, TT])
            su = m.sb("su", [P, TT])
            rs = m.sb("rs", [P, TT])
            gtm = m.sb("gtm", [P, TT, NE, NE])
            eqm = m.sb("eqm", [P, TT, NE, NE])
            cnt = m.sb("cnt", [P, TT, NE])
            cmb = m.sb("cmb", [P, TT, 16])
            cT = m.sb("cT", [P, 2, SEQ], F32R)
            r_loaded = m.sem("r_loaded")
            rh_done = m.sem("rh_done")
            rl_done = m.sem("rl_done")
            set_up = m.sem("set_up")
            exp_done = m.sem("exp_done")
            rt_link = m.sem("rt_link")
            cmb_ready = m.sem("cmb_ready")
            cT_ready = m.sem("cT_ready")
        SHARE_LINKS, RANK_LINKS = 4, 4
        RT_LINKS = SHARE_LINKS + RANK_LINKS
        block = ctx.enter_context(nc.Block())

        def of(t, n):
            return t[:, n % 2:n % 2 + 1] if isinstance(n, int) else t[:, bass.ds(n % 2, 1)]

        def tile_of(t, n, k):
            return of(t, n)[:, :, k, :].rearrange("p a n -> p (a n)")

        def weights_of(n, rows):
            return of(cT, n)[rows].rearrange("p a n -> p (a n)")

        def everything(engine, section):
            section(prologue, 0, 0, 0)
            section(opening, 0, BEFORE, 1)
            with engine.Fori(1, NSEQ - 1) as b:
                section(body, b, b * NMISC + BEFORE, b + 1)
            section(final, NSEQ - 1, (NSEQ - 1) * NMISC + BEFORE, NSEQ)

        @block.gpsimd
        def _(pool):
            def section(steps, b, item, n):
                for kind, _, _ in steps:
                    if kind == "center":
                        norm.power(nc, pool, n)
                    if kind == "y_center":
                        norm_y.power(nc, pool, b)

            everything(pool, section)

        @block.scalar
        def _(act):
            act.sem_inc(s_done, 2)

            def section(steps, b, item, n):
                for s, (kind, args, i) in enumerate(steps):
                    if kind == "weights":
                        t, = args
                        act.wait_ge(w_loaded[t % NSTAGE], (t // NSTAGE + 1) * 16)
                        nc.scalar.activation(wh[:, t, :], stage[:, t % NSTAGE, :], ACT.Copy).then_inc(wh_done, 1)
                    if kind == "router":
                        act.wait_ge(r_loaded, 48)
                        nc.scalar.activation(router[0][:], router_raw[:], ACT.Copy).then_inc(rh_done, 1)
                        nc.scalar.activation(spread[:], spread_raw[:], ACT.Copy).then_inc(rh_done, 1)
                    if kind == "xT":
                        act.wait_ge(misc_ready, item + i + 1)
                        nc.scalar.activation(tile_of(xTh, n, args[0]), misc[i % 2][:], ACT.Copy).then_inc(xh_ready, 1)
                    if kind == "share":
                        act.wait_ge(misc_free, item + last_item(steps, s, "logits") + 3)
                        nc.scalar.activation(ce[:], ce[:], ACT.Exp).then_inc(exp_done, 1)
                    if kind == "project":
                        t, = args
                        act.wait_ge(g_ready, b * NT + t + 1)
                        act.wait_ge(hf_done, b * NT + t + 1)
                        nc.scalar.activation(sg[:, t % 2, :], gb[t % 2][:], ACT.Silu).then_inc(s_done, 1)
                    if kind == "high":
                        t, = args
                        if moe:
                            act.wait_ge(misc_free, item + last_item(steps, s, "spread", t) + 3)
                        else:
                            act.wait_ge(hf_done, b * NT + t + 3)
                        act.wait_ge(dn_done, b * NT + t + 1)
                        nc.scalar.activation(hh[:, t % 2, :], hg[:, t % 2, :], ACT.Copy).then_inc(hh_done, 1)

            everything(act, section)

        @block.vector
        def _(dve):
            dve.sem_inc(misc_free, 2)
            dve.sem_inc(hf_done, 2)
            dve.sem_inc(y_left, 2)
            if moe:
                nc.vector.memset(cT[:].bitcast(F32), 0.0).then_inc(set_up, 1)
                nc.vector.memset(lt[:], 0.0).then_inc(set_up, 1)
                nc.vector.memset(cmb[:], 0.0).then_inc(set_up, 1)
                dve.wait_ge(set_up, 3)
                nc.vector.memset(cmb[:, :, NE:NE + 1], 1.0).then_inc(set_up, 1)
                dve.wait_ge(set_up, 4)

            def x_of(n):
                if isinstance(n, int):
                    return [x[:, n * TT + j, :] for j in range(TT)]
                return [x[:, bass.ds(n * TT + j, 1), :].rearrange("p a d -> p (a d)") for j in range(TT)]

            def section(steps, b, item, n):
                link_count = 0

                def link(ins):
                    nonlocal link_count
                    link_count += 1
                    ins.then_inc(rt_link, 1)
                    dve.wait_ge(rt_link, n * RT_LINKS + link_count)

                for s, (kind, args, i) in enumerate(steps):
                    if i is not None and kind != "xT":
                        dve.wait_ge(misc_ready, item + i + 1)
                    if kind == "weights":
                        t, = args
                        dve.wait_ge(wh_done, t + 1)
                        nc.vector.tensor_tensor(wl[:, t, :], stage[:, t % NSTAGE, :], wh[:, t, :].bitcast(F32),
                                                ALU.subtract).then_inc(wl_done, 1)
                    if kind == "router":
                        dve.wait_ge(rh_done, 1)
                        nc.vector.tensor_tensor(router[1][:], router_raw[:], router[0][:].bitcast(F32),
                                                ALU.subtract).then_inc(rl_done, 1)
                    if kind == "center":
                        norm.statistics(nc, dve, x_of(n), n)
                    if kind == "norm":
                        dve.wait_ge(norm.rstd_ready, n + 1)
                        for j, tile in enumerate(x_of(n)):
                            ins = norm.apply(nc, xn[:, j, :], tile, j)
                        ins.then_inc(xn_ready, 1)
                    if kind == "xT":
                        k, = args
                        dve.wait_ge(xh_ready, n * KD + k + 1)
                        nc.vector.tensor_tensor(tile_of(xTl, n, k), misc[i % 2][:],
                                                tile_of(xTh, n, k).bitcast(F32), ALU.subtract).then_inc(misc_free, 1)
                    if kind == "routerT":
                        nc.vector.tensor_copy(lt[0:NE, :], misc[i % 2][0:NE, :]).then_inc(misc_free, 1)
                    if kind == "logits":
                        logits = at(misc[i % 2], 0, (P, TT), (1, NE))
                        link(nc.vector.tensor_reduce(mx[:], logits, AX.X, ALU.max))
                        nc.vector.tensor_tensor(ce[:], logits, at(mx, 0, (1, TT), (0, NE)),
                                                ALU.subtract).then_inc(misc_free, 1)
                    if kind == "share":
                        dve.wait_ge(exp_done, n + 1)
                        link(nc.vector.tensor_reduce(su[:], ce[:], AX.X, ALU.add))
                        link(nc.vector.reciprocal(rs[:], su[:]))
                        link(nc.vector.tensor_tensor(ce[:], ce[:], at(rs, 0, (1, TT), (0, NE)), ALU.mult))
                        assert link_count == SHARE_LINKS
                    if kind == "rank":
                        mine = at(ce, 0, (NE, TT), (1, NE), (0, NE))
                        other = at(ce, 0, (NE, TT), (0, NE), (1, NE))
                        nc.vector.tensor_tensor(gtm[:], other, mine, ALU.is_gt)
                        link(nc.vector.tensor_tensor(eqm[:], other, mine, ALU.is_equal))
                        link(nc.vector.tensor_tensor(eqm[:], eqm[:], at(before, 0, (0, TT), (NE, NE), (1, NE)),
                                                     ALU.mult))
                        link(nc.vector.tensor_tensor(gtm[:], gtm[:], eqm[:], ALU.add))
                        link(nc.vector.tensor_reduce(cnt[:], gtm[:], AX.X, ALU.add))
                        nc.vector.scalar_tensor_tensor(out=cmb[:, :, 0:NE], in0=cnt[:], scalar=1.5, in1=ce[:],
                                                       op0=ALU.is_lt, op1=ALU.mult).then_inc(cmb_ready, 1)
                        assert link_count == RT_LINKS
                    if kind == "combine":
                        bank = misc[i % 2]
                        nc.vector.tensor_copy(weights_of(n, slice(0, 16)), bank[0:16, :]).then_inc(cT_ready, 1)
                        dve.wait_ge(cT_ready, n + 1)
                        nc.vector.tensor_tensor(weights_of(n, slice(32, 48)), bank[0:16, :],
                                                weights_of(n, slice(0, 16)).bitcast(F32),
                                                ALU.subtract).then_inc(misc_free, 1)
                    if kind == "even":
                        nc.vector.memset(pause[:], 0.0).then_inc(misc_free, 1)
                    if kind == "low":
                        t, = args
                        dve.wait_ge(hh_done, b * NT + t + 1)
                        nc.vector.tensor_tensor(hl[:, t % 2, :], hg[:, t % 2, :], hh[:, t % 2, :].bitcast(F32),
                                                ALU.subtract).then_inc(hl_done, 1)
                    if kind == "product":
                        t, = args
                        dve.wait_ge(s_done, b * NT + t + 3)
                        dve.wait_ge(u_ready, b * NT + t + 1)
                        if not isinstance(b, int) or t >= 2:
                            dve.wait_ge(hl_done, b * NT + t - 1)
                        nc.vector.tensor_tensor(hf[:, t % 2, :], sg[:, t % 2, :], ub[t % 2][:],
                                                ALU.mult).then_inc(hf_done, 1)
                        if moe:
                            c = last_item(steps, s, "spread", t)
                            dve.wait_ge(misc_ready, item + c + 1)
                            dve.wait_ge(hf_done, b * NT + t + 3)
                            nc.vector.tensor_tensor(hg[:, t % 2, :], hf[:, t % 2, :], misc[c % 2][:],
                                                    ALU.mult).then_inc(misc_free, 1)
                    if kind == "leave":
                        dve.wait_ge(dn_done, b * NT + NT + 2)
                        for k in range(KD):
                            nc.vector.tensor_copy(yT[:, k, :], yb[k][:]).then_inc(y_left, 1)
                    if kind == "yT":
                        c, = args
                        nc.vector.tensor_copy(y[:, 2 * c:2 * c + 2, :].rearrange("p a d -> p (a d)"),
                                              misc[i % 2][:]).then_inc(misc_free, 1)
                    if kind == "y_center":
                        dve.wait_ge(misc_free, item + last_item(steps, s, "yT") + 3)
                        norm_y.statistics(nc, dve, [y[:, j, :] for j in range(TT)], b)
                    if kind == "residual":
                        dve.wait_ge(norm_y.rstd_ready, b + 1)
                        for j in range(TT):
                            ins = norm_y.apply(nc, y[:, j, :], y[:, j, :], j)
                        ins.then_inc(y_normed, 1)
                        dve.wait_ge(y_normed, b + 1)
                        for j, tile in enumerate(x_of(b)):
                            ins = nc.vector.tensor_tensor(tile, tile, y[:, j, :], ALU.add)
                        ins.then_inc(x_done, 1)

            everything(dve, section)

        @block.tensor
        def _(pe):
            pe.sem_inc(dn_done, 2)

            def columns(w, t, c):
                return w[:, t % NT, c * P:(c + 1) * P]

            def project(bank, first, t, n):
                terms = [(columns(w, t, first + k), tile_of(xs, n, k)) for k in range(KD)
                         for w, xs in ((wh, xTh), (wh, xTl), (wl, xTh))]
                for s, (st, mv) in enumerate(terms):
                    ins = nc.tensor.matmul(bank[:], st, mv, start=(s == 0), stop=(s == len(terms) - 1))
                return ins

            def section(steps, b, item, n):
                for s, (kind, args, i) in enumerate(steps):
                    if i is not None:
                        pe.wait_ge(misc_free, item + i + 1)
                        bank = misc[i % 2]
                    if kind == "xT":
                        k, = args
                        pe.wait_ge(xn_ready, n + 1)
                        for j in range(TT):
                            ins = nc.tensor.transpose(bank[:, j * P:(j + 1) * P], xn[:, j, k * P:(k + 1) * P], ident[:])
                        ins.then_inc(misc_ready, 1)
                    if kind == "weights":
                        pe.wait_ge(wl_done, args[0] + 1)
                    if kind == "router":
                        pe.wait_ge(rl_done, 1)
                        pe.wait_ge(rh_done, 2)
                    if kind == "routerT":
                        pe.wait_ge(misc_free, item + last_item(steps, s, "xT") + 3)
                        terms = [(r[:, k, :], tile_of(xs, n, k)) for k in range(KD)
                                 for r, xs in ((router[0], xTh), (router[0], xTl), (router[1], xTh))]
                        for c, (st, mv) in enumerate(terms):
                            ins = nc.tensor.matmul(bank[0:NE, :], st, mv, start=(c == 0), stop=(c == len(terms) - 1))
                        ins.then_inc(misc_ready, 1)
                    if kind == "logits":
                        pe.wait_ge(misc_free, item + last_item(steps, s, "routerT") + 3)
                        for j in range(TT):
                            ins = nc.tensor.transpose(bank[:, j * P:(j + 1) * P], lt[:, j * P:(j + 1) * P], ident[:])
                        ins.then_inc(misc_ready, 1)
                    if kind == "combine":
                        pe.wait_ge(cmb_ready, n + 1)
                        for j in range(TT):
                            ins = nc.tensor.transpose(bank[0:16, j * P:(j + 1) * P], cmb[:, j, :], ident[:])
                        ins.then_inc(misc_ready, 1)
                    if kind == "even":
                        nc.tensor.transpose(bank[0:16, 0:P], cmb[:, 0, :], ident[:]).then_inc(misc_ready, 1)
                    if kind == "project":
                        t, = args
                        if t % NT == 0:
                            pe.wait_ge(misc_free, item + last_item(steps, s, "xT") + 3)
                        whose = n if t % NT < AHEAD else b
                        pe.wait_ge(s_done, b * NT + t + 1)
                        project(gb[t % 2], 0, t, whose).then_inc(g_ready, 1)
                        pe.wait_ge(hf_done, b * NT + t + 1)
                        project(ub[t % 2], KD, t, whose).then_inc(u_ready, 1)
                    if kind == "spread":
                        t, = args
                        whose = n if t % NT < AHEAD else b
                        if t % NT == 0:
                            pe.wait_ge(misc_free, item + last_item(steps, s, "combine") + 3)
                        nc.tensor.matmul(bank[:], spread[:, t % NT * P:(t % NT + 1) * P], weights_of(whose, slice(0, P)),
                                         start=True, stop=True).then_inc(misc_ready, 1)
                    if kind == "down":
                        t, = args
                        first, last = t % NT == 0, t % NT == NT - 1
                        pe.wait_ge(hl_done, b * NT + t + 1)
                        if first:
                            pe.wait_ge(y_left, n * KD + 2)
                        for k in range(KD):
                            for c, (wt, hs) in enumerate(((wh, hh), (wh, hl), (wl, hh))):
                                ins = nc.tensor.matmul(yb[k][:], columns(wt, t, 2 * KD + k), hs[:, t % 2, :], start=(first and c == 0),
                                                       stop=(last and c == 2))
                        ins.then_inc(dn_done, 1)
                    if kind == "yT":
                        c, = args
                        pe.wait_ge(y_left, b * KD + KD + 2)
                        for j in range(2):
                            tok = slice((2 * c + j) * P, (2 * c + j + 1) * P)
                            for k in range(KD):
                                ins = nc.tensor.transpose(bank[:, j * D + k * P:j * D + (k + 1) * P],
                                                          yT[:, k, tok], ident[:])
                        ins.then_inc(misc_ready, 1)

            everything(pe, section)

        @block.sync
        def _(sp):
            for t in range(NT):
                if moe and t == 2:
                    sp.dma_start(flat(router_raw), moe[0]).then_inc(r_loaded, 16)
                    sp.dma_start(spread_raw[:], moe[1]).then_inc(r_loaded, 16)
                    sp.dma_start(flat(before), moe[2]).then_inc(r_loaded, 16)
                if t >= NSTAGE:
                    sp.wait_ge(wl_done, t - NSTAGE + 1)
                sp.dma_start(stage[:, t % NSTAGE, :], weights[:, t * TW:(t + 1) * TW]).then_inc(
                    w_loaded[t % NSTAGE], 16)
            if out is not None:
                with sp.Fori(0, NSEQ) as b:
                    sp.wait_ge(x_done, b + 1)
                    sp.dma_start(out[:, bass.ds(b * TT, TT), :], x[:, bass.ds(b * TT, TT), :]).then_inc(stored, 16)
                sp.wait_ge(stored, 16 * NSEQ)




HIGH = ("xT", "value", "keyT", "queryT")


def attention_steps(latent, rslots):
    npair = (NH1 if latent else NH0) // HPAIR
    steps = []
    count = {"m": 0, "top": 0, "unit": 0, "evac": 0, "rope": 0, "high": 0, "wquery": 0}

    def add(kind, *args, ring=None):
        n = None
        if ring:
            n = count[ring]
            count[ring] += 1
        steps.append((kind, args, n))
        count["high"] += kind in HIGH

    def rope(kind, *args):
        n = count["m"]
        count["m"] += 1
        steps.append((kind, (*args, count["rope"]), n))
        count["rope"] += 1

    def query_weights(p):
        return [] if latent else [lambda: add("wquery", p, ring="wquery")]

    def query(p):
        return [lambda c=c: rope("query", p, c) for c in range(TT * (2 if latent else 1))]

    def queryT(p):
        return [lambda i=i: add("queryT", p, i, ring="m") for i in range(HPAIR if latent else HPAIR // 2)]

    def tops(p, q):
        n = P * (q + 1)
        per = max(1, 512 // n)
        per = {1: 4, 2: 2, 3: 1, 4: 1}[q + 1]
        return [lambda h=h: add("top", p, q, tuple(range(h, h + per)), ring="top")
                for h in range(0, HPAIR, per)]

    def topT(p, q):
        return [lambda: add("topT", p, q, ring="m")]

    def output(p):
        chain = [lambda: add("dload", p), lambda: add("recip", p)]
        for hp in range(HG + rslots - 1):
            if hp < HG:
                chain.append(lambda hp=hp: add("rload", p, hp))
            if hp >= rslots - 1:
                chain.append(lambda hp=hp: add("scale", p, hp - rslots + 1))
        return chain, [lambda k=k: add("oproj", p, k, ring="m") for k in range(KD)]

    def run(fs):
        for f in fs:
            f()

    last_keyT = 0 if latent else NKV0 // 2 - 1

    def early(place=None):
        return ([lambda: add("norm")] + query_weights(0) + [lambda k=k: add("xT", k, ring="m") for k in range(KD)] +
                [lambda j=j: rope("key", j) for j in range(TT)] +
                [lambda h=h: add("keyT", h, ring="m") for h in range(last_keyT)])

    def late():
        fs = [lambda: add("cnorm")] if latent else [lambda j=j: add("value", j, ring="m") for j in range(TT)]
        return (fs + [lambda: add("keyT", last_keyT, ring="m")] + query(0) + queryT(0) + tops(0, 0) +
                topT(0, 0) + tops(0, 1))

    run(early() + late())
    if count["m"] % 2:
        add("even", ring="m")
    assert count["top"] % 2 == 0
    prologue, before = steps, dict(count)
    units = [(p, q, g, k) for p in range(npair) for q in range(TT) for g in range(2) for k in range(q + 1)]
    UNITS = TT * (TT + 1)

    def finish(u):
        add("pv", *units[u], u)
        p, q, g, k = units[u]
        if k == q:
            add("evac", p, q, g, u, ring="evac")

    def beside(p, has_next):
        after = [[] for _ in range(UNITS)]

        def place(items, places):
            for f, n in zip(items, places, strict=True):
                after[n].append(f)

        place(topT(p, 1), [0])
        place(tops(p, 2), [0, 1, 1, 2, 2, 3, 3, 3])
        place(topT(p, 2), [4])
        place(tops(p, 3), [5, 5, 6, 6, 7, 7, 8, 8])
        place(topT(p, 3), [9])
        if p:
            chain, proj = output(p - 1)
            place(chain, [3, 5, 6, 8, 8, 10, 10, 12, 12, 14] if rslots == 1 else [3, 5, 6, 6, 8, 8, 10, 10, 12, 14])
            place(proj, [15, 16])
        if p + 1 == npair and has_next:
            place(early(), [5, 6, 7, 9, 10, 11, 12] if latent else [5, 5, 6, 7, 9, 10, 11, 12, 13, 14, 15])
        if p + 1 < npair:
            place(query_weights(p + 1), [] if latent else [1])
            place(query(p + 1), range(3, 11) if latent else [4, 6, 8, 10])
            place(queryT(p + 1), [11, 12, 12, 13, 13, 14, 14, 15] if latent else [11, 12, 13, 14])
            place(tops(p + 1, 0), [16, 16])
            place(tops(p + 1, 1), [16, 17, 17, 18])
            place(topT(p + 1, 0), [18])
        return after

    def sequence(has_next):
        nonlocal steps
        steps = []
        for k in count:
            count[k] = 0
        u = 0
        for p in range(npair):
            for share in beside(p, has_next):
                add("unit", *units[u], ring="unit")
                run(share)
                if u >= 2:
                    finish(u - 2)
                u += 1
        finish(u - 2)
        finish(u - 1)
        chain, proj = output(npair - 1)
        end = chain + proj + [lambda c=c: add("yT", c, ring="m") for c in range(2)] + [lambda: add("residual")]
        start = late() if has_next else []
        ahead = 0
        for t, f in enumerate(end):
            f()
            upto = -(-(t + 1) * len(start) // (len(end) - 3))
            run(start[ahead:upto])
            ahead = max(ahead, upto)
        if count["m"] % 2:
            add("even", ring="m")
        assert ahead >= len(start) and count["top"] % 2 == 0
        return steps

    final = sequence(False)
    body = sequence(True)
    before["norm"], count["norm"] = 1, 1
    return prologue, body, final, before, count, npair


def attention(nc, tag, x, const, w, a):
    latent = w["latent"]
    prologue, body, final, before, count, NPAIR = attention_steps(latent, w["rslots"])
    NM, NTOP, NU, NG, NR, NHIGH = (count[k] for k in ("m", "top", "unit", "evac", "rope", "high"))
    none = dict.fromkeys(before, 0)

    def numbering(b, base):
        return lambda ring, i: base[ring] + b * count[ring] + i
    scale = w["scale"]
    KW = P if latent else NKV0 * HD0
    with ExitStack() as ctx:
        m = Names(nc, ctx, tag)
        norm = Norm(m, const, "in")
        norm_y = Norm(m, const, "out")
        ident = const["ident"]
        yT = m.sb("yT", [P, KD, SEQ])
        addend = at(yT, 0, (D, TT), (1, D))
        xTh = m.sb("xTh", [P, KD, SEQ], F32R)
        xTl = m.sb("xTl", [P, KD, SEQ], F32R)
        nkey = 1 if latent else NKV0
        keyh = m.sb("keyh", [P, nkey, SEQ], F32R)
        keyl = m.sb("keyl", [P, nkey, SEQ], F32R)
        VH = 1 if latent else NKV0 // 2
        VW = P if latent else 192
        Vh = m.sb("Vh", [P, TT, VH, VW], F32R)
        Vl = m.sb("Vl", [P, TT, VH, VW], F32R)
        qa = m.sb("qa", [P, 2, HPAIR, SEQ], F32R)
        qb = m.sb("qb", [P, 2, HPAIR, SEQ], F32R) if latent else None
        QW = HPAIR * (P if latent else HD0)
        RW = max(QW, KW)
        rot = m.sb("rot", [P, TT, RW])
        xnt = at(rot, 0, (D, TT), (1, D))
        CW = 256 if latent else 512
        crossed = m.sb("crossed", [P, 2, CW])
        probs_h = m.sb("probs_h", [P, 3, 512], F32R)
        probs = m.sb("probs", [P, 2, 512])
        probs_l = m.sb("probs_l", [P, 2, 512], F32R)
        out = m.sb("out", [P, 2, HG, SEQ])
        mcol = m.sb("mcol", [P, TT, HPAIR])
        mrow = m.sb("mrow", [P, 2, HPAIR, P], F32R)
        drow = m.sb("drow", [P, 512])
        dcol = m.sb("dcol", [P, 32])
        rcol = dcol
        RSLOTS = w["rslots"]
        rtile = m.sb("rtile", [P, RSLOTS, SEQ])
        misc = [m.ps(f"misc{i}", [P, 512]) for i in range(2)]
        topb = [m.ps(f"top{i}", [P, 512]) for i in range(2)]
        score = [m.ps(f"score{i}", [P, 512]) for i in range(2)]
        pvb = [m.ps(f"pv{i}", [P, 512]) for i in range(2)]
        d_dram = nc.dram_tensor(f"{tag}_rowsums", [NPAIR, HPAIR, SEQ], F32, kind="Internal").ap()
        r_dram = nc.dram_tensor(f"{tag}_recips", [NPAIR, HPAIR, SEQ], F32, kind="Internal").ap()
        if not latent:
            wo = m.sb("wo", [P, HG, D])
            wq_raw = m.sb("wq_raw", [P, KD, QW])
            wq = [m.sb(f"wq{s}", [P, KD, QW], F32R) for s in "hl"]
            wq_loaded = m.sem("wq_loaded")
            wq_high = m.sem("wq_high")
            wq_low = m.sem("wq_low")
        else:
            craw = at(rot, 64, (RW, TT), (1, 64))
            csq = m.sb("csq", [P, TT, 64])
            css = m.sb("css", [P, TT])
            crs = m.sb("crs", [P, TT])

        pause = m.sb("pause", [P, 3])
        set_up = m.sem("set_up")
        xn_ready = m.sem("xn_ready")
        misc_ready = m.sem("misc_ready")
        misc_free = m.sem("misc_free")
        high_done = m.sem("high_done")
        parts = m.sem("parts")
        rotated = m.sem("rotated")
        top_ready = m.sem("top_ready")
        top_free = m.sem("top_free")
        score_ready = m.sem("score_ready")
        probs_ready = m.sem("probs_ready")
        lows_ready = m.sem("lows_ready")
        pv_done = m.sem("pv_done")
        pv_free = m.sem("pv_free")
        drow_done = m.sem("drow_done")
        d_stored = [m.sem(f"d_stored{i}") for i in range(4)]
        d_loaded = m.sem("d_loaded")
        recips = m.sem("recips")
        r_stored = m.sem("r_stored")
        passed = m.sem("passed")
        r_loaded = [m.sem(f"r_loaded{i}") for i in range(RSLOTS)]
        scaled = m.sem("scaled")
        wo_loaded = m.sem("wo_loaded")
        x_done = m.sem("x_done")
        if latent:
            c_link = m.sem("c_link")
            c_var = m.sem("c_var")
            c_rstd = m.sem("c_rstd")
            c_ready = m.sem("c_ready")
            c_high = m.sem("c_high")
        block = ctx.enter_context(nc.Block())

        def vals(V, h, k):
            return V[:, k, h // 2, 64 * (h % 2):64 * (h % 2) + P]

        def rotated_at(kind, args, split=False):
            if kind == "key":
                off, step, heads = args[0] * RW, 64, 1 if latent else NKV0
            elif latent:
                off, step, heads = (args[1] // 2) * RW + (args[1] % 2) * 512, P, HG
            else:
                off, step, heads = args[1] * RW, 64, HPAIR
            return at(rot, off, (step, heads), (32, 2), (1, 32)) if split else at(rot, off, (step, heads), (1, 64))

        @block.gpsimd
        def _(pool):
            pool.sem_inc(rotated, 2)
            pool.sem_inc(lows_ready, 2)

            def section(steps, b, base):
                item = numbering(b, base)
                for kind, args, i in steps:
                    if kind == "norm":
                        norm.power(nc, pool, b + base["norm"])
                    if kind == "residual":
                        norm_y.power(nc, pool, b)
                    if kind in ("key", "query"):
                        r = args[-1]
                        pool.wait_ge(parts, item("rope", r) + 1)
                        heads = (1 if latent else NKV0) if kind == "key" else HG if latent else HPAIR
                        dst = rotated_at(kind, args)
                        nc.gpsimd.tensor_tensor(dst, dst, at(crossed, r % 2 * CW, (64, heads), (1, 64)),
                                                ALU.add).then_inc(rotated, 1)
                    if kind == "unit":
                        pool.wait_ge(probs_ready, b * NU + i + 3)
                        pool.wait_ge(pv_done, b * NU + i + 1)
                        nc.gpsimd.tensor_tensor(probs_l[:, i % 2, :], probs[:, i % 2, :], probs_h[:, i % 3, :].bitcast(F32),
                                                ALU.subtract).then_inc(lows_ready, 1)
                    if kind == "cnorm":
                        pool.wait_ge(c_var, b + base["norm"] + 1)
                        nc.gpsimd.tensor_tensor(crs[:], css[:], const["minus_half"][:, 0:TT],
                                                ALU.pow).then_inc(c_rstd, 1)

            section(prologue, 0, none)
            with pool.Fori(0, NSEQ - 1) as b:
                section(body, b, before)
            section(final, NSEQ - 1, before)

        @block.scalar
        def _(act):
            act.sem_inc(probs_ready, 2)
            act.sem_inc(pv_free, 2)

            def section(steps, b, base):
                item = numbering(b, base)
                for s, (kind, args, i) in enumerate(steps):
                    if kind in HIGH:
                        act.wait_ge(misc_ready, item("m", i) + 1)
                        bank = misc[i % 2]
                    if kind == "wquery":
                        act.wait_ge(wq_loaded, (item("wquery", i) + 1) * 16)
                        if steps is not prologue:
                            act.wait_ge(misc_ready, item("m", last_item(steps, s, "query")) + 1)
                        nc.scalar.activation(wq[0][:], wq_raw[:], ACT.Copy).then_inc(wq_high, 1)
                    if kind == "value":
                        nc.scalar.activation(at(Vh, args[0] * VH * VW, (VW, VH), (P, 2), (1, 64)),
                                             at(bank, 0, (P, VH), (64, 2), (1, 64)), ACT.Copy).then_inc(high_done, 1)
                    if kind == "cnorm":
                        act.wait_ge(c_ready, b + base["norm"] + 1)
                        nc.scalar.activation(Vh[:, :, 0, 0:64], craw, ACT.Copy).then_inc(c_high, 1)
                    if kind == "xT":
                        nc.scalar.activation(xTh[:, args[0], :], bank[:], ACT.Copy).then_inc(high_done, 1)
                    if kind == "keyT":
                        if latent:
                            nc.scalar.activation(keyh[:, 0, :], bank[:], ACT.Copy).then_inc(high_done, 1)
                        else:
                            for src in (0, 64):
                                for dst in (0, 64):
                                    ins = nc.scalar.activation(keyh[dst:dst + 64, 2 * args[0] + src // 64, :],
                                                               bank[src:src + 64, :], ACT.Copy)
                            ins.then_inc(high_done, 1)
                    if kind == "queryT":
                        p, n = args
                        if latent:
                            nc.scalar.activation(qa[:, p % 2, n, :], bank[:], ACT.Copy).then_inc(high_done, 1)
                        else:
                            nc.scalar.activation(qa[0:64, p % 2, 2 * n, :], bank[0:64, :], ACT.Copy)
                            nc.scalar.activation(qa[64:128, p % 2, 2 * n + 1, :], bank[64:128, :],
                                                 ACT.Copy).then_inc(high_done, 1)
                    if kind == "unit":
                        act.wait_ge(score_ready, b * NU + i + 1)
                        nc.scalar.activation(probs_h[:, i % 3, :], score[i % 2][:], ACT.Exp, scale=scale)
                        act.wait_ge(lows_ready, b * NU + i + 1)
                        nc.scalar.activation(probs[:, i % 2, :], score[i % 2][:], ACT.Exp,
                                             scale=scale).then_inc(probs_ready, 1)
                    if kind == "evac":
                        p, q, g, u = args
                        act.wait_ge(pv_done, b * NU + u + 3)
                        bank = pvb[i % 2]
                        slot = i % 4
                        act.wait_ge(d_stored[slot], (b * (NG // 4) + i // 4 + 1) * 16)
                        vals_at, sums_at = (0, 64) if latent or g == 0 else (64, 0)
                        nc.scalar.activation(drow[32 * slot:32 * slot + 1, :], bank[sums_at:sums_at + 1, :],
                                             ACT.Copy).then_inc(drow_done, 1)
                        for odd in range(2):
                            dst = bass.AP(tensor=out[:].tensor,
                                          offset=out[64 * odd:64 * odd + 64, p % 2, 2 * g, q * P:q * P + P].offset,
                                          ap=[[out[:].ap[0][0], 64], [SEQ, 2], [1, P]])
                            v = bank[vals_at:vals_at + 64, :].rearrange("p (h n) -> p h n", h=HG)
                            ins = nc.scalar.activation(dst, v[:, odd::2, :], ACT.Copy)
                        ins.then_inc(pv_free, 1)

            section(prologue, 0, none)
            with act.Fori(0, NSEQ - 1) as b:
                section(body, b, before)
            section(final, NSEQ - 1, before)

        @block.vector
        def _(dve):
            dve.sem_inc(misc_free, 2)
            dve.sem_inc(top_free, 2)
            dve.sem_inc(scaled, RSLOTS)
            nc.vector.memset(mrow[:].bitcast(F32), 0.0).then_inc(set_up, 1)
            nc.vector.memset(Vh[:, :, :, 64:128].bitcast(F32), 1.0).then_inc(set_up, 1)
            nc.vector.memset(Vl[:].bitcast(F32), 0.0).then_inc(set_up, 1)
            dve.wait_ge(set_up, 3)

            def tiles_of(n):
                if isinstance(n, int):
                    return [x[:, n * TT + j, :] for j in range(TT)]
                return [x[:, bass.ds(n * TT + j, 1), :].rearrange("p a d -> p (a d)") for j in range(TT)]

            def section(steps, b, base):
                item = numbering(b, base)
                high = 0
                for s, (kind, args, i) in enumerate(steps):
                    if kind == "norm":
                        xb = tiles_of(b + base["norm"])
                        norm.statistics(nc, dve, xb, b + base["norm"])
                        dve.wait_ge(norm.rstd_ready, b + base["norm"] + 1)
                        for j in range(TT):
                            ins = norm.apply(nc, xnt[:, j, :], xb[j], j)
                        ins.then_inc(xn_ready, 1)
                    if kind in HIGH:
                        high += 1
                        dve.wait_ge(high_done, item("high", high - 1) + 1)
                        bank = misc[i % 2]
                    if kind == "wquery":
                        dve.wait_ge(wq_high, item("wquery", i) + 1)
                        nc.vector.tensor_tensor(wq[1][:], wq_raw[:], wq[0][:].bitcast(F32),
                                                ALU.subtract).then_inc(wq_low, 1)
                    if kind == "xT":
                        k, = args
                        nc.vector.tensor_tensor(xTl[:, k, :], bank[:], xTh[:, k, :].bitcast(F32),
                                                ALU.subtract).then_inc(misc_free, 1)
                    if kind == "keyT":
                        h, = args
                        if latent:
                            ins = nc.vector.tensor_tensor(keyl[:, 0, :], bank[:], keyh[:, 0, :].bitcast(F32),
                                                          ALU.subtract)
                        else:
                            for src in (0, 64):
                                for dst in (0, 64):
                                    k = 2 * h + src // 64
                                    ins = nc.vector.tensor_tensor(keyl[dst:dst + 64, k, :], bank[src:src + 64, :],
                                                                  keyh[dst:dst + 64, k, :].bitcast(F32), ALU.subtract)
                        ins.then_inc(misc_free, 1)
                    if kind == "queryT":
                        p, n = args
                        if latent:
                            nc.vector.tensor_tensor(qb[:, p % 2, n, :], bank[:], qa[:, p % 2, n, :].bitcast(F32),
                                                    ALU.subtract).then_inc(misc_free, 1)
                        else:
                            e, o = qa[:, p % 2, 2 * n, :], qa[:, p % 2, 2 * n + 1, :]
                            nc.vector.tensor_tensor(e[64:128], bank[0:64, :], e[0:64].bitcast(F32), ALU.subtract)
                            nc.vector.tensor_tensor(o[0:64], bank[64:128, :], o[64:128].bitcast(F32),
                                                    ALU.subtract).then_inc(misc_free, 1)
                    if kind in ("key", "query"):
                        r = args[-1]
                        dve.wait_ge(misc_ready, item("m", i) + 1)
                        dve.wait_ge(rotated, item("rope", r) + 1)
                        bank = misc[i % 2]
                        if kind == "key":
                            j, (cos, sin) = args[0], w["key_tables"]
                            heads, step = (1, 64) if latent else (NKV0, 64)
                        else:
                            j = args[1] // 2 if latent else args[1]
                            cos, sin = w["query_tables"]
                            heads, step = (HG, P) if latent else (HPAIR, 64)
                        nc.vector.tensor_tensor(rotated_at(kind, args, split=True),
                                                at(bank, 0, (step, heads), (32, 2), (1, 32)),
                                                at(cos, j * 32, (0, heads), (0, 2), (1, 32)), ALU.mult)
                        for lo, hi in ((0, 32), (32, 0)):
                            ins = nc.vector.tensor_tensor(at(crossed, r % 2 * CW + lo, (64, heads), (1, 32)),
                                                          at(bank, hi, (step, heads), (1, 32)),
                                                          at(sin, j * 64 + lo, (0, heads), (1, 32)), ALU.mult)
                        ins.then_inc(parts, 1)
                        if latent and kind == "key":
                            nc.vector.tensor_copy(at(rot, j * RW + 64, (1, 64)), bank[:, 64:128]).then_inc(misc_free, 1)
                        elif latent:
                            nc.vector.tensor_copy(at(rot, j * RW + (args[1] % 2) * 512 + 64, (P, HG), (1, 64)),
                                                  at(bank, 64, (P, HG), (1, 64))).then_inc(misc_free, 1)
                        else:
                            dve.wait_ge(parts, item("rope", r) + 1)
                            nc.vector.memset(pause[:, 0:1], 0.0).then_inc(misc_free, 1)
                    if kind == "value":
                        hi, lo = (at(V, args[0] * VH * VW, (VW, VH), (P, 2), (1, 64)) for V in (Vh, Vl))
                        nc.vector.tensor_tensor(lo, at(bank, 0, (P, VH), (64, 2), (1, 64)), hi.bitcast(F32),
                                                ALU.subtract).then_inc(misc_free, 1)
                    if kind == "cnorm":
                        dve.wait_ge(misc_free, item("m", last_item(steps, s, "key")) + 3)
                        nc.vector.tensor_tensor(csq[:], craw, craw, ALU.mult).then_inc(c_link, 1)
                        dve.wait_ge(c_link, (b + base["norm"]) * 4 + 1)
                        nc.vector.tensor_reduce(css[:], csq[:], AX.X, ALU.add).then_inc(c_link, 1)
                        dve.wait_ge(c_link, (b + base["norm"]) * 4 + 2)
                        nc.vector.tensor_scalar(css[:], css[:], 1.0 / LAT1, RMS_EPS, ALU.mult, ALU.add).then_inc(c_var, 1)
                        dve.wait_ge(c_rstd, b + base["norm"] + 1)
                        nc.vector.tensor_tensor(csq[:], craw, at(crs, 0, (1, TT), (0, 64)), ALU.mult).then_inc(c_link, 1)
                        dve.wait_ge(c_link, (b + base["norm"]) * 4 + 3)
                        if base["norm"]:
                            dve.wait_ge(pv_done, b * NU + NU + 2)
                        weight = at(w["norm_w"], 0, (0, TT), (1, 64))
                        nc.vector.tensor_tensor(craw, csq[:], weight, ALU.mult).then_inc(c_ready, 1)
                        dve.wait_ge(c_high, b + base["norm"] + 1)
                        nc.vector.tensor_tensor(Vl[:, :, 0, 0:64], craw, Vh[:, :, 0, 0:64].bitcast(F32),
                                                ALU.subtract).then_inc(c_link, 1)
                        dve.wait_ge(c_link, (b + base["norm"]) * 4 + 4)
                    if kind == "top":
                        p, q, heads = args
                        dve.wait_ge(top_ready, item("top", i) + 1)
                        n = P * (q + 1)
                        v = topb[i % 2][:, 0:len(heads) * n].rearrange("p (h n) -> p h n", h=len(heads))
                        nc.vector.tensor_reduce(mcol[:, q, heads[0]:heads[-1] + 1], v, AX.X,
                                                ALU.max).then_inc(top_free, 1)
                    if kind == "topT":
                        p, q = args
                        dve.wait_ge(misc_ready, item("m", i) + 1)
                        nc.vector.tensor_tensor(mrow[0:HPAIR, q % 2, :, :],
                                                bass.AP(tensor=misc[i % 2][:].tensor, offset=misc[i % 2][:].offset,
                                                        ap=[[misc[i % 2][:].ap[0][0], HPAIR], [0, HPAIR], [1, P]]),
                                                bass.AP(tensor=ident[:].tensor, offset=ident[:].offset,
                                                        ap=[[ident[:].ap[0][0], HPAIR], [1, HPAIR], [0, P]]),
                                                ALU.mult).then_inc(misc_free, 1)
                    if kind == "even":
                        dve.wait_ge(misc_ready, item("m", i) + 1)
                        nc.vector.memset(pause[:, 1:2], 0.0).then_inc(misc_free, 1)
                    if kind == "recip":
                        p, = args
                        dve.wait_ge(d_loaded, (b * NPAIR + p + 1) * 16)
                        nc.vector.reciprocal(rcol[:], dcol[:]).then_inc(recips, 1)
                    if kind == "scale":
                        p, hp = args
                        n = (b * NPAIR + p) * (HG // RSLOTS) + hp // RSLOTS
                        dve.wait_ge(r_loaded[hp % RSLOTS], (n + 1) * 32)
                        dve.wait_ge(pv_free, b * NG + (p + 1) * 2 * TT + 2)
                        o = out[:, p % 2, hp, :]
                        nc.vector.tensor_tensor(o, o, rtile[:, hp % RSLOTS, :], ALU.mult).then_inc(scaled, 1)
                    if kind == "oproj":
                        p, k = args
                        dve.wait_ge(misc_ready, item("m", i) + 1)
                        if p == 0:
                            nc.vector.tensor_copy(yT[:, k, :], misc[i % 2][:]).then_inc(misc_free, 1)
                        else:
                            nc.vector.tensor_tensor(yT[:, k, :], yT[:, k, :], misc[i % 2][:],
                                                    ALU.add).then_inc(misc_free, 1)
                    if kind == "residual":
                        c = last_item(steps, s, "yT", 0)
                        dve.wait_ge(misc_ready, item("m", last_item(steps, s, "yT", 1)) + 1)
                        half = [misc[c % 2], misc[last_item(steps, s, "yT", 1) % 2]]
                        yt = [half[j // 2][:, (j % 2) * D:(j % 2 + 1) * D] for j in range(TT)]
                        norm_y.statistics(nc, dve, yt, b)
                        dve.wait_ge(norm_y.rstd_ready, b + 1)
                        for j in range(TT):
                            ins = norm_y.apply(nc, addend[:, j, :], yt[j], j)
                            if j % 2:
                                ins.then_inc(misc_free, 1)
                        dve.wait_ge(misc_free, item("m", last_item(steps, s, "yT", 1)) + 3)
                        xb = tiles_of(b)
                        for j in range(TT):
                            ins = nc.vector.tensor_tensor(xb[j], xb[j], addend[:, j, :], ALU.add)
                        ins.then_inc(x_done, 1)
                        dve.wait_ge(x_done, b + 1)
                        nc.vector.memset(pause[:, 2:3], 0.0)

            section(prologue, 0, none)
            with dve.Fori(0, NSEQ - 1) as b:
                section(body, b, before)
            section(final, NSEQ - 1, before)

        @block.tensor
        def _(pe):
            pe.sem_inc(pv_done, 2)
            pe.wait_ge(set_up, 3)

            def section(steps, b, base):
                item = numbering(b, base)
                for s, (kind, args, i) in enumerate(steps):
                    if kind in ("xT", "key", "value", "keyT", "query", "queryT", "topT", "oproj", "yT", "even"):
                        pe.wait_ge(misc_free, item("m", i) + 1)
                        bank = misc[i % 2]
                    if kind == "xT":
                        k, = args
                        pe.wait_ge(xn_ready, b + base["norm"] + 1)
                        for j in range(TT):
                            ins = nc.tensor.transpose(bank[:, j * P:(j + 1) * P], xnt[:, j, k * P:(k + 1) * P],
                                                      ident[:])
                        ins.then_inc(misc_ready, 1)
                    if kind in ("key", "value", "query"):
                        if kind == "key":
                            j, n = args[0], (P if latent else 512)
                            wh, wl = (t[:, :, 0:n] for t in w["key"])
                            if j == 0:
                                pe.wait_ge(misc_free, item("m", last_item(steps, s, "xT")) + 3)
                        elif kind == "value":
                            j, n = args[0], 512
                            wh, wl = (t[:, :, 512:1024] for t in w["key"])
                        else:
                            p, c, _ = args
                            j, half = divmod(c, 2) if latent else (c, 0)
                            n = 512
                            if not latent and c == 0:
                                last = last_item(steps, s, "wquery")
                                pe.wait_ge(wq_low, item("wquery", last) + 1)
                            off = p * QW + half * 512 if latent else 0
                            wh, wl = (t[:, :, off:off + 512] for t in (w["query"] if latent else wq))
                        tok = slice(j * P, (j + 1) * P)
                        terms = [(xs[:, k, tok], ws[:, k, :]) for k in range(KD)
                                 for xs, ws in ((xTh, wh), (xTh, wl), (xTl, wh))]
                        for t, (st, mv) in enumerate(terms):
                            ins = nc.tensor.matmul(bank[:, 0:n], st, mv, start=(t == 0), stop=(t == len(terms) - 1))
                        ins.then_inc(misc_ready, 1)
                        if kind != "value":
                            last_rope = item("rope", args[-1])
                    if kind == "keyT":
                        pe.wait_ge(rotated, last_rope + 3)
                        if latent:
                            pe.wait_ge(c_ready, b + base["norm"] + 1)
                        for j in range(TT):
                            ins = nc.tensor.transpose(bank[:, j * P:(j + 1) * P],
                                                      rot[:, j, args[0] * P:(args[0] + 1) * P], ident[:])
                        ins.then_inc(misc_ready, 1)
                    if kind == "queryT":
                        pe.wait_ge(rotated, last_rope + 3)
                        if latent:
                            pe.wait_ge(misc_free, item("m", last_item(steps, s, "query", args[0])) + 3)
                        for j in range(TT):
                            ins = nc.tensor.transpose(bank[:, j * P:(j + 1) * P],
                                                      rot[:, j, args[1] * P:(args[1] + 1) * P], ident[:])
                        ins.then_inc(misc_ready, 1)
                    if kind == "top":
                        p, q, heads = args
                        pe.wait_ge(top_free, item("top", i) + 1)
                        if q == 0:
                            pe.wait_ge(misc_free, item("m", last_item(steps, s, "queryT", p)) + 3)
                        n = P * (q + 1)
                        for c, h in enumerate(heads):
                            kh = keyh[:, 0 if latent else 2 * p + h // HG, 0:n]
                            nc.tensor.matmul(topb[i % 2][:, c * n:(c + 1) * n], qa[:, p % 2, h, q * P:(q + 1) * P], kh,
                                             start=True, stop=False)
                            ins = nc.tensor.matmul(topb[i % 2][:, (c + 1) * n - P:(c + 1) * n], w["identb"][:],
                                                   w["mask_q"][:], start=False, stop=True)
                        ins.then_inc(top_ready, 1)
                    if kind == "topT":
                        p, q = args
                        pe.wait_ge(top_free, item("top", last_item(steps, s, "top", p, q)) + 3)
                        nc.tensor.transpose(bank[0:HPAIR, 0:P], mcol[:, q, :], ident[:]).then_inc(misc_ready, 1)
                    if kind == "even":
                        nc.tensor.transpose(bank[0:HPAIR, 0:P], mcol[:, 0, :], ident[:]).then_inc(misc_ready, 1)
                    if kind == "unit":
                        p, q, g, k = args
                        pe.wait_ge(probs_ready, b * NU + i + 1)
                        if g == 0 and k == 0:
                            pe.wait_ge(misc_free, item("m", last_item(steps, s, "topT", p, q)) + 3)
                        bank = score[i % 2]
                        kt = slice(k * P, (k + 1) * P)
                        kv = 0 if latent else 2 * p + g
                        qs = [t[:, p % 2, g * HG:(g + 1) * HG, q * P:(q + 1) * P] for t in (qa, qb) if t is not None]
                        terms = [(keyh[:, kv, kt], qs[0]), (keyl[:, kv, kt], qs[0])]
                        if latent:
                            terms.append((keyh[:, kv, kt], qs[1]))
                        terms.append((w["minus_one"][:], mrow[:, q % 2, g * HG:(g + 1) * HG, :]))
                        if k == q:
                            terms.append((w["identb"][:], at(w["mask_k"], 0, (0, HG), (1, P))))
                        for t, (st, mv) in enumerate(terms):
                            ins = nc.tensor.matmul(bank[:], st, mv, start=(t == 0), stop=(t == len(terms) - 1))
                        ins.then_inc(score_ready, 1)
                    if kind == "pv":
                        p, q, g, k, u = args
                        group = (p * TT + q) * 2 + g
                        pe.wait_ge(lows_ready, b * NU + u + 3)
                        if k == 0:
                            pe.wait_ge(pv_free, b * NG + group + 1)
                        h = 0 if latent else 2 * p + g
                        hi, lo = probs_h[:, u % 3, :], probs_l[:, u % 2, :]
                        for t, (V, e) in enumerate(((Vh, hi), (Vh, lo), (Vl, hi))):
                            ins = nc.tensor.matmul(pvb[group % 2][:], vals(V, h, k), e,
                                                   start=(k == 0 and t == 0), stop=(k == q and t == 2))
                        ins.then_inc(pv_done, 1)
                    if kind == "oproj":
                        p, k = args
                        pe.wait_ge(scaled, (b * NPAIR + p + 1) * HG + RSLOTS)
                        if not latent:
                            pe.wait_ge(wo_loaded, (b * NPAIR + p + 1) * 16)
                        for hp in range(HG):
                            st = (w["out"][:, p * HG + hp, k * P:(k + 1) * P] if latent else
                                  wo[:, hp, k * P:(k + 1) * P])
                            ins = nc.tensor.matmul(bank[:], st, out[:, p % 2, hp, :], start=(hp == 0), stop=(hp == HG - 1))
                        ins.then_inc(misc_ready, 1)
                    if kind == "yT":
                        c, = args
                        if c == 0:
                            pe.wait_ge(misc_free, item("m", last_item(steps, s, "oproj")) + 3)
                        for j in range(2):
                            tok = slice((2 * c + j) * P, (2 * c + j + 1) * P)
                            for k in range(KD):
                                ins = nc.tensor.transpose(bank[:, j * D + k * P:j * D + (k + 1) * P],
                                                          yT[:, k, tok], ident[:])
                        ins.then_inc(misc_ready, 1)

            section(prologue, 0, none)
            with pe.Fori(0, NSEQ - 1) as b:
                section(body, b, before)
            section(final, NSEQ - 1, before)

        @block.sync
        def _(sp):
            for s in d_stored:
                sp.sem_inc(s, 16)
            if not latent:
                sp.dma_start(flat(wq_raw), w["query"][0]).then_inc(wq_loaded, 16)
                sp.dma_start(flat(wo), w["out"][0]).then_inc(wo_loaded, 16)

            def section(steps, b, base):
                for kind, args, i in steps:
                    if kind == "wquery" and not (steps is final and args[0] == NPAIR - 1):
                        sp.wait_ge(wq_low, numbering(b, base)("wquery", i) + 1)
                        sp.dma_start(flat(wq_raw), w["query"][(args[0] + 1) % NPAIR]).then_inc(wq_loaded, 16)
                    if kind == "evac":
                        p, q, g, _ = args
                        slot = i % 4
                        sp.wait_ge(drow_done, b * NG + i + 1)
                        sp.dma_start(d_dram[p:p + 1, g * HG:(g + 1) * HG, q * P:(q + 1) * P],
                                     drow[32 * slot:32 * slot + 1, :].rearrange("p (h n) -> p h n", h=HG)
                                     ).then_inc(d_stored[slot], 16)
                    if kind == "dload":
                        p, = args
                        last = (p + 1) * 2 * TT - 1
                        for g in range(last - 3, last + 1):
                            sp.wait_ge(d_stored[g % 4], (b * (NG // 4) + g // 4 + 2) * 16)
                        sp.dma_start(dcol[:], d_dram[p].rearrange("h n -> (h n)").rearrange("(a c) -> a c", c=32)
                                     ).then_inc(d_loaded, 16)
                    if kind == "recip":
                        p, = args
                        sp.wait_ge(recips, b * NPAIR + p + 1)
                        sp.dma_start(r_dram[p].rearrange("h n -> (h n)").rearrange("(a c) -> a c", c=32),
                                     rcol[:]).then_inc(r_stored, 16)
                        sp.wait_ge(r_stored, (b * NPAIR + p + 1) * 16)
                        sp.sem_inc(passed, 1)
                    if kind == "rload":
                        p, hp = args
                        sp.wait_ge(scaled, (b * NPAIR + p) * HG + hp + 1)
                        for odd in range(2):
                            row = r_dram[p, 2 * hp + odd, :]
                            sp.dma_start(rtile[64 * odd:64 * odd + 64, hp % RSLOTS, :],
                                         bass.AP(tensor=row.tensor, offset=row.offset, ap=[[0, 64], [1, SEQ]])
                                         ).then_inc(r_loaded[hp % RSLOTS], 16)
                    if kind == "oproj" and args[1] == KD - 1 and not latent:
                        p, _ = args
                        sp.wait_ge(misc_ready, before["m"] + b * NM + i + 1)
                        sp.dma_start(flat(wo), w["out"][(p + 1) % NPAIR]).then_inc(wo_loaded, 16)

            section(prologue, 0, none)
            with sp.Fori(0, NSEQ - 1) as b:
                section(body, b, before)
            section(final, NSEQ - 1, before)
            if not latent:
                sp.wait_ge(wo_loaded, (NSEQ * NPAIR + 1) * 16)


def attention_constants(nc, m, a, tag, rows):
    c = {"identb": m.sb("identb", [P, P], BF16), "mask_q": m.sb("mask_q", [P, P], BF16),
         "mask_k": m.sb("mask_k", [P, P], BF16), "minus_one": m.sb("minus_one", [P, P], F32R)}
    raw = [("ident", c["identb"]), ("mask_q", c["mask_q"]), ("mask_k", c["mask_k"])]
    tables = {n: m.sb(n, shape) for n, shape in rows.items()}
    with ExitStack() as c0:
        s = c0.enter_context(nc.semaphore(f"{tag}_table_loaded"))
        made = c0.enter_context(nc.semaphore(f"{tag}_masks_made"))
        stage = c0.enter_context(nc.sbuf_tensor(f"{tag}_mask_stage", [P, 4, P], F32))
        block = c0.enter_context(nc.Block())

        @block.sync
        def _(sp):
            for n, (src, _) in enumerate(raw):
                sp.dma_start(stage[:, n, :], a[src]).then_inc(s, 16)
            for n in tables:
                sp.dma_start(flat(tables[n]), a[f"{tag}_{n}"]).then_inc(s, 16)
            sp.wait_ge(s, 16 * (len(raw) + len(tables)))

        @block.vector
        def _(dve):
            nc.vector.memset(stage[:, 3, :], -1.0).then_inc(made, 1)
            dve.wait_ge(s, 16 * (len(raw) + len(tables)))
            dve.wait_ge(made, 1)
            for n, (_, dst) in enumerate(raw):
                nc.vector.tensor_copy(dst[:], stage[:, n, :])
            nc.vector.tensor_copy(c["minus_one"][:], stage[:, 3, :]).then_inc(made, 1)
            dve.wait_ge(made, 2)
    return c | tables


def attention0(nc, a, x, const):
    with ExitStack() as ctx:
        m = Names(nc, ctx, "a0")
        key = [m.sb(f"wkey{s}", [P, KD, 2 * NKV0 * HD0], F32R) for s in "hl"]
        G, HALF = 2 * NKV0, HD0 // 2

        def products(f, bank):
            down, upk, upv = f
            for k in range(KD):
                hid = slice(k * P, (k + 1) * P)
                stat = [down[:, r, hid] for r in range(KD)]
                yield ([(0, 0, D, stat[r], upk[:, r, :], r == 0, r == KD - 1) for r in range(KD)],
                       None, [at(t, k * 1024 + ROPE0, (HALF, G), (1, HALF - ROPE0)) for t in key])
                yield ([(0, 0, 512, stat[r], upv[:, r, :], r == 0, r == KD - 1) for r in range(KD)],
                       None, [t[:, k, 512:1024] for t in key])

        def listed(f, bank):
            got = []
            for i, (mm, _, (hi, lo)) in enumerate(products(f, bank)):
                view = at(bank[i % 2], 0, (16, G), (1, 16)) if i % 2 == 0 else bank[i % 2][:]
                got.append((mm, view, hi, lo))
            return got

        jobs = []
        for k in range(KD):
            hi, lo = (at(t, k * 1024, (HALF, G), (1, ROPE0)) for t in key)
            jobs.append((a["a0_rope"][:, k * 256:(k + 1) * 256], hi, lo))
        split_weights(nc, "a0", jobs, [(a["a0_down"], [P, KD, D]), (a["a0_upk"], [P, KD, 256]),
                                       (a["a0_upv"], [P, KD, 512])], listed)
        t = attention_constants(nc, m, a, "a0", {"qcos": [P, TT, 32], "qsin": [P, TT, 64],
                                                 "kcos": [P, TT, 32], "ksin": [P, TT, 64]})
        w = dict(t, latent=False, rslots=1, scale=1.0 / 8.0, query=a["a0_query"], key=key, out=a["a0_out"],
                 query_tables=(t["qcos"], t["qsin"]), key_tables=(t["kcos"], t["ksin"]))
        attention(nc, "a0", x, const, w, a)


def attention1(nc, a, x, const):
    with ExitStack() as ctx:
        m = Names(nc, ctx, "a1")
        query = [m.sb(f"wquery{s}", [P, KD, NH1 * P], F32R) for s in "hl"]
        key = [m.sb(f"wkey{s}", [P, KD, P], F32R) for s in "hl"]
        outw = m.sb("outw", [P, NH1 // 2, D])

        def folds(f, bank):
            qn, bk, bv, wo = f
            got = []
            for k in range(KD):
                for half in range(2):
                    mm = [(0, h * 64, 64, qn[:, half * 8 + h, k * P:(k + 1) * P], bk[:, half * 8 + h, :], True, True)
                          for h in range(8)]
                    hi, lo = (at(t, k * NH1 * P + half * 8 * P + 64, (P, 8), (1, 64)) for t in query)
                    got.append((mm, at(bank[len(got) % 2], 0, (64, 8), (1, 64)), hi, lo))
            for hp in range(NH1 // 2):
                mm = [(64 * o, 0, D, bv[:, 2 * hp + o, :], wo[:, 2 * hp + o, :], True, True) for o in range(2)]
                got.append((mm, bank[len(got) % 2][:, 0:D], outw[:, hp, :], None))
            return got

        jobs = [(a["a1_key"], flat(key[0]), flat(key[1]))]
        for k in range(KD):
            hi, lo = (at(t, k * NH1 * P, (P, NH1), (1, 64)) for t in query)
            jobs.append((a["a1_rope"][:, k * 1024:(k + 1) * 1024], hi, lo))
        split_weights(nc, "a1", jobs, [(a["a1_nope"], [P, NH1, D]), (a["a1_bk"], [P, NH1, 64]),
                                       (a["a1_bv"], [P, NH1, 64]), (a["a1_wo"], [P, NH1, D])], folds)
        t = attention_constants(nc, m, a, "a1", {"qcos": [P, TT, 32], "qsin": [P, TT, 64], "norm_w": [P, 64]})
        w = dict(t, latent=True, rslots=1, scale=float(1.0 / np.sqrt(ROT1 + NOPE1)), query=query, key=key, out=outw,
                 query_tables=(t["qcos"], t["qsin"]), key_tables=(t["qcos"], t["qsin"]))
        attention(nc, "a1", x, const, w, a)



def build_program(nc, a, out, stages=("a0", "f0", "a1", "f1")):
    with ExitStack() as ctx:
        m = Names(nc, ctx, "all")
        x = m.sb("x", [P, NSEQ * TT, D])
        const = {
            "ident": m.sb("ident", [P, P]),
            "minus_half": m.sb("minus_half", [P, 8]),
        }
        with ExitStack() as c0:
            loaded, made = c0.enter_context(nc.semaphore("const_loaded")), c0.enter_context(nc.semaphore("const_made"))
            block = c0.enter_context(nc.Block())

            @block.sync
            def _(sp):
                sp.dma_start(x[:], a["x"]).then_inc(loaded, 16)
                sp.dma_start(const["ident"][:], a["ident"]).then_inc(loaded, 16)
                sp.wait_ge(loaded, 32)

            @block.vector
            def _(dve):
                nc.vector.memset(const["minus_half"][:], -0.5).then_inc(made, 1)
                dve.wait_ge(made, 1)

        if "a0" in stages:
            attention0(nc, a, x, const)
        if "f0" in stages:
            feed_forward(nc, "f0", x, const, a["f0_weights"], MOE_H,
                         moe=(a["f0_router"], a["f0_spread"], a["f0_before"]), out=out if stages[-1] == "f0" else None)
        if "a1" in stages:
            attention1(nc, a, x, const)
        if "f1" in stages:
            feed_forward(nc, "f1", x, const, a["f1_weights"], INTER, out=out)
        if stages[-1] not in ("f0", "f1"):
            with ExitStack() as c0:
                s = c0.enter_context(nc.semaphore("dbg"))
                block = c0.enter_context(nc.Block())

                @block.sync
                def _(sp):
                    sp.dma_start(out, x[:]).then_inc(s, 16)
                    sp.wait_ge(s, 16)


def flat(t, p=P):
    v = t[:] if not isinstance(t, bass.AP) else t
    names = " ".join(f"d{i}" for i in range(v.ndim - 1))
    return v.rearrange(f"p {names} -> p ({names})")[0:p, :] if v.ndim > 2 else v[0:p, :]



def _layouts(inputs):
    f = {k: np.asarray(v) for k, v in inputs.items()}
    tiles = lambda w: np.ascontiguousarray(w.reshape(-1, P, w.shape[-1]).transpose(1, 0, 2).reshape(P, -1))

    g = {}
    g["x"] = np.ascontiguousarray(f["L0_attn_hidden_states"].reshape(NSEQ * TT, P, D).transpose(1, 0, 2))
    g["ident"] = np.eye(P, dtype=np.float32)
    def by_hidden_tile(gate, up, down):
        nt = -(-gate.shape[1] // P)
        out = np.zeros((P, nt, 3 * D), gate.dtype)
        for c, w in enumerate((gate, up)):
            full = np.zeros((D, nt * P), w.dtype)
            full[:, :w.shape[1]] = w
            out[:, :, c * D:(c + 1) * D] = full.reshape(KD, P, nt, P).transpose(1, 2, 0, 3).reshape(P, nt, D)
        full = np.zeros((nt * P, D), down.dtype)
        full[:down.shape[0]] = down
        out[:, :, 2 * D:] = full.reshape(nt, P, D).transpose(1, 0, 2)
        return out.reshape(P, -1)

    w = f["L1_ffn_w_gate_up"].T
    g["f1_weights"] = by_hidden_tile(w[:, :INTER], w[:, INTER:], f["L1_ffn_w_down"].T)
    beside = lambda e: e.transpose(1, 0, 2).reshape(D, NE * DE)
    g["f0_weights"] = by_hidden_tile(
        np.concatenate([beside(f["L0_ffn_We_gate"]), f["L0_ffn_Ws_gate"]], 1),
        np.concatenate([beside(f["L0_ffn_We_up"]), f["L0_ffn_Ws_up"]], 1),
        np.concatenate([f["L0_ffn_We_down"].reshape(NE * DE, D), f["L0_ffn_Ws_down"]], 0))
    g["f0_router"] = tiles(f["L0_ffn_W_router"])
    owner = np.minimum(np.arange(MOE_H) // DE, NE)
    spread = np.zeros((P, -(-MOE_H // P) * P), np.float32)
    for base in (0, 32):
        spread[base + owner, np.arange(MOE_H)] = 1.0
    g["f0_spread"] = spread
    g["f0_before"] = np.tile((np.arange(NE)[None, :] < np.arange(NE)[:, None]).astype(np.float32).reshape(1, -1), (P, 1))
    i = np.arange(P)
    g["mask_q"] = np.where(i[None, :] > i[:, None], MASKED, 0.0).astype(np.float32)
    g["mask_k"] = np.ascontiguousarray(g["mask_q"].T)
    g["a0_query"] = np.ascontiguousarray(
        f["L0_attn_q_w"].T.reshape(KD, P, NH0 // HPAIR, HPAIR * HD0).transpose(2, 1, 0, 3).reshape(NH0 // HPAIR, P, -1))
    g["a0_rope"] = tiles(f["L0_attn_kr_w"].T)
    g["a0_down"] = tiles(f["L0_attn_down_w"])
    g["a0_upk"] = tiles(f["L0_attn_upk_w"].T)
    g["a0_upv"] = tiles(f["L0_attn_upv_w"].T)
    g["a0_out"] = np.ascontiguousarray(
        f["L0_attn_o_w"].T.reshape(NH0 // HPAIR, HG, P, D).transpose(0, 2, 1, 3).reshape(NH0 // HPAIR, P, HG * D))
    pos = np.arange(SEQ, dtype=np.float32)

    def table(freq):
        angle = (pos[:, None] * freq[None, :]).astype(np.float32).astype(np.float64)
        c = np.cos(angle)
        s = np.concatenate([-np.sin(angle), np.sin(angle)], 1)
        return c.astype(np.float32), s.astype(np.float32)

    inv = (np.float32(1.0) / np.float32(10000.0) ** (np.arange(0, 64, 2, dtype=np.float32) / np.float32(64))).astype(np.float32)
    cos, sin = table(inv)
    for tag in ("a0", "a1"):
        g[f"{tag}_qcos"], g[f"{tag}_qsin"] = tiles(cos), tiles(sin)
    rotated = np.tile(np.arange(HD0 // 2) < ROPE0, 2)
    g["a0_kcos"] = tiles(np.where(rotated[:32], cos, np.float32(1.0)))
    g["a0_ksin"] = tiles(np.where(rotated, sin, np.float32(0.0)))
    apart = np.concatenate([np.arange(0, ROT1, 2), np.arange(1, ROT1, 2)])
    wq = f["L1_attn_Wq"].reshape(D, NH1, NOPE1 + ROT1)
    g["a1_rope"] = tiles(np.ascontiguousarray(wq[:, :, NOPE1 + apart]).reshape(D, NH1 * ROT1))
    g["a1_nope"] = np.ascontiguousarray(wq[:, :, :NOPE1].transpose(2, 1, 0)).reshape(NOPE1, NH1 * D)
    wb = f["L1_attn_Wkv_b"].reshape(LAT1, NH1, NOPE1 + VD1)
    g["a1_bk"] = np.ascontiguousarray(wb[:, :, :NOPE1].transpose(2, 1, 0)).reshape(NOPE1, NH1 * LAT1)
    g["a1_bv"] = np.ascontiguousarray(wb[:, :, NOPE1:].transpose(2, 1, 0)).reshape(VD1, NH1 * LAT1)
    g["a1_wo"] = np.ascontiguousarray(f["L1_attn_Wo"].reshape(NH1, VD1, D).transpose(1, 0, 2)).reshape(VD1, NH1 * D)
    wa = f["L1_attn_Wkv_a"]
    g["a1_key"] = tiles(np.concatenate([wa[:, LAT1 + apart], wa[:, :LAT1]], 1))
    g["a1_norm_w"] = np.tile(f["L1_attn_kv_norm_w"][None, :], (P, 1))
    return g


def kernel(**inputs):
    import numpy as _np
    import concourse.bacc as _bacc
    from concourse import mybir as _mybir
    from concourse.bass_utils import run_bass_kernel_spmd as _run

    g = _layouts(inputs)
    nc = _bacc.Bacc("TRN2", target_bir_lowering=False, num_devices=1)
    a = {k: nc.dram_tensor(f"in_{k}", v.shape, _mybir.dt.from_np(v.dtype), kind="ExternalInput").ap()
         for k, v in g.items()}
    out = nc.dram_tensor("out_x", [P, NSEQ * TT, D], _mybir.dt.float32, kind="ExternalOutput").ap()
    build_program(nc, a, out)
    r = _run(nc, [{f"in_{k}": v for k, v in g.items()}], core_ids=[0])
    y = r.results[0]["out_x"]
    return _np.ascontiguousarray(y.reshape(P, NSEQ * TT, D).transpose(1, 0, 2)).reshape(NSEQ, SEQ, D)
```

```python
from contextlib import ExitStack

import numpy as np

import concourse.bass as bass
from concourse import mybir

F32 = mybir.dt.float32
F32R = mybir.dt.float32r
BF16 = mybir.dt.bfloat16
ALU = mybir.AluOpType
ACT = mybir.ActivationFunctionType
AX = mybir.AxisListType

P = 128
D = 256
KD = D // P
NSEQ, SEQ = 4, 512
TT = SEQ // P
LN_EPS = 1e-5
RMS_EPS = 1.1920928955078125e-07
MASKED = -1e30

NH0, NKV0, HD0 = 32, 8, 64
ROPE0 = 16
NE, DE, DS = 8, 176, 352
MOE_H = NE * DE + DS
NH1, NOPE1, ROT1, LAT1, VD1 = 16, 128, 64, 64, 128
INTER = 1024

HG = 4
HPAIR = 2 * HG


def at(t, offset, *dims):
    base = t[:] if not isinstance(t, bass.AP) else t
    return bass.AP(tensor=base.tensor, offset=base.offset + offset,
                   ap=[list(base.ap[0])] + [list(d) for d in dims])


class Names:

    def __init__(self, nc, ctx, tag):
        self.nc, self.ctx, self.tag = nc, ctx, tag

    def sb(self, name, shape, dt=F32):
        return self.ctx.enter_context(self.nc.sbuf_tensor(f"{self.tag}_{name}", shape, dt))

    def ps(self, name, shape, dt=F32):
        return self.ctx.enter_context(self.nc.psum_tensor(f"{self.tag}_{name}", shape, dt))

    def sem(self, name):
        return self.ctx.enter_context(self.nc.semaphore(f"{self.tag}_{name}"))





class Norm:

    def __init__(self, m, const, which):
        self.stats = m.sb(f"{which}_stats", [P, TT, 6])
        self.mv = m.sb(f"{which}_mv", [P, TT, 2])
        self.var = m.sb(f"{which}_var", [P, TT])
        self.rstd = m.sb(f"{which}_rstd", [P, TT])
        self.pause = m.sb(f"{which}_pause", [P, 1])
        self.minus_half = const["minus_half"]
        self.linked = m.sem(f"{which}_ln_linked")
        self.var_ready = m.sem(f"{which}_ln_var_ready")
        self.rstd_ready = m.sem(f"{which}_ln_rstd_ready")

    def statistics(self, nc, dve, tiles, count):
        for j, tile in enumerate(tiles):
            ins = nc.vector.bn_stats(self.stats[:, j, :], tile)
        ins.then_inc(self.linked, 1)
        dve.wait_ge(self.linked, count * 2 + 1)
        nc.vector.memset(self.pause[:], 0.0)
        for j in range(len(tiles)):
            ins = nc.vector.bn_aggr(self.mv[:, j, :], self.stats[:, j, :])
        ins.then_inc(self.linked, 1)
        dve.wait_ge(self.linked, count * 2 + 2)
        nc.vector.tensor_scalar(self.var[:], self.mv[:, :, 1], LN_EPS, None, ALU.add).then_inc(self.var_ready, 1)

    def power(self, nc, pool, count):
        pool.wait_ge(self.var_ready, count + 1)
        nc.gpsimd.tensor_tensor(self.rstd[:], self.var[:], self.minus_half[:, 0:TT],
                                ALU.pow).then_inc(self.rstd_ready, 1)

    def apply(self, nc, out, tile, j):
        return nc.vector.tensor_scalar(out, tile, self.mv[:, j, 0:1], self.rstd[:, j:j + 1],
                                       ALU.subtract, ALU.mult)



def split_weights(nc, tag, jobs, sources=(), products=None, loads=()):
    CHUNK = 2048
    pieces = []
    for src, hi, lo in jobs:
        if hi.ndim == 3:
            pieces.append((src, hi, lo))
            continue
        for c in range(0, src.shape[1], CHUNK):
            e = min(c + CHUNK, src.shape[1])
            pieces.append((src[:, c:e], hi[:, c:e], lo[:, c:e] if lo is not None else None))
    with ExitStack() as ctx:
        w = Names(nc, ctx, f"{tag}_w")
        NB = 3
        stage = w.sb("stage", [P, NB, CHUNK])
        junk = w.sb("junk", [P, 32])
        loaded = [w.sem(f"piece_loaded{i}") for i in range(NB)]
        hi_done = w.sem("hi_done")
        lo_done = w.sem("lo_done")
        if sources:
            src_loaded = w.sem("src_loaded")
            fold_ready = w.sem("fold_ready")
        bank = [w.ps(f"fold{i}", [P, 512]) for i in range(2)]
        factors = [w.sb(f"factor{k}", shape) for k, (_, shape) in enumerate(sources)]
        folds = products(factors, bank) if products else []
        block = ctx.enter_context(nc.Block())

        def slot(i):
            src, hi, _ = pieces[i]
            v = stage[:, i % NB, 0:src.shape[1]]
            return v.rearrange("p (a b) -> p a b", a=hi.shape[1]) if hi.ndim == 3 else v

        @block.sync
        def _(sp):
            for t, (src, _) in zip(factors, sources):
                sp.dma_start(flat(t), src).then_inc(src_loaded, 16)
            for i, (src, _, _) in enumerate(pieces):
                if i >= NB:
                    sp.wait_ge(lo_done, i - NB + 1)
                sp.dma_start(stage[:, i % NB, 0:src.shape[1]], src).then_inc(loaded[i % NB], 16)
            if loads:
                sp.wait_ge(src_loaded, 16 * len(sources))
            for dst, src in loads:
                sp.dma_start(dst, src).then_inc(src_loaded, 16)
            if loads:
                sp.wait_ge(src_loaded, 16 * (len(sources) + len(loads)))

        @block.scalar
        def _(act):
            for i, (_, hi, _) in enumerate(pieces):
                act.wait_ge(loaded[i % NB], 16 * (i // NB + 1))
                nc.scalar.activation(hi, slot(i), ACT.Copy).then_inc(hi_done, 1)
            for i, (_, view, hi, _) in enumerate(folds):
                act.wait_ge(fold_ready, i + 1)
                nc.scalar.activation(hi, view, ACT.Copy).then_inc(hi_done, 1)

        @block.vector
        def _(dve):
            for i, (_, hi, lo) in enumerate(pieces):
                dve.wait_ge(hi_done, i + 1)
                ins = (nc.vector.memset(junk[:, i:i + 1], 0.0) if lo is None else
                       nc.vector.tensor_tensor(lo, slot(i), hi.bitcast(F32), ALU.subtract))
                ins.then_inc(lo_done, 1)
            for i, (_, view, hi, lo) in enumerate(folds):
                dve.wait_ge(hi_done, len(pieces) + i + 1)
                ins = (nc.vector.memset(junk[:, len(pieces) + i:len(pieces) + i + 1], 0.0) if lo is None else
                       nc.vector.tensor_tensor(lo, view, hi.bitcast(F32), ALU.subtract))
                ins.then_inc(lo_done, 1)

        @block.tensor
        def _(pe):
            if folds:
                pe.wait_ge(src_loaded, 16 * len(factors))
            for i, (matmuls, _, _, _) in enumerate(folds):
                if i >= 2:
                    pe.wait_ge(lo_done, len(pieces) + i - 1)
                for part, col, n, stat, mov, start, stop in matmuls:
                    ins = nc.tensor.matmul(bank[i % 2][part:part + stat.shape[1], col:col + n], stat, mov,
                                           start=start, stop=stop)
                ins.then_inc(fold_ready, 1)


def last_item(steps, s, kind, *args):
    found = [i for k, a, i in steps[:s] if k == kind and a[:len(args)] == args]
    return found[-1] if found else -1



AHEAD = 5


def feed_forward_steps(nt, moe):
    counts = {}

    def build(tiles, begin_at, end_at, first=False):
        steps, items = [], 0

        def add(kind, *args, ring=False):
            nonlocal items
            steps.append((kind, args, items if ring else None))
            items += ring

        def begin(stage):
            if stage == 0:
                add("center")
            if stage == 1:
                add("norm")
                for k in range(KD):
                    add("xT", k, ring=True)
            if stage == 2 and moe:
                add("routerT", ring=True)
                add("logits", ring=True)
            if stage == 3 and moe:
                add("share")
            if stage == 4 and moe:
                add("rank")
                add("combine", ring=True)

        def down(t):
            add("down", t)
            if t == nt - 1:
                add("leave")

        if tiles[0] == 0:
            begin(0)
            add("weights", 0)
            begin(1)
            if moe:
                add("router")
                begin(2)
                add("project", 0)
                add("weights", 1)
                begin(3)
                add("project", 1)
                add("table")
                begin(4)
            else:
                add("weights", 1)
        for t in tiles:
            if begin_at is not None:
                begin(t - begin_at)
                if moe and t == begin_at + 6:
                    add("even", ring=True)
            if t >= 2:
                add("low", t - 2)
            if not (moe and tiles[0] == 0 and t < 2):
                add("project", t)
            if first and t + 2 < nt:
                add("weights", t + 2)
            if t == end_at:
                for c in range(2):
                    add("yT", c, ring=True)
            if moe:
                add("spread", t, ring=True)
            add("product", t)
            if t >= 1:
                add("high", t - 1)
            if t >= 2:
                down(t - 2)
            if t == end_at + 1:
                add("y_center")
            if t == end_at + 2:
                add("residual")
        if tiles[-1] == nt - 1:
            add("low", nt - 2)
            add("high", nt - 1)
            down(nt - 2)
            add("low", nt - 1)
            down(nt - 1)
            for c in range(2):
                add("yT", c, ring=True)
            add("y_center")
            add("residual")
        counts[len(counts)] = items
        return steps

    prologue = build(range(AHEAD), None, nt + 2, first=True)
    opening = build(range(AHEAD, nt + AHEAD), AHEAD, nt + 2, first=True)
    body = build(range(AHEAD, nt + AHEAD), AHEAD, nt + 2)
    final = build(range(AHEAD, nt), None, nt + 2)
    if counts[0] % 2:
        raise ValueError("the prologue needs an even number of items")
    assert counts[1] == counts[2] and counts[1] % 2 == 0
    return prologue, opening, body, final, counts[0], counts[1]


def feed_forward(nc, tag, x, const, weights, hidden, moe=None, out=None):
    NT = -(-hidden // P)
    TW = 2 * D + D
    NSTAGE = 3
    prologue, opening, body, final, BEFORE, NMISC = feed_forward_steps(NT, moe is not None)
    with ExitStack() as ctx:
        m = Names(nc, ctx, tag)
        norm = Norm(m, const, "in")
        norm_y = Norm(m, const, "out")
        ident = const["ident"]
        xn = m.sb("xn", [P, TT, D])
        y = m.sb("y", [P, TT, D])
        xTh = m.sb("xTh", [P, 2, KD, SEQ], F32R)
        xTl = m.sb("xTl", [P, 2, KD, SEQ], F32R)
        sg = m.sb("sg", [P, 2, SEQ])
        hf = m.sb("hf", [P, 2, SEQ])
        hg = m.sb("hg", [P, 2, SEQ]) if moe else hf
        hh = m.sb("hh", [P, 2, SEQ], F32R)
        hl = m.sb("hl", [P, 2, SEQ], F32R)
        yT = m.sb("yT", [P, KD, SEQ])
        wh = m.sb("wh", [P, NT, TW], F32R)
        wl = m.sb("wl", [P, NT, TW], F32R)
        stage = m.sb("stage", [P, NSTAGE, TW])
        pause = m.sb("pause", [P, 1])
        misc = [m.ps(f"misc{i}", [P, 512]) for i in range(2)]
        gb = [m.ps(f"gate{i}", [P, 512]) for i in range(2)]
        ub = [m.ps(f"up{i}", [P, 512]) for i in range(2)]
        yb = [m.ps(f"y{i}", [P, 512]) for i in range(KD)]

        xn_ready = m.sem("xn_ready")
        misc_ready = m.sem("misc_ready")
        misc_free = m.sem("misc_free")
        xh_ready = m.sem("xh_ready")
        g_ready = m.sem("g_ready")
        u_ready = m.sem("u_ready")
        s_done = m.sem("s_done")
        hf_done = m.sem("hf_done")
        hh_done = m.sem("hh_done")
        hl_done = m.sem("hl_done")
        dn_done = m.sem("dn_done")
        y_left = m.sem("y_left")
        y_normed = m.sem("y_normed")
        x_done = m.sem("x_done")
        if out is not None:
            stored = m.sem("stored")
        w_loaded = [m.sem(f"w_loaded{i}") for i in range(NSTAGE)]
        wh_done = m.sem("wh_done")
        wl_done = m.sem("wl_done")
        if moe:
            router_raw = m.sb("router_raw", [P, KD, NE])
            spread_raw = m.sb("spread_raw", [P, NT * P])
            before = m.sb("before", [P, NE, NE])
            router = [m.sb(f"router{s}", [P, KD, NE], F32R) for s in "hl"]
            spread = m.sb("spread", [P, NT * P], F32R)
            lt = m.sb("lt", [P, SEQ])
            ce = m.sb("ce", [P, TT, NE])
            mx = m.sb("mx", [P, TT])
            su = m.sb("su", [P, TT])
            rs = m.sb("rs", [P, TT])
            gtm = m.sb("gtm", [P, TT, NE, NE])
            eqm = m.sb("eqm", [P, TT, NE, NE])
            cnt = m.sb("cnt", [P, TT, NE])
            cmb = m.sb("cmb", [P, TT, 16])
            cT = m.sb("cT", [P, 2, SEQ], F32R)
            r_loaded = m.sem("r_loaded")
            spread_loaded = m.sem("spread_loaded")
            rh_done = m.sem("rh_done")
            rl_done = m.sem("rl_done")
            set_up = m.sem("set_up")
            exp_done = m.sem("exp_done")
            rt_link = m.sem("rt_link")
            cmb_ready = m.sem("cmb_ready")
            cT_ready = m.sem("cT_ready")
        SHARE_LINKS, RANK_LINKS = 4, 4
        RT_LINKS = SHARE_LINKS + RANK_LINKS
        block = ctx.enter_context(nc.Block())

        def of(t, n):
            return t[:, n % 2:n % 2 + 1] if isinstance(n, int) else t[:, bass.ds(n % 2, 1)]

        def tile_of(t, n, k):
            return of(t, n)[:, :, k, :].rearrange("p a n -> p (a n)")

        def weights_of(n, rows):
            return of(cT, n)[rows].rearrange("p a n -> p (a n)")

        def everything(engine, section):
            section(prologue, 0, 0, 0)
            section(opening, 0, BEFORE, 1)
            with engine.Fori(1, NSEQ - 1) as b:
                section(body, b, b * NMISC + BEFORE, b + 1)
            section(final, NSEQ - 1, (NSEQ - 1) * NMISC + BEFORE, NSEQ)

        @block.gpsimd
        def _(pool):
            def section(steps, b, item, n):
                for kind, _, _ in steps:
                    if kind == "center":
                        norm.power(nc, pool, n)
                    if kind == "y_center":
                        norm_y.power(nc, pool, b)

            everything(pool, section)

        @block.scalar
        def _(act):
            act.sem_inc(s_done, 2)

            def section(steps, b, item, n):
                for s, (kind, args, i) in enumerate(steps):
                    if kind == "weights":
                        t, = args
                        act.wait_ge(w_loaded[t % NSTAGE], (t // NSTAGE + 1) * 16)
                        nc.scalar.activation(wh[:, t, :], stage[:, t % NSTAGE, :], ACT.Copy).then_inc(wh_done, 1)
                    if kind == "router":
                        act.wait_ge(r_loaded, 32)
                        nc.scalar.activation(router[0][:], router_raw[:], ACT.Copy).then_inc(rh_done, 1)
                    if kind == "table":
                        act.wait_ge(spread_loaded, 16)
                        nc.scalar.activation(spread[:], spread_raw[:], ACT.Copy).then_inc(rh_done, 1)
                    if kind == "xT":
                        act.wait_ge(misc_ready, item + i + 1)
                        nc.scalar.activation(tile_of(xTh, n, args[0]), misc[i % 2][:], ACT.Copy).then_inc(xh_ready, 1)
                    if kind == "share":
                        act.wait_ge(misc_free, item + last_item(steps, s, "logits") + 3)
                        nc.scalar.activation(ce[:], ce[:], ACT.Exp).then_inc(exp_done, 1)
                    if kind == "project":
                        t, = args
                        act.wait_ge(g_ready, b * NT + t + 1)
                        act.wait_ge(hf_done, b * NT + t + 1)
                        nc.scalar.activation(sg[:, t % 2, :], gb[t % 2][:], ACT.Silu).then_inc(s_done, 1)
                    if kind == "high":
                        t, = args
                        if moe:
                            act.wait_ge(misc_free, item + last_item(steps, s, "spread", t) + 3)
                        else:
                            act.wait_ge(hf_done, b * NT + t + 3)
                        act.wait_ge(dn_done, b * NT + t + 1)
                        nc.scalar.activation(hh[:, t % 2, :], hg[:, t % 2, :], ACT.Copy).then_inc(hh_done, 1)

            everything(act, section)

        @block.vector
        def _(dve):
            dve.sem_inc(misc_free, 2)
            dve.sem_inc(hf_done, 2)
            dve.sem_inc(y_left, 2)
            if moe:
                nc.vector.memset(cT[:].bitcast(F32), 0.0).then_inc(set_up, 1)
                nc.vector.memset(lt[:], 0.0).then_inc(set_up, 1)
                nc.vector.memset(cmb[:], 0.0).then_inc(set_up, 1)
                dve.wait_ge(set_up, 3)
                nc.vector.memset(cmb[:, :, NE:NE + 1], 1.0).then_inc(set_up, 1)
                dve.wait_ge(set_up, 4)

            def x_of(n):
                if isinstance(n, int):
                    return [x[:, n * TT + j, :] for j in range(TT)]
                return [x[:, bass.ds(n * TT + j, 1), :].rearrange("p a d -> p (a d)") for j in range(TT)]

            def section(steps, b, item, n):
                link_count = 0

                def link(ins):
                    nonlocal link_count
                    link_count += 1
                    ins.then_inc(rt_link, 1)
                    dve.wait_ge(rt_link, n * RT_LINKS + link_count)

                for s, (kind, args, i) in enumerate(steps):
                    if i is not None and kind != "xT":
                        dve.wait_ge(misc_ready, item + i + 1)
                    if kind == "weights":
                        t, = args
                        dve.wait_ge(wh_done, t + 1)
                        nc.vector.tensor_tensor(wl[:, t, :], stage[:, t % NSTAGE, :], wh[:, t, :].bitcast(F32),
                                                ALU.subtract).then_inc(wl_done, 1)
                    if kind == "router":
                        dve.wait_ge(rh_done, 1)
                        nc.vector.tensor_tensor(router[1][:], router_raw[:], router[0][:].bitcast(F32),
                                                ALU.subtract).then_inc(rl_done, 1)
                    if kind == "center":
                        norm.statistics(nc, dve, x_of(n), n)
                    if kind == "norm":
                        dve.wait_ge(norm.rstd_ready, n + 1)
                        for j, tile in enumerate(x_of(n)):
                            ins = norm.apply(nc, xn[:, j, :], tile, j)
                        ins.then_inc(xn_ready, 1)
                    if kind == "xT":
                        k, = args
                        dve.wait_ge(xh_ready, n * KD + k + 1)
                        nc.vector.tensor_tensor(tile_of(xTl, n, k), misc[i % 2][:],
                                                tile_of(xTh, n, k).bitcast(F32), ALU.subtract).then_inc(misc_free, 1)
                    if kind == "routerT":
                        nc.vector.tensor_copy(lt[0:NE, :], misc[i % 2][0:NE, :]).then_inc(misc_free, 1)
                    if kind == "logits":
                        logits = at(misc[i % 2], 0, (P, TT), (1, NE))
                        link(nc.vector.tensor_reduce(mx[:], logits, AX.X, ALU.max))
                        nc.vector.tensor_tensor(ce[:], logits, at(mx, 0, (1, TT), (0, NE)),
                                                ALU.subtract).then_inc(misc_free, 1)
                    if kind == "share":
                        dve.wait_ge(exp_done, n + 1)
                        link(nc.vector.tensor_reduce(su[:], ce[:], AX.X, ALU.add))
                        link(nc.vector.reciprocal(rs[:], su[:]))
                        link(nc.vector.tensor_tensor(ce[:], ce[:], at(rs, 0, (1, TT), (0, NE)), ALU.mult))
                        assert link_count == SHARE_LINKS
                    if kind == "rank":
                        mine = at(ce, 0, (NE, TT), (1, NE), (0, NE))
                        other = at(ce, 0, (NE, TT), (0, NE), (1, NE))
                        nc.vector.tensor_tensor(gtm[:], other, mine, ALU.is_gt)
                        link(nc.vector.tensor_tensor(eqm[:], other, mine, ALU.is_equal))
                        link(nc.vector.tensor_tensor(eqm[:], eqm[:], at(before, 0, (0, TT), (NE, NE), (1, NE)),
                                                     ALU.mult))
                        link(nc.vector.tensor_tensor(gtm[:], gtm[:], eqm[:], ALU.add))
                        link(nc.vector.tensor_reduce(cnt[:], gtm[:], AX.X, ALU.add))
                        nc.vector.scalar_tensor_tensor(out=cmb[:, :, 0:NE], in0=cnt[:], scalar=1.5, in1=ce[:],
                                                       op0=ALU.is_lt, op1=ALU.mult).then_inc(cmb_ready, 1)
                        assert link_count == RT_LINKS
                    if kind == "combine":
                        bank = misc[i % 2]
                        nc.vector.tensor_copy(weights_of(n, slice(0, 16)), bank[0:16, :]).then_inc(cT_ready, 1)
                        dve.wait_ge(cT_ready, n + 1)
                        nc.vector.tensor_tensor(weights_of(n, slice(32, 48)), bank[0:16, :],
                                                weights_of(n, slice(0, 16)).bitcast(F32),
                                                ALU.subtract).then_inc(misc_free, 1)
                    if kind == "even":
                        nc.vector.memset(pause[:], 0.0).then_inc(misc_free, 1)
                    if kind == "low":
                        t, = args
                        dve.wait_ge(hh_done, b * NT + t + 1)
                        nc.vector.tensor_tensor(hl[:, t % 2, :], hg[:, t % 2, :], hh[:, t % 2, :].bitcast(F32),
                                                ALU.subtract).then_inc(hl_done, 1)
                    if kind == "product":
                        t, = args
                        dve.wait_ge(s_done, b * NT + t + 3)
                        dve.wait_ge(u_ready, b * NT + t + 1)
                        if not isinstance(b, int) or t >= 2:
                            dve.wait_ge(hl_done, b * NT + t - 1)
                        nc.vector.tensor_tensor(hf[:, t % 2, :], sg[:, t % 2, :], ub[t % 2][:],
                                                ALU.mult).then_inc(hf_done, 1)
                        if moe:
                            c = last_item(steps, s, "spread", t)
                            dve.wait_ge(misc_ready, item + c + 1)
                            dve.wait_ge(hf_done, b * NT + t + 3)
                            nc.vector.tensor_tensor(hg[:, t % 2, :], hf[:, t % 2, :], misc[c % 2][:],
                                                    ALU.mult).then_inc(misc_free, 1)
                    if kind == "leave":
                        dve.wait_ge(dn_done, b * NT + NT + 2)
                        for k in range(KD):
                            nc.vector.tensor_copy(yT[:, k, :], yb[k][:]).then_inc(y_left, 1)
                    if kind == "yT":
                        c, = args
                        nc.vector.tensor_copy(y[:, 2 * c:2 * c + 2, :].rearrange("p a d -> p (a d)"),
                                              misc[i % 2][:]).then_inc(misc_free, 1)
                    if kind == "y_center":
                        dve.wait_ge(misc_free, item + last_item(steps, s, "yT") + 3)
                        norm_y.statistics(nc, dve, [y[:, j, :] for j in range(TT)], b)
                    if kind == "residual":
                        dve.wait_ge(norm_y.rstd_ready, b + 1)
                        for j in range(TT):
                            ins = norm_y.apply(nc, y[:, j, :], y[:, j, :], j)
                        ins.then_inc(y_normed, 1)
                        dve.wait_ge(y_normed, b + 1)
                        for j, tile in enumerate(x_of(b)):
                            ins = nc.vector.tensor_tensor(tile, tile, y[:, j, :], ALU.add)
                        ins.then_inc(x_done, 1)

            everything(dve, section)

        @block.tensor
        def _(pe):
            pe.sem_inc(dn_done, 2)

            def columns(w, t, c):
                return w[:, t % NT, c * P:(c + 1) * P]

            def project(bank, first, t, n):
                terms = [(columns(w, t, first + k), tile_of(xs, n, k)) for k in range(KD)
                         for w, xs in ((wh, xTh), (wh, xTl), (wl, xTh))]
                for s, (st, mv) in enumerate(terms):
                    ins = nc.tensor.matmul(bank[:], st, mv, start=(s == 0), stop=(s == len(terms) - 1))
                return ins

            def section(steps, b, item, n):
                for s, (kind, args, i) in enumerate(steps):
                    if i is not None:
                        pe.wait_ge(misc_free, item + i + 1)
                        bank = misc[i % 2]
                    if kind == "xT":
                        k, = args
                        pe.wait_ge(xn_ready, n + 1)
                        for j in range(TT):
                            ins = nc.tensor.transpose(bank[:, j * P:(j + 1) * P], xn[:, j, k * P:(k + 1) * P], ident[:])
                        ins.then_inc(misc_ready, 1)
                    if kind == "weights":
                        pe.wait_ge(wl_done, args[0] + 1)
                    if kind == "router":
                        pe.wait_ge(rl_done, 1)
                    if kind == "table":
                        pe.wait_ge(rh_done, 2)
                    if kind == "routerT":
                        pe.wait_ge(misc_free, item + last_item(steps, s, "xT") + 3)
                        terms = [(r[:, k, :], tile_of(xs, n, k)) for k in range(KD)
                                 for r, xs in ((router[0], xTh), (router[0], xTl), (router[1], xTh))]
                        for c, (st, mv) in enumerate(terms):
                            ins = nc.tensor.matmul(bank[0:NE, :], st, mv, start=(c == 0), stop=(c == len(terms) - 1))
                        ins.then_inc(misc_ready, 1)
                    if kind == "logits":
                        pe.wait_ge(misc_free, item + last_item(steps, s, "routerT") + 3)
                        for j in range(TT):
                            ins = nc.tensor.transpose(bank[:, j * P:(j + 1) * P], lt[:, j * P:(j + 1) * P], ident[:])
                        ins.then_inc(misc_ready, 1)
                    if kind == "combine":
                        pe.wait_ge(cmb_ready, n + 1)
                        for j in range(TT):
                            ins = nc.tensor.transpose(bank[0:16, j * P:(j + 1) * P], cmb[:, j, :], ident[:])
                        ins.then_inc(misc_ready, 1)
                    if kind == "even":
                        nc.tensor.transpose(bank[0:16, 0:P], cmb[:, 0, :], ident[:]).then_inc(misc_ready, 1)
                    if kind == "project":
                        t, = args
                        if t % NT == 0:
                            pe.wait_ge(misc_free, item + last_item(steps, s, "xT") + 3)
                        whose = n if t % NT < AHEAD else b
                        pe.wait_ge(s_done, b * NT + t + 1)
                        project(gb[t % 2], 0, t, whose).then_inc(g_ready, 1)
                        pe.wait_ge(hf_done, b * NT + t + 1)
                        project(ub[t % 2], KD, t, whose).then_inc(u_ready, 1)
                    if kind == "spread":
                        t, = args
                        whose = n if t % NT < AHEAD else b
                        if t % NT == 0:
                            pe.wait_ge(misc_free, item + last_item(steps, s, "combine") + 3)
                        nc.tensor.matmul(bank[:], spread[:, t % NT * P:(t % NT + 1) * P], weights_of(whose, slice(0, P)),
                                         start=True, stop=True).then_inc(misc_ready, 1)
                    if kind == "down":
                        t, = args
                        first, last = t % NT == 0, t % NT == NT - 1
                        pe.wait_ge(hl_done, b * NT + t + 1)
                        if first:
                            pe.wait_ge(y_left, n * KD + 2)
                        for k in range(KD):
                            for c, (wt, hs) in enumerate(((wh, hh), (wh, hl), (wl, hh))):
                                ins = nc.tensor.matmul(yb[k][:], columns(wt, t, 2 * KD + k), hs[:, t % 2, :], start=(first and c == 0),
                                                       stop=(last and c == 2))
                        ins.then_inc(dn_done, 1)
                    if kind == "yT":
                        c, = args
                        pe.wait_ge(y_left, b * KD + KD + 2)
                        for j in range(2):
                            tok = slice((2 * c + j) * P, (2 * c + j + 1) * P)
                            for k in range(KD):
                                ins = nc.tensor.transpose(bank[:, j * D + k * P:j * D + (k + 1) * P],
                                                          yT[:, k, tok], ident[:])
                        ins.then_inc(misc_ready, 1)

            everything(pe, section)

        @block.sync
        def _(sp):
            for t in range(NT):
                if moe and t == 1:
                    sp.dma_start(flat(router_raw), moe[0]).then_inc(r_loaded, 16)
                    sp.dma_start(flat(before), moe[2]).then_inc(r_loaded, 16)
                if moe and t == 2:
                    sp.dma_start(spread_raw[:], moe[1]).then_inc(spread_loaded, 16)
                if t >= NSTAGE:
                    sp.wait_ge(wl_done, t - NSTAGE + 1)
                sp.dma_start(stage[:, t % NSTAGE, :], weights[:, t * TW:(t + 1) * TW]).then_inc(
                    w_loaded[t % NSTAGE], 16)
            if out is not None:
                with sp.Fori(0, NSEQ) as b:
                    sp.wait_ge(x_done, b + 1)
                    sp.dma_start(out[:, bass.ds(b * TT, TT), :], x[:, bass.ds(b * TT, TT), :]).then_inc(stored, 16)
                sp.wait_ge(stored, 16 * NSEQ)




HIGH = ("xT", "value", "keyT", "queryT")


def attention_steps(latent, rslots):
    npair = (NH1 if latent else NH0) // HPAIR
    steps = []
    count = {"m": 0, "top": 0, "unit": 0, "evac": 0, "rope": 0, "high": 0, "wquery": 0}

    def add(kind, *args, ring=None):
        n = None
        if ring:
            n = count[ring]
            count[ring] += 1
        steps.append((kind, args, n))
        count["high"] += kind in HIGH

    def rope(kind, *args):
        n = count["m"]
        count["m"] += 1
        steps.append((kind, (*args, count["rope"]), n))
        count["rope"] += 1

    def query_weights(p):
        return [] if latent else [lambda: add("wquery", p, ring="wquery")]

    def query(p):
        return [lambda c=c: rope("query", p, c) for c in range(TT * (2 if latent else 1))]

    def queryT(p):
        return [lambda i=i: add("queryT", p, i, ring="m") for i in range(HPAIR if latent else HPAIR // 2)]

    def tops(p, q):
        per = max(1, SEQ // (P * (q + 1)))
        return [lambda h=h: add("top", p, q, tuple(range(h, h + per)), ring="top")
                for h in range(0, HPAIR, per)]

    def topT(p, q):
        return [lambda: add("topT", p, q, ring="m")]

    def output(p):
        chain = [lambda: add("dload", p), lambda: add("recip", p)]
        for hp in range(HG + rslots - 1):
            if hp < HG:
                chain.append(lambda hp=hp: add("rload", p, hp))
            if hp >= rslots - 1:
                chain.append(lambda hp=hp: add("scale", p, hp - rslots + 1))
        return chain, [lambda k=k: add("oproj", p, k, ring="m") for k in range(KD)]

    def run(fs):
        for f in fs:
            f()

    def early():
        return ([lambda: add("center"), lambda: add("norm")] +
                [lambda k=k: add("xT", k, ring="m") for k in range(KD)] + query_weights(0) +
                [lambda j=j: rope("key", j) for j in range(TT)] +
                ([lambda: add("cnorm")] if latent else
                 [lambda h=h: add("keyT", h, ring="m") for h in range(NKV0 // 2 - 1)]) +
                [lambda: add("hold", 0 if latent else NKV0 // 2 - 1, ring="m")] + query(0) + queryT(0))

    def late():
        maxima = tops(0, 0) + topT(0, 0), tops(0, 1) + topT(0, 1)
        if (count["m"] + (2 if latent else TT + 2)) % 2:
            add("even", ring="m")
        if latent:
            return [lambda: add("keysplit")] + maxima[0], maxima[1], [lambda: add("csplit")]
        values = [lambda j=j: add("value", j, ring="m") for j in range(TT)]
        return maxima[0], maxima[1], values + [lambda: add("keysplit")]

    run(early())
    for part in late():
        run(part)
    assert count["m"] % 2 == 0 and count["top"] % 2 == 0
    prologue, before = steps, dict(count)
    units = [(p, q, g, k) for p in range(npair) for q in range(TT) for g in range(2) for k in range(q + 1)]
    UNITS = TT * (TT + 1)

    def finish(u):
        add("pv", *units[u], u)
        p, q, g, k = units[u]
        if k == q:
            add("evac", p, q, g, u, ring="evac")

    def beside(p, has_prev, has_next):
        after = [[] for _ in range(UNITS)]

        def place(items, places):
            for f, n in zip(items, places, strict=True):
                after[n].append(f)

        place(tops(p, 2), [0, 1, 1, 2, 2, 3, 3, 3])
        place(topT(p, 2), [4])
        place(tops(p, 3), [5, 5, 6, 6, 7, 7, 8, 8])
        place(topT(p, 3), [9])
        chain, proj = output(p - 1)
        if p:
            place(chain, [3, 5, 6, 8, 8, 10, 10, 12, 12, 14])
            place(proj, [17, 18])
            if p == 1 and has_prev:
                place(finish_y(True)[3:], [11, 14] if latent else [5, 8])
        elif has_prev:
            place(chain, [0, 3, 3, 6, 6, 8, 8, 10, 10, 12])
            place(proj, [13, 14])
            place(finish_y(True)[:3], [15, 15, 15])
        if p + 1 < npair:
            place(query_weights(p + 1), [] if latent else [2 if p == 0 else 0])
            place(query(p + 1), range(2, 10) if latent else [4, 5, 6, 7] if p == 0 else [2, 4, 5, 6])
            place(queryT(p + 1), [11, 11, 12, 12, 13, 13, 14, 14] if latent else [9, 11, 12, 13])
            place(tops(p + 1, 0), [16, 16])
            place(topT(p + 1, 0), [17])
            place(tops(p + 1, 1), [17, 17, 18, 18])
            place(topT(p + 1, 1), [19])
        elif has_next:
            place(early(), [0, 1, 2, 3, 4, 4, 5, 5, 7, 9, 10, 11, 11, 12, 12, 13, 14, 14,
                            16, 16, 17, 17, 18, 18, 19, 19] if latent else
                  [0, 1, 3, 4, 4, 5, 5, 6, 7, 9, 10, 11, 11, 12, 13, 14, 14, 16, 17, 18, 18])
        return after

    def finish_y(prev):
        return ([lambda c=c: add("yT", c, prev, ring="m") for c in range(2)] +
                [lambda: add("y_copy", prev), lambda: add("y_center", prev), lambda: add("residual", prev)])

    def sequence(has_prev, has_next):
        nonlocal steps
        steps = []
        for k in count:
            count[k] = 0
        u = 0
        for p in range(npair):
            for share in beside(p, has_prev, has_next):
                add("unit", *units[u], ring="unit")
                run(share)
                if u >= 2:
                    finish(u - 2)
                u += 1
        if has_next:
            first, second, overwriting = late()
            run(first)
            finish(u - 2)
            run(second)
            finish(u - 1)
            run(overwriting)
            assert count["m"] % 2 == 0 and count["top"] % 2 == 0
        else:
            finish(u - 2)
            finish(u - 1)
            chain, proj = output(npair - 1)
            run(chain[:2])
            for kind in ("rload", "scale"):
                for hp in range(HG):
                    add(kind, npair - 1, hp)
            run(proj + finish_y(False))
        return steps

    final = sequence(True, False)
    opening = sequence(False, True)
    opening_count = dict(count)
    body = sequence(True, True)
    start = {k: before[k] + opening_count[k] - count[k] for k in count}
    return prologue, opening, body, final, before, start, dict(count), npair


def attention(nc, tag, x, const, w, a):
    latent = w["latent"]
    prologue, opening, body, final, before, later, count, NPAIR = attention_steps(latent, w["rslots"])
    NU, NG = count["unit"], count["evac"]
    none = dict.fromkeys(before, 0)

    def everything(engine, section):
        def numbering(b, base):
            return lambda ring, i: base[ring] + b * count[ring] + i

        section(prologue, numbering(0, none), 0, 0)
        section(opening, numbering(0, before), 0, 1)
        with engine.Fori(1, NSEQ - 1) as b:
            section(body, numbering(b, later), b, b + 1)
        section(final, numbering(NSEQ - 1, later), NSEQ - 1, NSEQ)

    def last(steps, s, kind, *args):
        if any(k == kind and a[:len(args)] == args for k, a, _ in steps[:s]):
            return last_item(steps, s, kind, *args)
        return last_item(body, len(body), kind, *args) - count["top" if kind == "top" else "m"]

    scale = w["scale"]
    KW = P if latent else NKV0 * HD0
    with ExitStack() as ctx:
        m = Names(nc, ctx, tag)
        norm = Norm(m, const, "in")
        norm_y = Norm(m, const, "out")
        ident = const["ident"]
        yT = m.sb("yT", [P, KD, SEQ])
        addend = at(yT, 0, (D, TT), (1, D))
        xTh = m.sb("xTh", [P, KD, SEQ], F32R)
        xTl = m.sb("xTl", [P, KD, SEQ], F32R)
        nkey = 1 if latent else NKV0
        keyh = m.sb("keyh", [P, nkey, SEQ], F32R)
        keyl = m.sb("keyl", [P, nkey, SEQ], F32R)
        VH = 1 if latent else NKV0 // 2
        VW = P if latent else 192
        Vh = m.sb("Vh", [P, TT, VH, VW], F32R)
        Vl = m.sb("Vl", [P, TT, VH, VW], F32R)
        qa = m.sb("qa", [P, 2, HPAIR, SEQ], F32R)
        qb = m.sb("qb", [P, 2, HPAIR, SEQ], F32R) if latent else None
        QW = HPAIR * (P if latent else HD0)
        RW = max(QW, KW)
        rot = m.sb("rot", [P, TT, RW])
        xnt = at(rot, 0, (D, TT), (1, D))
        CW = 256 if latent else 512
        crossed = m.sb("crossed", [P, 2, CW])
        probs_h = m.sb("probs_h", [P, 3, 512], F32R)
        WHOLE = 1 if latent else 2
        probs = m.sb("probs", [P, WHOLE, 512])
        probs_l = m.sb("probs_l", [P, 2, 512], F32R)
        out = m.sb("out", [P, 2, HG, SEQ])
        mcol = m.sb("mcol", [P, TT, HPAIR])
        mrow = m.sb("mrow", [P, 2, HPAIR, P], F32R)
        drow = m.sb("drow", [P, 512])
        dcol = m.sb("dcol", [P, 32])
        RSLOTS = w["rslots"]
        rtile = m.sb("rtile", [P, RSLOTS, SEQ])
        misc = [m.ps(f"misc{i}", [P, 512]) for i in range(2)]
        topb = [m.ps(f"top{i}", [P, 512]) for i in range(2)]
        score = [m.ps(f"score{i}", [P, 512]) for i in range(2)]
        pvb = [m.ps(f"pv{i}", [P, 512]) for i in range(2)]
        d_dram = nc.dram_tensor(f"{tag}_rowsums", [NPAIR, HPAIR, SEQ], F32, kind="Internal").ap()
        r_dram = nc.dram_tensor(f"{tag}_recips", [NPAIR, HPAIR, SEQ], F32, kind="Internal").ap()
        if not latent:
            wo = m.sb("wo", [P, HG, D])
            x_loaded = m.sem("x_loaded")
            wq_raw = m.sb("wq_raw", [P, KD, QW])
            wq = [m.sb(f"wq{s}", [P, KD, QW], F32R) for s in "hl"]
            held = wq_raw[:, 0, :]
            wq_loaded = m.sem("wq_loaded")
            wq_high = m.sem("wq_high")
            wq_low = m.sem("wq_low")
        else:
            craw = at(rot, 64, (RW, TT), (1, 64))
            held = m.sb("held", [P, SEQ])[:]
            csq = m.sb("csq", [P, TT, 64])
            css = m.sb("css", [P, TT])
            crs = m.sb("crs", [P, TT])

        pause = m.sb("pause", [P, 3])
        set_up = m.sem("set_up")
        xn_ready = m.sem("xn_ready")
        misc_ready = m.sem("misc_ready")
        misc_free = m.sem("misc_free")
        high_done = m.sem("high_done")
        parts = m.sem("parts")
        rotated = m.sem("rotated")
        top_ready = m.sem("top_ready")
        top_free = m.sem("top_free")
        score_ready = m.sem("score_ready")
        probs_ready = m.sem("probs_ready")
        lows_ready = m.sem("lows_ready")
        pv_done = m.sem("pv_done")
        pv_free = m.sem("pv_free")
        drow_done = m.sem("drow_done")
        d_stored = [m.sem(f"d_stored{i}") for i in range(4)]
        d_loaded = m.sem("d_loaded")
        recips = m.sem("recips")
        r_stored = m.sem("r_stored")
        passed = m.sem("passed")
        r_loaded = [m.sem(f"r_loaded{i}") for i in range(RSLOTS)]
        scaled = m.sem("scaled")
        wo_loaded = m.sem("wo_loaded")
        held_high = m.sem("held_high")
        held_low = m.sem("held_low")
        y_normed = m.sem("y_normed")
        if latent:
            c_link = m.sem("c_link")
            c_var = m.sem("c_var")
            c_rstd = m.sem("c_rstd")
            c_ready = m.sem("c_ready")
            c_low = m.sem("c_low")
            c_high = m.sem("c_high")
        block = ctx.enter_context(nc.Block())

        def vals(V, h, k):
            return V[:, k, h // 2, 64 * (h % 2):64 * (h % 2) + P]

        KSPLIT = 0 if latent else NKV0 // 2 - 1

        def split_keys(h):
            if latent:
                return [(slice(0, P), slice(0, P), 0)]
            return [(slice(src, src + 64), slice(dst, dst + 64), 2 * h + src // 64)
                    for src in (0, 64) for dst in (0, 64)]

        def rotated_at(kind, args, split=False):
            if kind == "key":
                off, step, heads = args[0] * RW, 64, 1 if latent else NKV0
            elif latent:
                off, step, heads = (args[1] // 2) * RW + (args[1] % 2) * 512, P, HG
            else:
                off, step, heads = args[1] * RW, 64, HPAIR
            return at(rot, off, (step, heads), (32, 2), (1, 32)) if split else at(rot, off, (step, heads), (1, 64))

        @block.gpsimd
        def _(pool):
            pool.sem_inc(rotated, 2)
            pool.sem_inc(lows_ready, 2)

            def section(steps, item, b, nx):
                for kind, args, i in steps:
                    if kind == "center":
                        norm.power(nc, pool, nx)
                    if kind == "norm" and steps is prologue:
                        nc.gpsimd.memset(mrow[:].bitcast(F32), 0.0).then_inc(set_up, 1)
                        nc.gpsimd.memset(Vh[:, :, :, 64:128].bitcast(F32), 1.0).then_inc(set_up, 1)
                        nc.gpsimd.memset(Vl[:].bitcast(F32), 0.0).then_inc(set_up, 1)
                    if kind == "y_center":
                        norm_y.power(nc, pool, b - args[0])
                    if kind in ("key", "query"):
                        r = args[-1]
                        pool.wait_ge(parts, item("rope", r) + 1)
                        heads = (1 if latent else NKV0) if kind == "key" else HG if latent else HPAIR
                        dst = rotated_at(kind, args)
                        nc.gpsimd.tensor_tensor(dst, dst, at(crossed, r % 2 * CW, (64, heads), (1, 64)),
                                                ALU.add).then_inc(rotated, 1)
                    if kind == "unit":
                        pool.wait_ge(probs_ready, b * NU + i + 3)
                        pool.wait_ge(pv_done, b * NU + i + 1)
                        nc.gpsimd.tensor_tensor(probs_l[:, i % 2, :], probs[:, i % WHOLE, :], probs_h[:, i % 3, :].bitcast(F32),
                                                ALU.subtract).then_inc(lows_ready, 1)
                    if kind == "cnorm":
                        pool.wait_ge(c_var, nx + 1)
                        nc.gpsimd.tensor_tensor(crs[:], css[:], const["minus_half"][:, 0:TT],
                                                ALU.pow).then_inc(c_rstd, 1)

            everything(pool, section)

        @block.scalar
        def _(act):
            act.sem_inc(probs_ready, 2)
            act.sem_inc(pv_free, 2)

            def section(steps, item, b, nx):
                for s, (kind, args, i) in enumerate(steps):
                    if kind in HIGH:
                        act.wait_ge(misc_ready, item("m", i) + 1)
                        bank = misc[i % 2]
                    if kind == "wquery":
                        act.wait_ge(wq_loaded, (item("wquery", i) + 1) * 16)
                        if steps is not prologue:
                            act.wait_ge(misc_ready, item("m", last_item(steps, s, "query")) + 1)
                        nc.scalar.activation(wq[0][:], wq_raw[:], ACT.Copy).then_inc(wq_high, 1)
                    if kind in ("value", "csplit") and steps is prologue:
                        act.wait_ge(set_up, 3)
                    if kind == "value":
                        if steps is not prologue:
                            act.wait_ge(pv_done, b * NU + NU + 2)
                        nc.scalar.activation(at(Vh, args[0] * VH * VW, (VW, VH), (P, 2), (1, 64)),
                                             at(bank, 0, (P, VH), (64, 2), (1, 64)), ACT.Copy).then_inc(high_done, 1)
                    if kind == "keysplit":
                        act.wait_ge(misc_free, item("m", last_item(steps, s, "hold")) + 3)
                        if steps is not prologue:
                            act.wait_ge(score_ready, b * NU + NU)
                        for src, dst, k in split_keys(KSPLIT):
                            ins = nc.scalar.activation(keyh[dst, k, :], held[src, :], ACT.Copy)
                        ins.then_inc(held_high, 1)
                    if kind == "csplit":
                        act.wait_ge(c_ready, nx + 1)
                        if steps is not prologue:
                            act.wait_ge(pv_done, b * NU + NU + 2)
                        nc.scalar.activation(Vh[:, :, 0, 0:64], csq[:], ACT.Copy).then_inc(c_high, 1)
                    if kind == "xT":
                        nc.scalar.activation(xTh[:, args[0], :], bank[:], ACT.Copy).then_inc(high_done, 1)
                    if kind == "keyT":
                        for src, dst, k in split_keys(args[0]):
                            ins = nc.scalar.activation(keyh[dst, k, :], bank[src, :], ACT.Copy)
                        ins.then_inc(high_done, 1)
                    if kind == "queryT":
                        p, n = args
                        if latent:
                            nc.scalar.activation(qa[:, p % 2, n, :], bank[:], ACT.Copy).then_inc(high_done, 1)
                        else:
                            nc.scalar.activation(qa[0:64, p % 2, 2 * n, :], bank[0:64, :], ACT.Copy)
                            nc.scalar.activation(qa[64:128, p % 2, 2 * n + 1, :], bank[64:128, :],
                                                 ACT.Copy).then_inc(high_done, 1)
                    if kind == "unit":
                        act.wait_ge(score_ready, b * NU + i + 1)
                        nc.scalar.activation(probs_h[:, i % 3, :], score[i % 2][:], ACT.Exp, scale=scale)
                        act.wait_ge(lows_ready, b * NU + i + 3 - WHOLE)
                        nc.scalar.activation(probs[:, i % WHOLE, :], score[i % 2][:], ACT.Exp,
                                             scale=scale).then_inc(probs_ready, 1)
                    if kind == "evac":
                        p, q, g, u = args
                        act.wait_ge(pv_done, b * NU + u + 3)
                        bank = pvb[i % 2]
                        slot = i % 4
                        act.wait_ge(d_stored[slot], (b * (NG // 4) + i // 4 + 1) * 16)
                        vals_at, sums_at = (0, 64) if latent or g == 0 else (64, 0)
                        nc.scalar.activation(drow[32 * slot:32 * slot + 1, :], bank[sums_at:sums_at + 1, :],
                                             ACT.Copy).then_inc(drow_done, 1)
                        for odd in range(2):
                            dst = bass.AP(tensor=out[:].tensor,
                                          offset=out[64 * odd:64 * odd + 64, p % 2, 2 * g, q * P:q * P + P].offset,
                                          ap=[[out[:].ap[0][0], 64], [SEQ, 2], [1, P]])
                            v = bank[vals_at:vals_at + 64, :].rearrange("p (h n) -> p h n", h=HG)
                            ins = nc.scalar.activation(dst, v[:, odd::2, :], ACT.Copy)
                        ins.then_inc(pv_free, 1)

            everything(act, section)

        @block.vector
        def _(dve):
            dve.sem_inc(misc_free, 2)
            dve.sem_inc(top_free, 2)
            dve.sem_inc(scaled, RSLOTS)

            def tiles_of(n):
                if isinstance(n, int):
                    return [x[:, n * TT + j, :] for j in range(TT)]
                return [x[:, bass.ds(n * TT + j, 1), :].rearrange("p a d -> p (a d)") for j in range(TT)]

            def section(steps, item, b, nx):
                high = 0
                for s, (kind, args, i) in enumerate(steps):
                    if kind == "center":
                        if steps is opening and "x" in w:
                            dve.wait_ge(x_loaded, 16)
                        norm.statistics(nc, dve, tiles_of(nx), nx)
                    if kind == "norm":
                        xb = tiles_of(nx)
                        dve.wait_ge(norm.rstd_ready, nx + 1)
                        for j in range(TT):
                            ins = norm.apply(nc, xnt[:, j, :], xb[j], j)
                        ins.then_inc(xn_ready, 1)
                    if kind in HIGH:
                        high += 1
                        dve.wait_ge(high_done, item("high", high - 1) + 1)
                        bank = misc[i % 2]
                    if kind == "wquery":
                        dve.wait_ge(wq_high, item("wquery", i) + 1)
                        nc.vector.tensor_tensor(wq[1][:], wq_raw[:], wq[0][:].bitcast(F32),
                                                ALU.subtract).then_inc(wq_low, 1)
                    if kind == "xT":
                        k, = args
                        nc.vector.tensor_tensor(xTl[:, k, :], bank[:], xTh[:, k, :].bitcast(F32),
                                                ALU.subtract).then_inc(misc_free, 1)
                    if kind == "keyT":
                        for src, dst, k in split_keys(args[0]):
                            ins = nc.vector.tensor_tensor(keyl[dst, k, :], bank[src, :], keyh[dst, k, :].bitcast(F32),
                                                          ALU.subtract)
                        ins.then_inc(misc_free, 1)
                    if kind == "hold":
                        dve.wait_ge(misc_ready, item("m", i) + 1)
                        nc.vector.tensor_copy(held, misc[i % 2][:]).then_inc(misc_free, 1)
                    if kind == "keysplit":
                        dve.wait_ge(held_high, nx + 1)
                        for src, dst, k in split_keys(KSPLIT):
                            ins = nc.vector.tensor_tensor(keyl[dst, k, :], held[src, :], keyh[dst, k, :].bitcast(F32),
                                                          ALU.subtract)
                        ins.then_inc(held_low, 1)
                    if kind == "queryT":
                        p, n = args
                        if latent:
                            nc.vector.tensor_tensor(qb[:, p % 2, n, :], bank[:], qa[:, p % 2, n, :].bitcast(F32),
                                                    ALU.subtract).then_inc(misc_free, 1)
                        else:
                            e, o = qa[:, p % 2, 2 * n, :], qa[:, p % 2, 2 * n + 1, :]
                            nc.vector.tensor_tensor(e[64:128], bank[0:64, :], e[0:64].bitcast(F32), ALU.subtract)
                            nc.vector.tensor_tensor(o[0:64], bank[64:128, :], o[64:128].bitcast(F32),
                                                    ALU.subtract).then_inc(misc_free, 1)
                    if kind in ("key", "query"):
                        r = args[-1]
                        dve.wait_ge(misc_ready, item("m", i) + 1)
                        dve.wait_ge(rotated, item("rope", r) + 1)
                        bank = misc[i % 2]
                        if kind == "key":
                            j, (cos, sin) = args[0], w["key_tables"]
                            heads, step = (1, 64) if latent else (NKV0, 64)
                        else:
                            j = args[1] // 2 if latent else args[1]
                            cos, sin = w["query_tables"]
                            heads, step = (HG, P) if latent else (HPAIR, 64)
                        nc.vector.tensor_tensor(rotated_at(kind, args, split=True),
                                                at(bank, 0, (step, heads), (32, 2), (1, 32)),
                                                at(cos, j * 32, (0, heads), (0, 2), (1, 32)), ALU.mult)
                        for lo, hi in ((0, 32), (32, 0)):
                            ins = nc.vector.tensor_tensor(at(crossed, r % 2 * CW + lo, (64, heads), (1, 32)),
                                                          at(bank, hi, (step, heads), (1, 32)),
                                                          at(sin, j * 64 + lo, (0, heads), (1, 32)), ALU.mult)
                        ins.then_inc(parts, 1)
                        if latent and kind == "key":
                            nc.vector.tensor_copy(at(rot, j * RW + 64, (1, 64)), bank[:, 64:128]).then_inc(misc_free, 1)
                        elif latent:
                            nc.vector.tensor_copy(at(rot, j * RW + (args[1] % 2) * 512 + 64, (P, HG), (1, 64)),
                                                  at(bank, 64, (P, HG), (1, 64))).then_inc(misc_free, 1)
                        else:
                            dve.wait_ge(parts, item("rope", r) + 1)
                            nc.vector.memset(pause[:, 0:1], 0.0).then_inc(misc_free, 1)
                    if kind == "value":
                        hi, lo = (at(V, args[0] * VH * VW, (VW, VH), (P, 2), (1, 64)) for V in (Vh, Vl))
                        nc.vector.tensor_tensor(lo, at(bank, 0, (P, VH), (64, 2), (1, 64)), hi.bitcast(F32),
                                                ALU.subtract).then_inc(misc_free, 1)
                    if kind == "cnorm":
                        dve.wait_ge(misc_free, item("m", last_item(steps, s, "key")) + 3)
                        nc.vector.tensor_tensor(csq[:], craw, craw, ALU.mult).then_inc(c_link, 1)
                        dve.wait_ge(c_link, nx * 4 + 1)
                        nc.vector.tensor_reduce(css[:], csq[:], AX.X, ALU.add).then_inc(c_link, 1)
                        dve.wait_ge(c_link, nx * 4 + 2)
                        nc.vector.tensor_scalar(css[:], css[:], 1.0 / LAT1, RMS_EPS, ALU.mult, ALU.add).then_inc(c_var, 1)
                        dve.wait_ge(c_rstd, nx + 1)
                        nc.vector.tensor_tensor(csq[:], craw, at(crs, 0, (1, TT), (0, 64)), ALU.mult).then_inc(c_link, 1)
                        dve.wait_ge(c_link, nx * 4 + 3)
                        weight = at(w["norm_w"], 0, (0, TT), (1, 64))
                        nc.vector.tensor_tensor(craw, csq[:], weight, ALU.mult).then_inc(c_link, 1)
                        dve.wait_ge(c_link, nx * 4 + 4)
                        nc.vector.tensor_tensor(csq[:], csq[:], weight, ALU.mult).then_inc(c_ready, 1)
                    if kind == "csplit":
                        dve.wait_ge(c_high, nx + 1)
                        nc.vector.tensor_tensor(Vl[:, :, 0, 0:64], csq[:], Vh[:, :, 0, 0:64].bitcast(F32),
                                                ALU.subtract).then_inc(c_low, 1)
                    if kind == "top":
                        p, q, heads = args
                        dve.wait_ge(top_ready, item("top", i) + 1)
                        n = P * (q + 1)
                        v = topb[i % 2][:, 0:len(heads) * n].rearrange("p (h n) -> p h n", h=len(heads))
                        nc.vector.tensor_reduce(mcol[:, q, heads[0]:heads[-1] + 1], v, AX.X,
                                                ALU.max).then_inc(top_free, 1)
                    if kind == "topT":
                        p, q = args
                        if steps is prologue:
                            dve.wait_ge(set_up, 3)
                        dve.wait_ge(misc_ready, item("m", i) + 1)
                        nc.vector.tensor_tensor(mrow[0:HPAIR, q % 2, :, :],
                                                bass.AP(tensor=misc[i % 2][:].tensor, offset=misc[i % 2][:].offset,
                                                        ap=[[misc[i % 2][:].ap[0][0], HPAIR], [0, HPAIR], [1, P]]),
                                                bass.AP(tensor=ident[:].tensor, offset=ident[:].offset,
                                                        ap=[[ident[:].ap[0][0], HPAIR], [1, HPAIR], [0, P]]),
                                                ALU.mult).then_inc(misc_free, 1)
                    if kind == "even":
                        dve.wait_ge(misc_ready, item("m", i) + 1)
                        nc.vector.memset(pause[:, 1:2], 0.0).then_inc(misc_free, 1)
                    if kind == "recip":
                        p, = args
                        dve.wait_ge(d_loaded, (b * NPAIR + p + 1) * 16)
                        nc.vector.reciprocal(dcol[:], dcol[:]).then_inc(recips, 1)
                    if kind == "scale":
                        p, hp = args
                        n = (b * NPAIR + p) * (HG // RSLOTS) + hp // RSLOTS
                        r = rtile[:, hp % RSLOTS, :]
                        if steps is final and p == NPAIR - 1:
                            n, r = NSEQ * NPAIR * HG // RSLOTS - 1, at(rot, hp * SEQ, (1, SEQ))
                        dve.wait_ge(r_loaded[hp % RSLOTS], (n + 1) * 32)
                        dve.wait_ge(pv_free, b * NG + (p + 1) * 2 * TT + 2)
                        o = out[:, p % 2, hp, :]
                        nc.vector.tensor_tensor(o, o, r, ALU.mult).then_inc(scaled, 1)
                    if kind == "oproj":
                        p, k = args
                        dve.wait_ge(misc_ready, item("m", i) + 1)
                        if p == 0:
                            nc.vector.tensor_copy(yT[:, k, :], misc[i % 2][:]).then_inc(misc_free, 1)
                        else:
                            nc.vector.tensor_tensor(yT[:, k, :], yT[:, k, :], misc[i % 2][:],
                                                    ALU.add).then_inc(misc_free, 1)
                    if kind == "y_copy":
                        banks = [last_item(steps, s, "yT", c) for c in range(2)]
                        dve.wait_ge(misc_ready, item("m", banks[1]) + 1)
                        for c in range(2):
                            nc.vector.tensor_copy(addend[:, 2 * c:2 * c + 2, :].rearrange("p a d -> p (a d)"),
                                                  misc[banks[c] % 2][:]).then_inc(misc_free, 1)
                    if kind == "y_center":
                        dve.wait_ge(misc_free, item("m", last_item(steps, s, "yT", 1)) + 3)
                        norm_y.statistics(nc, dve, [addend[:, j, :] for j in range(TT)], b - args[0])
                    if kind == "residual":
                        done = b - args[0]
                        dve.wait_ge(norm_y.rstd_ready, done + 1)
                        for j in range(TT):
                            ins = norm_y.apply(nc, addend[:, j, :], addend[:, j, :], j)
                        ins.then_inc(y_normed, 1)
                        dve.wait_ge(y_normed, 2 * done + 1)
                        for j, tile in enumerate(tiles_of(done)):
                            ins = nc.vector.tensor_tensor(tile, tile, addend[:, j, :], ALU.add)
                        ins.then_inc(y_normed, 1)
                        dve.wait_ge(y_normed, 2 * done + 2)
                        nc.vector.memset(pause[:, 2:3], 0.0)

            everything(dve, section)

        @block.tensor
        def _(pe):
            pe.sem_inc(pv_done, 2)

            def section(steps, item, b, nx):
                for s, (kind, args, i) in enumerate(steps):
                    if kind in ("xT", "key", "value", "keyT", "query", "queryT", "topT", "oproj", "yT", "even", "hold"):
                        pe.wait_ge(misc_free, item("m", i) + 1)
                        bank = misc[i % 2]
                    if kind == "xT":
                        k, = args
                        pe.wait_ge(xn_ready, nx + 1)
                        for j in range(TT):
                            ins = nc.tensor.transpose(bank[:, j * P:(j + 1) * P], xnt[:, j, k * P:(k + 1) * P],
                                                      ident[:])
                        ins.then_inc(misc_ready, 1)
                    if kind in ("key", "value", "query"):
                        if kind == "key":
                            j, n = args[0], (P if latent else 512)
                            wh, wl = (t[:, :, 0:n] for t in w["key"])
                            if j == 0:
                                pe.wait_ge(misc_free, item("m", last_item(steps, s, "xT")) + 3)
                        elif kind == "value":
                            j, n = args[0], 512
                            wh, wl = (t[:, :, 512:1024] for t in w["key"])
                        else:
                            p, c, _ = args
                            j, half = divmod(c, 2) if latent else (c, 0)
                            n = 512
                            if not latent and c == 0:
                                newest = last_item(steps, s, "wquery")
                                pe.wait_ge(wq_low, item("wquery", newest) + 1)
                            off = p * QW + half * 512 if latent else 0
                            wh, wl = (t[:, :, off:off + 512] for t in (w["query"] if latent else wq))
                        tok = slice(j * P, (j + 1) * P)
                        terms = [(xs[:, k, tok], ws[:, k, :]) for k in range(KD)
                                 for xs, ws in ((xTh, wh), (xTh, wl), (xTl, wh))]
                        for t, (st, mv) in enumerate(terms):
                            ins = nc.tensor.matmul(bank[:, 0:n], st, mv, start=(t == 0), stop=(t == len(terms) - 1))
                        ins.then_inc(misc_ready, 1)
                        if kind != "value":
                            last_rope = item("rope", args[-1])
                    if kind in ("keyT", "hold"):
                        pe.wait_ge(rotated, last_rope + 3)
                        if latent:
                            pe.wait_ge(c_ready, nx + 1)
                        for j in range(TT):
                            ins = nc.tensor.transpose(bank[:, j * P:(j + 1) * P],
                                                      rot[:, j, args[0] * P:(args[0] + 1) * P], ident[:])
                        ins.then_inc(misc_ready, 1)
                    if kind == "queryT":
                        pe.wait_ge(rotated, last_rope + 3)
                        if latent:
                            pe.wait_ge(misc_free, item("m", last_item(steps, s, "query", args[0])) + 3)
                        for j in range(TT):
                            ins = nc.tensor.transpose(bank[:, j * P:(j + 1) * P],
                                                      rot[:, j, args[1] * P:(args[1] + 1) * P], ident[:])
                        ins.then_inc(misc_ready, 1)
                    if kind == "top":
                        p, q, heads = args
                        pe.wait_ge(top_free, item("top", i) + 1)
                        if q == 0:
                            pe.wait_ge(misc_free, item("m", last(steps, s, "queryT", p)) + 3)
                            if p == (0 if latent else NPAIR - 1) and heads[0] == 0:
                                pe.wait_ge(held_low, (nx if latent else b) + 1)
                        n = P * (q + 1)
                        for c, h in enumerate(heads):
                            kh = keyh[:, 0 if latent else 2 * p + h // HG, 0:n]
                            nc.tensor.matmul(topb[i % 2][:, c * n:(c + 1) * n], qa[:, p % 2, h, q * P:(q + 1) * P], kh,
                                             start=True, stop=False)
                            ins = nc.tensor.matmul(topb[i % 2][:, (c + 1) * n - P:(c + 1) * n], w["identb"][:],
                                                   w["mask_q"][:], start=False, stop=True)
                        ins.then_inc(top_ready, 1)
                    if kind == "topT":
                        p, q = args
                        pe.wait_ge(top_free, item("top", last(steps, s, "top", p, q)) + 3)
                        nc.tensor.transpose(bank[0:HPAIR, 0:P], mcol[:, q, :], ident[:]).then_inc(misc_ready, 1)
                    if kind == "even":
                        nc.tensor.transpose(bank[0:HPAIR, 0:P], mcol[:, 0, :], ident[:]).then_inc(misc_ready, 1)
                    if kind == "unit":
                        p, q, g, k = args
                        pe.wait_ge(probs_ready, b * NU + i + 1)
                        if g == 0 and k == 0:
                            pe.wait_ge(misc_free, item("m", last(steps, s, "topT", p, q)) + 3)
                        bank = score[i % 2]
                        kt = slice(k * P, (k + 1) * P)
                        kv = 0 if latent else 2 * p + g
                        qs = [t[:, p % 2, g * HG:(g + 1) * HG, q * P:(q + 1) * P] for t in (qa, qb) if t is not None]
                        terms = [(keyh[:, kv, kt], qs[0]), (keyl[:, kv, kt], qs[0])]
                        if latent:
                            terms.append((keyh[:, kv, kt], qs[1]))
                        terms.append((w["minus_one"][:], mrow[:, q % 2, g * HG:(g + 1) * HG, :]))
                        if k == q:
                            terms.append((w["identb"][:], at(w["mask_k"], 0, (0, HG), (1, P))))
                        for t, (st, mv) in enumerate(terms):
                            ins = nc.tensor.matmul(bank[:], st, mv, start=(t == 0), stop=(t == len(terms) - 1))
                        ins.then_inc(score_ready, 1)
                    if kind == "pv":
                        p, q, g, k, u = args
                        group = (p * TT + q) * 2 + g
                        pe.wait_ge(lows_ready, b * NU + u + 3)
                        if u == 0 and latent:
                            pe.wait_ge(c_low, b + 1)
                        if k == 0:
                            pe.wait_ge(pv_free, b * NG + group + 1)
                        h = 0 if latent else 2 * p + g
                        hi, lo = probs_h[:, u % 3, :], probs_l[:, u % 2, :]
                        for t, (V, e) in enumerate(((Vh, hi), (Vh, lo), (Vl, hi))):
                            ins = nc.tensor.matmul(pvb[group % 2][:], vals(V, h, k), e,
                                                   start=(k == 0 and t == 0), stop=(k == q and t == 2))
                        ins.then_inc(pv_done, 1)
                    if kind == "oproj":
                        p, k = args
                        pe.wait_ge(scaled, (b * NPAIR + p + 1) * HG + RSLOTS)
                        if not latent:
                            pe.wait_ge(wo_loaded, (b * NPAIR + p + 1) * 16)
                        for hp in range(HG):
                            st = (w["out"][:, p % NPAIR * HG + hp, k * P:(k + 1) * P] if latent else
                                  wo[:, hp, k * P:(k + 1) * P])
                            ins = nc.tensor.matmul(bank[:], st, out[:, p % 2, hp, :], start=(hp == 0), stop=(hp == HG - 1))
                        ins.then_inc(misc_ready, 1)
                    if kind == "yT":
                        c, _ = args
                        if c == 0:
                            pe.wait_ge(misc_free, item("m", last_item(steps, s, "oproj")) + 3)
                        for j in range(2):
                            tok = slice((2 * c + j) * P, (2 * c + j + 1) * P)
                            for k in range(KD):
                                ins = nc.tensor.transpose(bank[:, j * D + k * P:j * D + (k + 1) * P],
                                                          yT[:, k, tok], ident[:])
                        ins.then_inc(misc_ready, 1)

            everything(pe, section)

        @block.sync
        def _(sp):
            for s in d_stored:
                sp.sem_inc(s, 16)
            if not latent:
                sp.dma_start(flat(wq_raw), w["query"][0]).then_inc(wq_loaded, 16)
                sp.dma_start(flat(wo), w["out"][0]).then_inc(wo_loaded, 16)
                sp.dma_start(x[:, TT:, :], w["x"][:, TT:, :]).then_inc(x_loaded, 16)

            def section(steps, item, b, nx):
                for kind, args, i in steps:
                    if kind == "wquery" and not (steps is final and args[0] == NPAIR - 1):
                        if args[0] == 0:
                            continue
                        sp.wait_ge(wq_low, item("wquery", i) + 1)
                        sp.dma_start(flat(wq_raw), w["query"][(args[0] + 1) % NPAIR]).then_inc(wq_loaded, 16)
                    if kind == "keysplit" and not latent:
                        sp.wait_ge(held_low, nx + 1)
                        sp.dma_start(flat(wq_raw), w["query"][1]).then_inc(wq_loaded, 16)
                    if kind == "evac":
                        p, q, g, _ = args
                        slot = i % 4
                        sp.wait_ge(drow_done, b * NG + i + 1)
                        sp.dma_start(d_dram[p:p + 1, g * HG:(g + 1) * HG, q * P:(q + 1) * P],
                                     drow[32 * slot:32 * slot + 1, :].rearrange("p (h n) -> p h n", h=HG)
                                     ).then_inc(d_stored[slot], 16)
                    if kind == "dload":
                        p, = args
                        last = (p + 1) * 2 * TT - 1
                        for g in range(last - 3, last + 1):
                            sp.wait_ge(d_stored[g % 4], (b * (NG // 4) + g // 4 + 2) * 16)
                        sp.dma_start(dcol[:], d_dram[p % NPAIR].rearrange("h n -> (h n)").rearrange("(a c) -> a c", c=32)
                                     ).then_inc(d_loaded, 16)
                    if kind == "recip":
                        p, = args
                        sp.wait_ge(recips, b * NPAIR + p + 1)
                        sp.dma_start(r_dram[p % NPAIR].rearrange("h n -> (h n)").rearrange("(a c) -> a c", c=32),
                                     dcol[:]).then_inc(r_stored, 16)
                        sp.wait_ge(r_stored, (b * NPAIR + p + 1) * 16)
                        sp.sem_inc(passed, 1)
                    if kind == "rload":
                        p, hp = args
                        r = rtile[:, hp % RSLOTS, :]
                        if steps is final and p == NPAIR - 1:
                            r = at(rot, hp * SEQ, (1, SEQ))
                        else:
                            sp.wait_ge(scaled, (b * NPAIR + p) * HG + hp + 1)
                        for odd in range(2):
                            row = r_dram[p % NPAIR, 2 * hp + odd, :]
                            sp.dma_start(r[64 * odd:64 * odd + 64],
                                         bass.AP(tensor=row.tensor, offset=row.offset, ap=[[0, 64], [1, SEQ]])
                                         ).then_inc(r_loaded[hp % RSLOTS], 16)
                    if kind == "oproj" and args[1] == KD - 1 and not latent:
                        p, _ = args
                        sp.wait_ge(misc_ready, item("m", i) + 1)
                        sp.dma_start(flat(wo), w["out"][(p + 1) % NPAIR]).then_inc(wo_loaded, 16)

            everything(sp, section)
            if not latent:
                sp.wait_ge(wo_loaded, (NSEQ * NPAIR + 1) * 16)


def attention0(nc, a, x, const):
    with ExitStack() as ctx:
        m = Names(nc, ctx, "a0")
        key = [m.sb(f"wkey{s}", [P, KD, 2 * NKV0 * HD0], F32R) for s in "hl"]
        G, HALF = 2 * NKV0, HD0 // 2

        def products(f, bank):
            down, upk, upv = f
            for k in range(KD):
                hid = slice(k * P, (k + 1) * P)
                stat = [down[:, r, hid] for r in range(KD)]
                yield ([(0, 0, D, stat[r], upk[:, r, :], r == 0, r == KD - 1) for r in range(KD)],
                       None, [at(t, k * 1024 + ROPE0, (HALF, G), (1, HALF - ROPE0)) for t in key])
                yield ([(0, 0, 512, stat[r], upv[:, r, :], r == 0, r == KD - 1) for r in range(KD)],
                       None, [t[:, k, 512:1024] for t in key])

        def listed(f, bank):
            got = []
            for i, (mm, _, (hi, lo)) in enumerate(products(f, bank)):
                view = at(bank[i % 2], 0, (16, G), (1, 16)) if i % 2 == 0 else bank[i % 2][:]
                got.append((mm, view, hi, lo))
            return got

        jobs = []
        for k in range(KD):
            hi, lo = (at(t, k * 1024, (HALF, G), (1, ROPE0)) for t in key)
            jobs.append((a["a0_rope"][:, k * 256:(k + 1) * 256], hi, lo))
        split_weights(nc, "a0", jobs, [(a["a0_down"], [P, KD, D]), (a["a0_upk"], [P, KD, 256]),
                                       (a["a0_upv"], [P, KD, 512])], listed,
                      loads=[(x[:, 0:TT, :], a["x"][:, 0:TT, :])])
        w = dict(const, latent=False, x=a["x"], rslots=1, scale=1.0 / 8.0, query=a["a0_query"], key=key, out=a["a0_out"],
                 query_tables=(const["cos"], const["sin"]), key_tables=(const["kcos"], const["ksin"]))
        attention(nc, "a0", x, const, w, a)


def attention1(nc, a, x, const):
    with ExitStack() as ctx:
        m = Names(nc, ctx, "a1")
        query = [m.sb(f"wquery{s}", [P, KD, NH1 * P], F32R) for s in "hl"]
        key = [m.sb(f"wkey{s}", [P, KD, P], F32R) for s in "hl"]
        outw = m.sb("outw", [P, NH1 // 2, D])

        def folds(f, bank):
            qn, bk, bv, wo = f
            got = []
            for k in range(KD):
                for half in range(2):
                    mm = [(0, h * 64, 64, qn[:, half * 8 + h, k * P:(k + 1) * P], bk[:, half * 8 + h, :], True, True)
                          for h in range(8)]
                    hi, lo = (at(t, k * NH1 * P + half * 8 * P + 64, (P, 8), (1, 64)) for t in query)
                    got.append((mm, at(bank[len(got) % 2], 0, (64, 8), (1, 64)), hi, lo))
            for hp in range(NH1 // 2):
                mm = [(64 * o, 0, D, bv[:, 2 * hp + o, :], wo[:, 2 * hp + o, :], True, True) for o in range(2)]
                got.append((mm, bank[len(got) % 2][:, 0:D], outw[:, hp, :], None))
            return got

        jobs = [(a["a1_key"], flat(key[0]), flat(key[1]))]
        for k in range(KD):
            hi, lo = (at(t, k * NH1 * P, (P, NH1), (1, 64)) for t in query)
            jobs.append((a["a1_rope"][:, k * 1024:(k + 1) * 1024], hi, lo))
        split_weights(nc, "a1", jobs, [(a["a1_nope"], [P, NH1, D]), (a["a1_bk"], [P, NH1, 64]),
                                       (a["a1_bv"], [P, NH1, 64]), (a["a1_wo"], [P, NH1, D])], folds)
        w = dict(const, latent=True, rslots=1, scale=float(1.0 / np.sqrt(ROT1 + NOPE1)), query=query, key=key, out=outw,
                 query_tables=(const["cos"], const["sin"]), key_tables=(const["cos"], const["sin"]))
        attention(nc, "a1", x, const, w, a)



def build_program(nc, a, out):
    with ExitStack() as ctx:
        m = Names(nc, ctx, "all")
        x = m.sb("x", [P, NSEQ * TT, D])
        const = {
            "ident": m.sb("ident", [P, P]),
            "minus_half": m.sb("minus_half", [P, 8]),
            "cos": m.sb("cos", [P, TT, 32]), "sin": m.sb("sin", [P, TT, 64]),
            "norm_w": m.sb("norm_w", [P, 64]),
            "identb": m.sb("identb", [P, P], BF16), "mask_q": m.sb("mask_q", [P, P], BF16),
            "mask_k": m.sb("mask_k", [P, P], BF16), "minus_one": m.sb("minus_one", [P, P], F32R),
        }
        layer0 = ctx.enter_context(ExitStack())
        m0 = Names(nc, layer0, "layer0")
        const0 = dict(const, kcos=m0.sb("kcos", [P, TT, 32]), ksin=m0.sb("ksin", [P, TT, 64]))
        tables = ("ident", "cos", "sin", "kcos", "ksin", "norm_w")
        cast = ("identb", "mask_q", "mask_k")
        with ExitStack() as c0:
            loaded, made = c0.enter_context(nc.semaphore("const_loaded")), c0.enter_context(nc.semaphore("const_made"))
            stage = c0.enter_context(nc.sbuf_tensor("const_stage", [P, 4, P], F32))
            block = c0.enter_context(nc.Block())

            @block.sync
            def _(sp):
                for i, name in enumerate(cast):
                    sp.dma_start(stage[:, i, :], a["ident" if name == "identb" else name]).then_inc(loaded, 16)
                for name in tables:
                    sp.dma_start(flat(const0[name]), a[name]).then_inc(loaded, 16)
                sp.wait_ge(loaded, 16 * (len(cast) + len(tables)))

            @block.vector
            def _(dve):
                nc.vector.memset(const["minus_half"][:], -0.5)
                nc.vector.memset(stage[:, 3, :], -1.0).then_inc(made, 1)
                dve.wait_ge(loaded, 16 * (len(cast) + len(tables)))
                dve.wait_ge(made, 1)
                for i, name in enumerate(cast):
                    nc.vector.tensor_copy(const[name][:], stage[:, i, :])
                nc.vector.tensor_copy(const["minus_one"][:], stage[:, 3, :]).then_inc(made, 1)
                dve.wait_ge(made, 2)

        attention0(nc, a, x, const0)
        layer0.close()
        feed_forward(nc, "f0", x, const, a["f0_weights"], MOE_H, moe=(a["f0_router"], a["f0_spread"], a["f0_before"]))
        attention1(nc, a, x, const)
        feed_forward(nc, "f1", x, const, a["f1_weights"], INTER, out=out)


def flat(t, p=P):
    v = t[:] if not isinstance(t, bass.AP) else t
    names = " ".join(f"d{i}" for i in range(v.ndim - 1))
    return v.rearrange(f"p {names} -> p ({names})")[0:p, :] if v.ndim > 2 else v[0:p, :]



def _layouts(inputs):
    f = {k: np.asarray(v) for k, v in inputs.items()}
    tiles = lambda w: np.ascontiguousarray(w.reshape(-1, P, w.shape[-1]).transpose(1, 0, 2).reshape(P, -1))

    g = {}
    g["x"] = np.ascontiguousarray(f["L0_attn_hidden_states"].reshape(NSEQ * TT, P, D).transpose(1, 0, 2))
    g["ident"] = np.eye(P, dtype=np.float32)
    def by_hidden_tile(gate, up, down):
        nt = -(-gate.shape[1] // P)
        out = np.zeros((P, nt, 3 * D), gate.dtype)
        for c, w in enumerate((gate, up)):
            full = np.zeros((D, nt * P), w.dtype)
            full[:, :w.shape[1]] = w
            out[:, :, c * D:(c + 1) * D] = full.reshape(KD, P, nt, P).transpose(1, 2, 0, 3).reshape(P, nt, D)
        full = np.zeros((nt * P, D), down.dtype)
        full[:down.shape[0]] = down
        out[:, :, 2 * D:] = full.reshape(nt, P, D).transpose(1, 0, 2)
        return out.reshape(P, -1)

    w = f["L1_ffn_w_gate_up"].T
    g["f1_weights"] = by_hidden_tile(w[:, :INTER], w[:, INTER:], f["L1_ffn_w_down"].T)
    beside = lambda e: e.transpose(1, 0, 2).reshape(D, NE * DE)
    g["f0_weights"] = by_hidden_tile(
        np.concatenate([beside(f["L0_ffn_We_gate"]), f["L0_ffn_Ws_gate"]], 1),
        np.concatenate([beside(f["L0_ffn_We_up"]), f["L0_ffn_Ws_up"]], 1),
        np.concatenate([f["L0_ffn_We_down"].reshape(NE * DE, D), f["L0_ffn_Ws_down"]], 0))
    g["f0_router"] = tiles(f["L0_ffn_W_router"])
    owner = np.minimum(np.arange(MOE_H) // DE, NE)
    spread = np.zeros((P, -(-MOE_H // P) * P), np.float32)
    for base in (0, 32):
        spread[base + owner, np.arange(MOE_H)] = 1.0
    g["f0_spread"] = spread
    g["f0_before"] = np.tile((np.arange(NE)[None, :] < np.arange(NE)[:, None]).astype(np.float32).reshape(1, -1), (P, 1))
    i = np.arange(P)
    g["mask_q"] = np.where(i[None, :] > i[:, None], MASKED, 0.0).astype(np.float32)
    g["mask_k"] = np.ascontiguousarray(g["mask_q"].T)
    g["a0_query"] = np.ascontiguousarray(
        f["L0_attn_q_w"].T.reshape(KD, P, NH0 // HPAIR, HPAIR * HD0).transpose(2, 1, 0, 3).reshape(NH0 // HPAIR, P, -1))
    g["a0_rope"] = tiles(f["L0_attn_kr_w"].T)
    g["a0_down"] = tiles(f["L0_attn_down_w"])
    g["a0_upk"] = tiles(f["L0_attn_upk_w"].T)
    g["a0_upv"] = tiles(f["L0_attn_upv_w"].T)
    g["a0_out"] = np.ascontiguousarray(
        f["L0_attn_o_w"].T.reshape(NH0 // HPAIR, HG, P, D).transpose(0, 2, 1, 3).reshape(NH0 // HPAIR, P, HG * D))
    pos = np.arange(SEQ, dtype=np.float32)

    def table(freq):
        angle = (pos[:, None] * freq[None, :]).astype(np.float32).astype(np.float64)
        c = np.cos(angle)
        s = np.concatenate([-np.sin(angle), np.sin(angle)], 1)
        return c.astype(np.float32), s.astype(np.float32)

    inv = (np.float32(1.0) / np.float32(10000.0) ** (np.arange(0, 64, 2, dtype=np.float32) / np.float32(64))).astype(np.float32)
    cos, sin = table(inv)
    g["cos"], g["sin"] = tiles(cos), tiles(sin)
    rotated = np.tile(np.arange(HD0 // 2) < ROPE0, 2)
    g["kcos"] = tiles(np.where(rotated[:32], cos, np.float32(1.0)))
    g["ksin"] = tiles(np.where(rotated, sin, np.float32(0.0)))
    apart = np.concatenate([np.arange(0, ROT1, 2), np.arange(1, ROT1, 2)])
    wq = f["L1_attn_Wq"].reshape(D, NH1, NOPE1 + ROT1)
    g["a1_rope"] = tiles(np.ascontiguousarray(wq[:, :, NOPE1 + apart]).reshape(D, NH1 * ROT1))
    g["a1_nope"] = np.ascontiguousarray(wq[:, :, :NOPE1].transpose(2, 1, 0)).reshape(NOPE1, NH1 * D)
    wb = f["L1_attn_Wkv_b"].reshape(LAT1, NH1, NOPE1 + VD1)
    g["a1_bk"] = np.ascontiguousarray(wb[:, :, :NOPE1].transpose(2, 1, 0)).reshape(NOPE1, NH1 * LAT1)
    g["a1_bv"] = np.ascontiguousarray(wb[:, :, NOPE1:].transpose(2, 1, 0)).reshape(VD1, NH1 * LAT1)
    g["a1_wo"] = np.ascontiguousarray(f["L1_attn_Wo"].reshape(NH1, VD1, D).transpose(1, 0, 2)).reshape(VD1, NH1 * D)
    wa = f["L1_attn_Wkv_a"]
    g["a1_key"] = tiles(np.concatenate([wa[:, LAT1 + apart], wa[:, :LAT1]], 1))
    g["norm_w"] = np.tile(f["L1_attn_kv_norm_w"][None, :], (P, 1))
    return g


def kernel(**inputs):
    import numpy as _np
    import concourse.bacc as _bacc
    from concourse import mybir as _mybir
    from concourse.bass_utils import run_bass_kernel_spmd as _run

    g = _layouts(inputs)
    nc = _bacc.Bacc("TRN2", target_bir_lowering=False, num_devices=1)
    a = {k: nc.dram_tensor(f"in_{k}", v.shape, _mybir.dt.from_np(v.dtype), kind="ExternalInput").ap()
         for k, v in g.items()}
    out = nc.dram_tensor("out_x", [P, NSEQ * TT, D], _mybir.dt.float32, kind="ExternalOutput").ap()
    build_program(nc, a, out)
    r = _run(nc, [{f"in_{k}": v for k, v in g.items()}], core_ids=[0])
    y = r.results[0]["out_x"]
    return _np.ascontiguousarray(y.reshape(P, NSEQ * TT, D).transpose(1, 0, 2)).reshape(NSEQ, SEQ, D)
```
